# Optimizing a Trainium2 kernel written in Bass

```python
import numpy as np
import jax
import jax.numpy as jnp

def _softmax(x, axis=-1):
    return jax.nn.softmax(x, axis=axis)

def _gelu(x):
    return jax.nn.gelu(x, approximate=True)

def _silu(x):
    return jax.nn.silu(x)

def _sigmoid(x):
    return jax.nn.sigmoid(x)

def _layernorm(x, axis=-1, eps=1e-05):
    m = jnp.mean(x, axis=axis, keepdims=True)
    v = jnp.var(x, axis=axis, keepdims=True)
    return (x - m) / jnp.sqrt(v + eps)

def _scatter_add(tgt, idx, src, axis=0):
    return tgt.at[idx].add(src)

def _segment_sum(src, seg, n):
    return jax.ops.segment_sum(src, seg, n)
kernel_name = 'mk_audio_tower_d1_tok_audfeat256_r4_c56765'

def setup_inputs(seed: int=0):
    np.random.seed(seed)
    _w = jnp.asarray

    def _rec_inputs():
        import jax
        import jax.numpy as jnp
        _rk = jax.random.key(seed)
        x = -0.000392918 + 0.999932 * jax.random.normal(jax.random.fold_in(_rk, 1), (64, 750, 16), jnp.float32)
        return x
    x = _rec_inputs()

    def _L0_tok_setup():
        import jax, jax.numpy as jnp
        import numpy as np
        PATCH = 16
        STRIDE = 8
        EPS = 1e-05
        key = jax.random.key(seed)
        k1, k2, k3 = jax.random.split(key, 3)
        B, S, F, D = (128, 2048, 16, 64)
        in_dim = F * PATCH
        x = jax.random.normal(k1, (B, S, F), dtype=jnp.float32)
        bound = 1.0 / np.sqrt(in_dim)
        W = jax.random.uniform(k2, (D, in_dim), minval=-bound, maxval=bound, dtype=jnp.float32)
        b = jax.random.uniform(k3, (D,), minval=-bound, maxval=bound, dtype=jnp.float32)
        gamma = jnp.ones((D,), dtype=jnp.float32)
        beta = jnp.zeros((D,), dtype=jnp.float32)
        return {'x': x, 'W': W, 'b': b, 'gamma': gamma, 'beta': beta}
    _L0_tok_all = _L0_tok_setup()
    _L0_tok_in = {k: v for k, v in _L0_tok_all.items() if k in ('W', 'b', 'gamma', 'beta')}
    del _L0_tok_all

    def _L0_attn_setup():
        import jax, jax.numpy as jnp
        import numpy as np
        S, B, D, H, DH = (128, 32, 64, 8, 32)
        LN_EPS = 1e-05

        def elu_p1(x):
            return jax.nn.elu(x) + 1.0

        def sum_norm(x):
            return x / jnp.sum(x, axis=-1, keepdims=True)

        def layer_norm(x, g, b):
            mu = jnp.mean(x, axis=-1, keepdims=True)
            var = jnp.mean(jnp.square(x - mu), axis=-1, keepdims=True)
            return (x - mu) * jax.lax.rsqrt(var + LN_EPS) * g + b

        def _fast_rnn_forward(x, slow_W, out_W, ln_g, ln_b):
            slen, bsz, _ = x.shape
            o = layer_norm(x, ln_g, ln_b)
            qkv = jnp.einsum('sbd,ed->sbe', o, slow_W)
            qkv = qkv.reshape(slen, bsz, H, 5 * DH + 2)
            q, k, v, rk, rv, beta, rbeta = jnp.split(qkv, [DH, 2 * DH, 3 * DH, 4 * DH, 5 * DH, 5 * DH + 1], axis=-1)
            beta = jax.nn.sigmoid(beta)
            rbeta = jax.nn.sigmoid(rbeta)
            q = sum_norm(elu_p1(q))
            k = sum_norm(elu_p1(k))
            rk = jax.nn.softmax(rk, axis=-1)

            def ff_step(W, inp):
                qt, kt, vt, bt = inp
                v_old = jnp.einsum('bhij,bhj->bhi', W, kt)
                W = W + (bt * (vt - v_old))[..., :, None] * kt[..., None, :]
                z = jnp.einsum('bhij,bhj->bhi', W, qt)
                return (W, z)
            W0 = jnp.zeros((bsz, H, DH, DH), x.dtype)
            _, z = jax.lax.scan(ff_step, W0, (q, k, v, beta))

            def rec_step(carry, inp):
                R, h = carry
                zt, kt, vt, bt = inp
                q_rec = jax.nn.softmax(h, axis=-1)
                v_old = jnp.einsum('bhij,bhj->bhi', R, kt)
                R = R + (bt * (vt - v_old))[..., :, None] * kt[..., None, :]
                h = zt + jnp.einsum('bhij,bhj->bhi', R, q_rec)
                return ((R, h), h)
            R0 = jnp.zeros((bsz, H, DH, DH), x.dtype)
            h0 = jnp.zeros((bsz, H, DH), x.dtype)
            _, hs = jax.lax.scan(rec_step, (R0, h0), (z, rk, rv, rbeta))
            out = hs.reshape(slen, bsz, H * DH)
            out = jnp.einsum('sbe,de->sbd', out, out_W)
            return x + out
        key = jax.random.key(seed)
        k1, k2, k3 = jax.random.split(key, 3)
        x = jax.random.normal(k1, (S, B, D), jnp.float32)
        slow_W = jax.random.normal(k2, (H * (5 * DH + 2), D), jnp.float32) * 0.02
        out_W = jax.random.normal(k3, (D, H * DH), jnp.float32) * 0.02
        ln_g = jnp.ones((D,), jnp.float32)
        ln_b = jnp.zeros((D,), jnp.float32)
        return {'x': x, 'slow_W': slow_W, 'out_W': out_W, 'ln_g': ln_g, 'ln_b': ln_b}
    _L0_attn_all = _L0_attn_setup()
    _L0_attn_in = {k: v for k, v in _L0_attn_all.items() if k in ('slow_W', 'out_W', 'ln_g', 'ln_b')}
    del _L0_attn_all

    def _L0_ffn_setup():
        import jax, jax.numpy as jnp
        import numpy as np
        B, S, D, F, E, K = (8, 512, 64, 256, 8, 2)
        key = jax.random.key(seed)
        ks = jax.random.split(key, 10)
        s = 0.02
        return {'x': jax.random.normal(ks[0], (B, S, D), dtype=jnp.float32), 'Wr': jax.random.normal(ks[1], (D, E), dtype=jnp.float32) * s, 'W1s': jax.random.normal(ks[2], (D, F), dtype=jnp.float32) * s, 'b1s': jnp.zeros((F,), dtype=jnp.float32), 'W2s': jax.random.normal(ks[3], (F, D), dtype=jnp.float32) * s, 'b2s': jnp.zeros((D,), dtype=jnp.float32), 'W1p': jax.random.normal(ks[4], (E, D, F), dtype=jnp.float32) * s, 'b1p': jnp.zeros((E, F), dtype=jnp.float32), 'W2p': jax.random.normal(ks[5], (E, F, D), dtype=jnp.float32) * s, 'b2p': jnp.zeros((E, D), dtype=jnp.float32)}
    _L0_ffn_all = _L0_ffn_setup()
    _L0_ffn_in = {k: v for k, v in _L0_ffn_all.items() if k in ('Wr', 'W1s', 'b1s', 'W2s', 'b2s', 'W1p', 'b1p', 'W2p', 'b2p')}
    del _L0_ffn_all
    return {'x': x, 'L0_tok_W': _L0_tok_in['W'], 'L0_tok_b': _L0_tok_in['b'], 'L0_tok_gamma': _L0_tok_in['gamma'], 'L0_tok_beta': _L0_tok_in['beta'], 'L0_attn_slow_W': _L0_attn_in['slow_W'], 'L0_attn_out_W': _L0_attn_in['out_W'], 'L0_attn_ln_g': _L0_attn_in['ln_g'], 'L0_attn_ln_b': _L0_attn_in['ln_b'], 'L0_ffn_Wr': _L0_ffn_in['Wr'], 'L0_ffn_W1s': _L0_ffn_in['W1s'], 'L0_ffn_b1s': _L0_ffn_in['b1s'], 'L0_ffn_W2s': _L0_ffn_in['W2s'], 'L0_ffn_b2s': _L0_ffn_in['b2s'], 'L0_ffn_W1p': _L0_ffn_in['W1p'], 'L0_ffn_b1p': _L0_ffn_in['b1p'], 'L0_ffn_W2p': _L0_ffn_in['W2p'], 'L0_ffn_b2p': _L0_ffn_in['b2p']}

def reference(x, L0_tok_W, L0_tok_b, L0_tok_gamma, L0_tok_beta, L0_attn_slow_W, L0_attn_out_W, L0_attn_ln_g, L0_attn_ln_b, L0_ffn_Wr, L0_ffn_W1s, L0_ffn_b1s, L0_ffn_W2s, L0_ffn_b2s, L0_ffn_W1p, L0_ffn_b1p, L0_ffn_W2p, L0_ffn_b2p):
    import jax
    import jax.numpy as jnp

    def _L0_tok_ref(x, W, b, gamma, beta):
        import jax, jax.numpy as jnp
        import numpy as np
        PATCH = 16
        STRIDE = 8
        EPS = 1e-05
        B, S, F = x.shape
        starts = jnp.arange(0, S - PATCH + 1, STRIDE)
        idx = starts[:, None] + jnp.arange(PATCH)[None, :]
        patches = x[:, idx, :].reshape(B, idx.shape[0], PATCH * F)
        y = jnp.einsum('bpi,di->bpd', patches, W) + b
        mu = jnp.mean(y, axis=-1, keepdims=True)
        var = jnp.mean(jnp.square(y - mu), axis=-1, keepdims=True)
        return (y - mu) * jax.lax.rsqrt(var + EPS) * gamma + beta

    def _L0_attn_ref(x, slow_W, out_W, ln_g, ln_b):
        import jax, jax.numpy as jnp
        import numpy as np
        S, B, D, H, DH = (128, 32, 64, 8, 32)
        LN_EPS = 1e-05

        def elu_p1(x):
            return jax.nn.elu(x) + 1.0

        def sum_norm(x):
            return x / jnp.sum(x, axis=-1, keepdims=True)

        def layer_norm(x, g, b):
            mu = jnp.mean(x, axis=-1, keepdims=True)
            var = jnp.mean(jnp.square(x - mu), axis=-1, keepdims=True)
            return (x - mu) * jax.lax.rsqrt(var + LN_EPS) * g + b

        def _fast_rnn_forward(x, slow_W, out_W, ln_g, ln_b):
            slen, bsz, _ = x.shape
            o = layer_norm(x, ln_g, ln_b)
            qkv = jnp.einsum('sbd,ed->sbe', o, slow_W)
            qkv = qkv.reshape(slen, bsz, H, 5 * DH + 2)
            q, k, v, rk, rv, beta, rbeta = jnp.split(qkv, [DH, 2 * DH, 3 * DH, 4 * DH, 5 * DH, 5 * DH + 1], axis=-1)
            beta = jax.nn.sigmoid(beta)
            rbeta = jax.nn.sigmoid(rbeta)
            q = sum_norm(elu_p1(q))
            k = sum_norm(elu_p1(k))
            rk = jax.nn.softmax(rk, axis=-1)

            def ff_step(W, inp):
                qt, kt, vt, bt = inp
                v_old = jnp.einsum('bhij,bhj->bhi', W, kt)
                W = W + (bt * (vt - v_old))[..., :, None] * kt[..., None, :]
                z = jnp.einsum('bhij,bhj->bhi', W, qt)
                return (W, z)
            W0 = jnp.zeros((bsz, H, DH, DH), x.dtype)
            _, z = jax.lax.scan(ff_step, W0, (q, k, v, beta))

            def rec_step(carry, inp):
                R, h = carry
                zt, kt, vt, bt = inp
                q_rec = jax.nn.softmax(h, axis=-1)
                v_old = jnp.einsum('bhij,bhj->bhi', R, kt)
                R = R + (bt * (vt - v_old))[..., :, None] * kt[..., None, :]
                h = zt + jnp.einsum('bhij,bhj->bhi', R, q_rec)
                return ((R, h), h)
            R0 = jnp.zeros((bsz, H, DH, DH), x.dtype)
            h0 = jnp.zeros((bsz, H, DH), x.dtype)
            _, hs = jax.lax.scan(rec_step, (R0, h0), (z, rk, rv, rbeta))
            out = hs.reshape(slen, bsz, H * DH)
            out = jnp.einsum('sbe,de->sbd', out, out_W)
            return x + out
        return _fast_rnn_forward(x, slow_W, out_W, ln_g, ln_b)

    def _L0_ffn_ref(x, Wr, W1s, b1s, W2s, b2s, W1p, b1p, W2p, b2p):
        import jax, jax.numpy as jnp
        import numpy as np
        B, S, D, F, E, K = (8, 512, 64, 256, 8, 2)
        gelu = lambda t: jax.nn.gelu(t, approximate=False)
        shared = gelu(x @ W1s + b1s) @ W2s + b2s
        rw = jax.nn.softmax(x @ Wr, axis=-1)
        topw, topi = jax.lax.top_k(rw, K)
        topw = topw / jnp.sum(topw, axis=-1, keepdims=True)
        mask = jnp.sum(jax.nn.one_hot(topi, E, dtype=topw.dtype) * topw[..., None], axis=-2)
        h = gelu(jnp.einsum('bsd,edf->bsef', x, W1p) + b1p)
        priv = jnp.einsum('bsef,efd->bsed', h, W2p) + b2p
        routed = jnp.einsum('bsed,bse->bsd', priv, mask)
        return shared + routed
    h = _L0_tok_ref(x, L0_tok_W, L0_tok_b, L0_tok_gamma, L0_tok_beta)
    h = h + _L0_attn_ref(_layernorm(h, axis=-1), L0_attn_slow_W, L0_attn_out_W, L0_attn_ln_g, L0_attn_ln_b)
    h = h + _L0_ffn_ref(_layernorm(h, axis=-1), L0_ffn_Wr, L0_ffn_W1s, L0_ffn_b1s, L0_ffn_W2s, L0_ffn_b2s, L0_ffn_W1p, L0_ffn_b1p, L0_ffn_W2p, L0_ffn_b2p)
    return h

_drawn_inputs = setup_inputs


def setup_inputs(seed=0):
    import zlib

    import numpy as np

    out = dict(_drawn_inputs(seed))
    spreads = {'L0_tok_gamma': (1.0, 0.2),
     'L0_tok_beta': (0.0, 0.1),
     'L0_attn_ln_g': (1.0, 0.6),
     'L0_attn_ln_b': (0.0, 0.8),
     'L0_ffn_b1s': (0.0, 0.8),
     'L0_ffn_b2s': (0.0, 0.1),
     'L0_ffn_b1p': (0.0, 0.8),
     'L0_ffn_b2p': (0.0, 0.311)}
    factors = {'L0_attn_slow_W': 8.0,
     'L0_attn_out_W': 8.0,
     'L0_ffn_W1s': 4.33,
     'L0_ffn_W2s': 3.672,
     'L0_ffn_W1p': 6.176,
     'L0_ffn_W2p': 5.229}
    for name, (base, spread) in spreads.items():
        noise = np.random.default_rng([zlib.crc32(name.encode()), seed]).standard_normal(out[name].shape)
        drawn = base * np.exp(spread * noise) if base else spread * noise
        out[name] = jnp.asarray(drawn.astype(out[name].dtype))
    for name, factor in factors.items():
        out[name] = (out[name] * factor).astype(out[name].dtype)
    return out
```

```python
from contextlib import ExitStack

import numpy as np

import concourse.bass as bass
from concourse import mybir

F32 = mybir.dt.float32
ALU = mybir.AluOpType
ACT = mybir.ActivationFunctionType
AX = mybir.AxisListType

S = 64
B = 92
DM = 64
H = 8
D = 32
HQ = H // 4
NT = B // 2
HD = H * D
NCH = B + 1
BLK = 16
NB = S // BLK
NP = 3 * HD + 2 * HD + 2 * H
EPS = 1e-5
E = 8
FC = 18


def bc(ap, axis, n):
    v = ap.unsqueeze(axis)
    shape = list(v.shape)
    shape[axis] = n
    return v.broadcast_to(shape)


class Chain:

    def __init__(self, sem):
        self.sem, self.n = sem, 0

    def note(self, ins):
        self.n += 1
        ins.then_inc(self.sem, 1)
        return ins


def over_tiles(engine, body):
    body(0, 0)
    body(1, 1)
    with engine.Fori(1, NT // 2 - 1) as pair:
        body(2 * pair, 0)
        body(2 * pair + 1, 1)
    body(NT - 2, 0)
    body(NT - 1, 1)


def embed(nc, io, sb, res, oT):
    P2 = [(0, 24), (24, NT)]
    with ExitStack() as ctx:
        def tile(name, shape):
            return ctx.enter_context(nc.sbuf_tensor(name, shape, F32))

        def sem(name):
            return ctx.enter_context(nc.semaphore(name))

        frames = tile("frames", [128, NCH, S])
        tokw = tile("tokw", [128, 2, DM])
        x = tile("x_tok", [128, NT, DM])
        xc = tile("x_centred", [128, NT, DM])
        sq = tile("x_squared", [128, NT, DM])
        ssum = tile("row_sum", [128, NT])
        nmean = tile("neg_mean", [128, NT])
        var = tile("row_var", [128, NT])
        rstd = tile("row_rstd", [128, NT])
        mhalf = tile("minus_half", [128, NT])
        rows, ident = sb["rows"], sb["ident"]
        yP = ctx.enter_context(nc.psum_tensor("yP", [128, 6 * 512], F32))
        tP = ctx.enter_context(nc.psum_tensor("tP", [64, 2, 512], F32))

        s_const = sem("e_const")
        s_frames = [sem(f"e_frames{i}") for i in range(2)]
        s_y = sem("e_y")
        s_cen = sem("e_centred")
        s_sq = sem("e_squared")
        s_var = sem("e_var")
        s_rstd = sem("e_rstd")
        s_half = sem("e_half")
        s_o = sem("e_o")
        s_tr = sem("e_tr")
        s_ev = sem("e_ev")
        s_dve = sem("e_dve")

        with nc.Block() as block:
            @block.sync
            def _(sp):
                half = 2 * P2[1][0] + 1
                sp.dma_start(tokw[:], io["tok_w"]).then_inc(s_const, 16)
                sp.dma_start(frames[:, 0:half, :], io["frames"][:, 0:half, :]).then_inc(s_frames[0], 16)
                sp.dma_start(frames[:, half:NCH, :], io["frames"][:, half:NCH, :]).then_inc(s_frames[1], 16)
                sp.dma_start(rows[:], io["rows"]).then_inc(s_const, 16)
                sp.dma_start(ident[:], io["ident"]).then_inc(s_const, 16)

            @block.tensor
            def _(pe):
                pe.wait_ge(s_const, 48)
                pe.wait_ge(s_frames[0], 16)
                for n in range(NT):
                    if n == P2[1][0]:
                        last.then_inc(s_y, 1)
                        pe.wait_ge(s_frames[1], 16)
                    for g in range(2):
                        last = nc.tensor.matmul(yP[:, n * DM:(n + 1) * DM], frames[:, 2 * n + g:2 * n + g + 2, :],
                                                tokw[:, g, :], start=(g == 0), stop=(g == 1))
                last.then_inc(s_y, 1)
                for g in range((NT + 3) // 4):
                    pe.wait_ge(s_o, 1 if 4 * g + 4 <= P2[0][1] else 2)
                    if g >= 2:
                        pe.wait_ge(s_ev, g - 1)
                    for j in range(min(4, NT - 4 * g)):
                        last = nc.tensor.transpose(tP[:, g % 2, j * 128:(j + 1) * 128], xc[:, 4 * g + j, :], ident[:])
                    last.then_inc(s_tr, 1)

            @block.scalar
            def _(act):
                for ln in range(3):
                    for p, (a, b) in enumerate(P2):
                        act.wait_ge(s_cen, 2 * ln + p + 1)
                        nc.scalar.activation(sq[:, a:b, :], xc[:, a:b, :], ACT.Square).then_inc(s_sq, 1)
                for g in range((NT + 3) // 4):
                    w = min(4, NT - 4 * g) * 128
                    act.wait_ge(s_tr, g + 1)
                    nc.scalar.copy(oT[:, g * 512:g * 512 + w], tP[:, g % 2, 0:w]).then_inc(s_ev, 1)

            @block.gpsimd
            def _(pool):
                nc.gpsimd.memset(mhalf[:], -0.5).then_inc(s_half, 1)
                pool.wait_ge(s_half, 1)
                for ln in range(3):
                    for p, (a, b) in enumerate(P2):
                        pool.wait_ge(s_var, 2 * ln + p + 1)
                        nc.gpsimd.tensor_tensor(rstd[:, a:b], var[:, a:b], mhalf[:, a:b], ALU.pow).then_inc(s_rstd, 1)

            @block.vector
            def _(dve):
                own = Chain(s_dve)

                def then(ins):
                    own.note(ins)
                    dve.wait_ge(s_dve, own.n)

                def row(r, a, b):
                    return bc(rows[:, r, :], 1, b - a)

                dve.wait_ge(s_const, 48)
                for p, (a, b) in enumerate(P2):
                    dve.wait_ge(s_y, p + 1)
                    yv = yP[:, a * DM:b * DM].rearrange("p (n d) -> p n d", d=DM)
                    own.note(nc.vector.tensor_tensor(x[:, a:b, :], yv, row(0, a, b), ALU.add))
                for ln in range(3):
                    dve.wait_ge(s_dve, own.n)
                    for p, (a, b) in enumerate(P2):
                        then(nc.vector.tensor_reduce(ssum[:, a:b], x[:, a:b, :], AX.X, ALU.add))
                        then(nc.vector.tensor_scalar(nmean[:, a:b], ssum[:, a:b], -1.0 / DM, None, ALU.mult))
                        nc.vector.tensor_tensor(xc[:, a:b, :], x[:, a:b, :], bc(nmean[:, a:b], 2, DM),
                                                ALU.add).then_inc(s_cen, 1)
                    for p, (a, b) in enumerate(P2):
                        dve.wait_ge(s_sq, 2 * ln + p + 1)
                        then(nc.vector.tensor_reduce(ssum[:, a:b], sq[:, a:b, :], AX.X, ALU.add))
                        nc.vector.tensor_scalar(var[:, a:b], ssum[:, a:b], 1.0 / DM, EPS, ALU.mult,
                                                ALU.add).then_inc(s_var, 1)
                    for p, (a, b) in enumerate(P2):
                        r = bc(rstd[:, a:b], 2, DM)
                        dve.wait_ge(s_rstd, 2 * ln + p + 1)
                        if ln == 0:
                            then(nc.vector.tensor_tensor(xc[:, a:b, :], xc[:, a:b, :], r, ALU.mult))
                            then(nc.vector.tensor_tensor(xc[:, a:b, :], xc[:, a:b, :], row(1, a, b), ALU.mult))
                            then(nc.vector.tensor_tensor(x[:, a:b, :], xc[:, a:b, :], row(2, a, b), ALU.add))
                        elif ln == 1:
                            own.note(nc.vector.tensor_tensor(res[:, a:b, :], xc[:, a:b, :], r, ALU.mult))
                            dve.wait_ge(s_dve, own.n)
                            own.note(nc.vector.tensor_tensor(sq[:, a:b, :], x[:, a:b, :], res[:, a:b, :], ALU.add))
                            dve.wait_ge(s_dve, own.n)
                            own.note(nc.vector.tensor_copy(x[:, a:b, :], res[:, a:b, :]))
                            dve.wait_ge(s_dve, own.n)
                            own.note(nc.vector.tensor_copy(res[:, a:b, :], sq[:, a:b, :]))
                            dve.wait_ge(s_dve, own.n)
                        else:
                            then(nc.vector.tensor_tensor(xc[:, a:b, :], xc[:, a:b, :], r, ALU.mult))
                            then(nc.vector.tensor_tensor(xc[:, a:b, :], xc[:, a:b, :], row(3, a, b), ALU.mult))
                            nc.vector.tensor_tensor(xc[:, a:b, :], xc[:, a:b, :], row(4, a, b),
                                                    ALU.add).then_inc(s_o, 1)


def features(nc, io, sb, oT):
    OWN = 3
    with ExitStack() as ctx:
        def tile(name, shape):
            return ctx.enter_context(nc.sbuf_tensor(name, shape, F32))

        def sem(name):
            return ctx.enter_context(nc.semaphore(name))

        ident = sb["ident"]
        w = tile("slow_w", [DM, NP])
        ot = tile("o_tile", [DM, 2, 128])
        low = tile("min_qk", [128, 2 * HD])
        top = tile("max_rk", [128, H])
        feat = tile("feat", [128, 3 * HD])
        tot = tile("feat_sum", [128, 3 * H])
        rtot = tile("feat_rsum", [128, 3 * H])
        gate = tile("gate", [128, 2 * H])
        fn = tile("feat_n", [128, 2, 3 * HD])
        ft = tile("feat_t", [128, 2, 3 * HD])
        val = tile("val", [128, 2, 2 * HD + 2 * H])
        diag = tile("diag", [128, 2, 2, HD])
        pq = ctx.enter_context(nc.psum_tensor("proj", [128, 3, 512], F32))
        pt = ctx.enter_context(nc.psum_tensor("turned", [128, 512], F32))
        pg = ctx.enter_context(nc.psum_tensor("gram", [128, 4, 512], F32))

        s_w = sem("f_w")
        s_ot = sem("f_ot")
        s_proj = sem("f_proj")
        s_low = sem("f_low")
        s_exp = sem("f_exp")
        s_rk0 = sem("f_rk0")
        s_rk1 = sem("f_rk1")
        s_pqdve = sem("f_pqdve")
        s_pqact = sem("f_pqact")
        s_gate = sem("f_gate")
        s_gexp = sem("f_gexp")
        s_rs = sem("f_rs")
        s_fn = sem("f_fn")
        s_val = sem("f_val")
        s_tr = sem("f_tr")
        s_ft = sem("f_ft")
        s_alone = sem("f_alone")
        s_gr = sem("f_gr")
        s_dg = sem("f_dg")
        s_out = [[sem(f"f_out{p}{j}") for j in range(3)] for p in range(2)]
        s_dve = sem("f_dve")

        with nc.Block() as block:
            @block.sync
            def _(sp):
                sp.dma_start(w[:], io["slow_w"]).then_inc(s_w, 16)
                for p in range(2):
                    sp.sem_inc(s_out[p][2], 16)

                def body(n, p):
                    sp.wait_ge(s_ft, 2 * n + 2)
                    sp.dma_start(io["feat"][n], ft[:, p, :]).then_inc(s_out[p][0], 16)
                    for g in range(HQ):
                        src = ft[:, p, (4 + g) * 128:(5 + g) * 128].rearrange("p (b a s) -> p a b s", b=2, a=2)
                        dst = io["rk"][:, g].rearrange("p a (n b s) -> p n a b s", b=2, s=S // 2)
                        for half in range(2):
                            sp.dma_start(dst[:, n, half], src[:, half]).then_inc(s_out[p][0], 16)
                    sp.wait_ge(s_val, n + 1)
                    sp.dma_start(io["val"][n], val[:, p, :]).then_inc(s_out[p][1], 16)
                    sp.wait_ge(s_dg, n + 1)
                    for y in range(2):
                        sp.dma_start(io["diag"][y][n], diag[:, p, y, :]).then_inc(s_out[p][2], 16)

                over_tiles(sp, body)
                for p in range(2):
                    sp.wait_ge(s_out[p][0], 80 * (NT // 2))
                    sp.wait_ge(s_out[p][1], 16 * (NT // 2))
                    sp.wait_ge(s_out[p][2], 32 * (NT // 2) + 16)

            def stored(eng, n, p, which, per=16):
                if isinstance(n, int):
                    if n < 2:
                        return
                    eng.wait_ge(s_out[p][which], per * (n // 2))
                else:
                    eng.wait_ge(s_out[p][which], (n - p) * (per // 2))

            def after(eng, sem_, v):
                if not isinstance(v, int) or v > 0:
                    eng.wait_ge(sem_, v)

            @block.gpsimd
            def _(pool):
                def body(n, p):
                    after(pool, s_proj, n - 1)
                    nc.gpsimd.tensor_copy(ot[:, p, :], oT[:, bass.ts(n, 128)]).then_inc(s_ot, 1)
                    pool.wait_ge(s_rs, n + 1)
                    after(pool, s_tr, 2 * n - 2)
                    f3 = feat[:].rearrange("p (g d) -> p g d", d=D)
                    nc.gpsimd.tensor_tensor(fn[:, p, :].rearrange("p (g d) -> p g d", d=D), f3,
                                            bc(rtot[:], 2, D), ALU.mult).then_inc(s_fn, 1)
                over_tiles(pool, body)

            @block.tensor
            def _(pe):
                def project(n, p):
                    pe.wait_ge(s_ot, n + 1)
                    after(pe, s_pqdve, n)
                    after(pe, s_pqact, n)
                    nc.tensor.matmul(pq[:, 0, :], ot[:, p, :], w[:, 0:512], start=True, stop=True)
                    nc.tensor.matmul(pq[:, 1, 0:HD + 2 * H], ot[:, p, :], w[:, 2 * HD:3 * HD + 2 * H], start=True,
                                     stop=True)
                    nc.tensor.matmul(pq[:, 2, :], ot[:, p, :], w[:, 3 * HD + 2 * H:NP], start=True,
                                     stop=True).then_inc(s_proj, 1)

                def grams(n, p):
                    pe.wait_ge(s_fn, n + 1)
                    after(pe, s_ft, 2 * n)
                    after(pe, s_dg, n)
                    for j in range(4):
                        last = nc.tensor.transpose(pt[:, j * 128:(j + 1) * 128],
                                                   fn[:, p, j * 128:(j + 1) * 128], ident[:])
                    last.then_inc(s_tr, 1)
                    for j in range(2):
                        last = nc.tensor.transpose(pg[:, j, 256:384], fn[:, p, (4 + j) * 128:(5 + j) * 128], ident[:])
                    last.then_inc(s_tr, 1)
                    pe.wait_ge(s_ft, 2 * n + 2)
                    nc.tensor.sem_inc(s_alone, 1)
                    for y in range(2):
                        for g in range(HQ):
                            c = (2 + 2 * y + g) * 128
                            for tb in range(4):
                                for h4 in range(4):
                                    q = slice(32 * h4, 32 * h4 + 32)
                                    cc = c + 32 * tb
                                    o = (y * HQ + g) * 32
                                    last = nc.tensor.matmul(pg[32 * tb:32 * tb + 32, h4, o:o + 32],
                                                            ft[q, p, cc:cc + 32], ft[q, p, cc:cc + 32],
                                                            start=True, stop=True)
                    last.then_inc(s_gr, 1)

                pe.wait_ge(s_w, 16)
                project(0, 0)

                def body(n, p):
                    if isinstance(n, int) and n == NT - 1:
                        grams(n, p)
                        return
                    project(n + 1, 1 - p)
                    grams(n, p)
                over_tiles(pe, body)

            @block.scalar
            def _(act):
                def body(n, p):
                    act.wait_ge(s_proj, n + 1)
                    stored(act, n, p, 1)
                    nc.scalar.copy(val[:, p, 0:2 * HD], pq[:, 2, :]).then_inc(s_pqact, 1)
                    act.wait_ge(s_low, n + 1)
                    nc.scalar.activation(low[:], low[:], ACT.Exp).then_inc(s_exp, 1)
                    act.wait_ge(s_gate, n + 1)
                    nc.scalar.activation(gate[:], gate[:], ACT.Exp, scale=-1.0).then_inc(s_gexp, 1)
                    act.wait_ge(s_rk0, n + 1)
                    nc.scalar.activation(feat[:, 2 * HD:3 * HD], feat[:, 2 * HD:3 * HD], ACT.Exp).then_inc(s_rk1, 1)
                    act.wait_ge(s_tr, 2 * n + 1)
                    stored(act, n, p, 0, 80)
                    nc.scalar.copy(ft[:, p, 0:512], pt[:]).then_inc(s_ft, 1)
                    act.wait_ge(s_tr, 2 * n + 2)
                    nc.scalar.copy(ft[:, p, 512:768].rearrange("p (a b) -> p a b", a=2),
                                   pg[:, 0:2, 256:384]).then_inc(s_ft, 1)
                over_tiles(act, body)

            @block.vector
            def _(dve):
                def scale_diag(n, p):
                    dve.wait_ge(s_gr, n + 1)
                    if not isinstance(n, int):
                        dve.wait_ge(s_out[p][2], (n - p) * 16 + 16)
                    elif n >= 2:
                        dve.wait_ge(s_out[p][2], 32 * (n // 2) + 16)
                    for y in range(2):
                        for g in range(HQ):
                            o = (y * HQ + g) * 32
                            b4 = val[:, p, 2 * HD + y * H + 4 * g:2 * HD + y * H + 4 * g + 4]
                            last = nc.vector.tensor_tensor(
                                diag[:, p, y, g * 128:(g + 1) * 128].rearrange("p (h s) -> p h s", s=32),
                                pg[:, :, o:o + 32], bc(b4, 2, 32), ALU.mult)
                    last.then_inc(s_dg, 1)

                def body(n, p):
                    f3 = feat[:].rearrange("p (g d) -> p g d", d=D)
                    dve.wait_ge(s_proj, n + 1)
                    after(dve, s_exp, n)
                    nc.vector.tensor_scalar(low[:], pq[:, 0, :], 0.0, None, ALU.min).then_inc(s_low, 1)
                    r3 = pq[:, 1, 0:HD].rearrange("p (g d) -> p g d", d=D)
                    nc.vector.tensor_reduce(top[:], r3, AX.X, ALU.max).then_inc(s_dve, 1)
                    nc.vector.tensor_copy(gate[:], pq[:, 1, HD:HD + 2 * H]).then_inc(s_gate, 1)
                    after(dve, s_fn, n)
                    dve.wait_ge(s_dve, OWN * n + 1)
                    nc.vector.tensor_tensor(f3[:, 2 * H:3 * H, :], r3, bc(top[:], 2, D),
                                            ALU.subtract).then_inc(s_rk0, 1)
                    dve.wait_ge(s_exp, n + 1)
                    nc.vector.scalar_tensor_tensor(out=feat[:, 0:2 * HD], in0=pq[:, 0, :], scalar=0.0, in1=low[:],
                                                   op0=ALU.max, op1=ALU.add).then_inc(s_pqdve, 1)
                    dve.wait_ge(s_gexp, n + 1)
                    nc.vector.tensor_scalar(gate[:], gate[:], 1.0, None, ALU.add).then_inc(s_dve, 1)
                    dve.wait_ge(s_rk1, n + 1)
                    dve.wait_ge(s_pqdve, n + 1)
                    nc.vector.tensor_reduce(tot[:], f3, AX.X, ALU.add).then_inc(s_dve, 1)
                    dve.wait_ge(s_dve, OWN * n + 2)
                    dve.wait_ge(s_pqact, n + 1)
                    stored(dve, n, p, 1)
                    nc.vector.reciprocal(val[:, p, 2 * HD:2 * HD + 2 * H], gate[:]).then_inc(s_val, 1)
                    dve.wait_ge(s_dve, OWN * n + 3)
                    nc.vector.reciprocal(rtot[:], tot[:]).then_inc(s_rs, 1)
                    if not (isinstance(n, int) and n == 0):
                        scale_diag(n - 1, 1 - p)
                over_tiles(dve, body)
                scale_diag(NT - 1, (NT - 1) % 2)


def inverses(nc, io):
    with ExitStack() as ctx:
        def tile(name, shape):
            return ctx.enter_context(nc.sbuf_tensor(name, shape, F32))

        def sem(name):
            return ctx.enter_context(nc.semaphore(name))

        HS = S // 2
        a = tile("a_half", [B, 2, HS, HD])
        tt = tile("t_transposed", [B, 2, S, H * BLK])
        prod = tile("products", [B, 2, H * (BLK - 1) * (BLK - 1)])
        s_in = [sem(f"i_in{j}") for j in range(2)]
        s_init = sem("i_init")
        s_done = sem("i_done")
        s_out = sem("i_out")
        s_dve = sem("i_dve")
        parts = [(y, half) for y in range(2) for half in range(2)]

        with nc.Block() as block:
            @block.sync
            def _(sp):
                for k, (y, half) in enumerate(parts):
                    if k >= 2:
                        sp.wait_ge(s_done, k - 1)
                    src = io["diag"][y][:].rearrange("n (b t) c -> (n b) t c", b=2)
                    sp.dma_start(a[:, k % 2], src[:, half * HS:(half + 1) * HS, :]).then_inc(s_in[k % 2], 16)
                    if k >= 1:
                        yy, hh = parts[k - 1]
                        sp.wait_ge(s_done, k)
                        dst = io["tinv"][yy][:].rearrange("n (b t) c -> (n b) t c", b=2)
                        sp.dma_start(dst[:, hh * HS:(hh + 1) * HS, :],
                                     tt[:, yy, hh * HS:(hh + 1) * HS, :]).then_inc(s_out, 16)
                yy, hh = parts[-1]
                sp.wait_ge(s_done, len(parts))
                dst = io["tinv"][yy][:].rearrange("n (b t) c -> (n b) t c", b=2)
                sp.dma_start(dst[:, hh * HS:(hh + 1) * HS, :],
                             tt[:, yy, hh * HS:(hh + 1) * HS, :]).then_inc(s_out, 16)
                sp.wait_ge(s_out, 16 * len(parts))

            @block.gpsimd
            def _(pool):
                nc.gpsimd.memset(tt[:], 0.0).then_inc(s_init, 1)
                pool.wait_ge(s_init, 1)
                for x in range(BLK):
                    diag = tt[:].rearrange("p y (k x) (h t) -> p (y k) x h t", x=BLK, t=BLK)[:, :, x, :, x]
                    last = nc.gpsimd.memset(diag, 1.0)
                last.then_inc(s_init, 1)

            @block.vector
            def _(dve):
                own = Chain(s_dve)
                dve.wait_ge(s_init, 2)
                for k, (y, half) in enumerate(parts):
                    dve.wait_ge(s_in[k % 2], 16 * (k // 2 + 1))
                    for t in range(1, BLK):
                        n = H * t * t
                        for blk in range(2):
                            rows_ = a[:, k % 2, blk * BLK + t, :].rearrange("p (h s) -> p h s", s=2 * BLK)
                            arow = bc(rows_[:, :, blk * BLK:blk * BLK + t], 2, t)
                            x0 = (half * 2 + blk) * BLK
                            tprev = tt[:, y, x0:x0 + t, :].rearrange("p x (h t) -> p h x t", t=BLK)[:, :, :, 0:t]
                            dve.wait_ge(s_dve, own.n)
                            pr = prod[:, blk, 0:n].rearrange("p (h x s) -> p h x s", x=t, s=t)
                            own.note(nc.vector.tensor_tensor(pr, arow, tprev, ALU.mult))
                        for blk in range(2):
                            x0 = (half * 2 + blk) * BLK
                            pr = prod[:, blk, 0:n].rearrange("p (h x s) -> p h x s", x=t, s=t)
                            dst = tt[:, y, x0:x0 + t, :].rearrange("p x (h t) -> p h x t", t=BLK)[:, :, :, t]
                            dve.wait_ge(s_dve, own.n - (1 if blk == 0 else 1))
                            last = own.note(nc.vector.tensor_reduce(dst, pr, AX.X, ALU.add, negate=True))
                    dve.wait_ge(s_dve, own.n)
                    nc.vector.sem_inc(s_done, 1)


def solve(nc, io):
    with ExitStack() as ctx:
        def tile(name, shape):
            return ctx.enter_context(nc.sbuf_tensor(name, shape, F32))

        def sem(name):
            return ctx.enter_context(nc.semaphore(name))

        ROUNDS = NB - 1
        ft = tile("s_ft", [128, 2, 3 * HD])
        val = tile("s_val", [128, 2, 2 * HD + 2 * H])
        tc = tile("s_tcompact", [128, 2, 2, H * BLK])
        masks = tile("s_masks", [128, 2, 128])
        own_blk = tile("s_ownblk", [128, 8])
        tx = [tile(f"s_tx{p}", [128, 2, H, 128]) for p in range(2)]
        gm = [tile(f"s_gm{p}", [128, 3, 4, HQ, 128]) for p in range(2)]
        u = tile("s_u", [128, 2, 2, HD])
        r = tile("s_r", [128, 2, HD])
        zo = tile("s_z", [128, 2, HQ * 128])
        pg = ctx.enter_context(nc.psum_tensor("s_gram", [128, 4, 512], F32))
        pu = ctx.enter_context(nc.psum_tensor("s_pu", [128, 2, 512], F32))
        pr = ctx.enter_context(nc.psum_tensor("s_pr", [128, 2, 512], F32))

        s_c = sem("s_const")
        s_in = [sem(f"s_in{p}") for p in range(2)]
        s_tb = sem("s_tb")
        s_tx = sem("s_txr")
        s_pg = sem("s_pg")
        s_gm = sem("s_gmr")
        s_pu = [sem(f"s_pu{y}") for y in range(2)]
        s_u = [sem(f"s_ur{y}") for y in range(2)]
        s_pr = [sem(f"s_pr{y}") for y in range(2)]
        s_r = [sem(f"s_rr{y}") for y in range(2)]
        s_pz = sem("s_pz")
        s_z = sem("s_zr")
        s_zout = [sem(f"s_zout{p}") for p in range(2)]
        s_uout = [sem(f"s_uout{p}") for p in range(2)]

        def after(eng, sem_, v):
            if not isinstance(v, int) or v > 0:
                eng.wait_ge(sem_, v)

        def loaded(eng, n, p):
            if isinstance(n, int):
                eng.wait_ge(s_in[p], 64 * (n // 2 + 1))
            else:
                eng.wait_ge(s_in[p], (n - p) * 32 + 64)

        def stored(eng, sems, n, p):
            if isinstance(n, int):
                if n >= 2:
                    eng.wait_ge(sems[p], 16 * (n // 2))
            else:
                eng.wait_ge(sems[p], (n - p) * 8)

        with nc.Block() as block:
            @block.sync
            def _(sp):
                sp.dma_start(masks[:], io["masks"]).then_inc(s_c, 16)
                sp.dma_start(own_blk[:], io["own_blk"]).then_inc(s_c, 16)

                def load(n, p):
                    after(sp, s_r[0], ROUNDS * (n - 1))
                    after(sp, s_r[1], ROUNDS * (n - 1))
                    after(sp, s_pg, 3 * (n - 1))
                    sp.dma_start(ft[:, p, :], io["feat"][n]).then_inc(s_in[p], 16)
                    sp.dma_start(val[:, p, :], io["val"][n]).then_inc(s_in[p], 16)
                    for y in range(2):
                        sp.dma_start(tc[:, p, y, :], io["tinv"][y][n]).then_inc(s_in[p], 16)

                def store(n, p):
                    sp.wait_ge(s_u[1], (ROUNDS + 1) * (n + 1))
                    sp.dma_start(io["u2"][n], u[:, p, 1, :]).then_inc(s_uout[p], 16)
                    sp.wait_ge(s_z, n + 1)
                    sp.dma_start(io["z"][:, :, n, :], zo[:, p, :].rearrange("p (a b) -> p a b", a=HQ)).then_inc(
                        s_zout[p], 16)

                load(0, 0)
                load(1, 1)

                def body(n, p):
                    if not (isinstance(n, int) and n < 2):
                        load(n, p)
                        store(n - 2, p)
                over_tiles(sp, body)
                store(NT - 2, 0)
                store(NT - 1, 1)
                for p in range(2):
                    sp.wait_ge(s_uout[p], 16 * (NT // 2))
                    sp.wait_ge(s_zout[p], 16 * (NT // 2))

            @block.gpsimd
            def _(pool):
                pool.wait_ge(s_c, 32)

                def body(n, p):
                    loaded(pool, n, p)
                    for y in range(2):
                        c3 = tc[:, p, y, :].rearrange("p (h t) -> p h t", t=BLK)
                        gates = val[:, p, 2 * HD + y * H:2 * HD + (y + 1) * H]
                        nc.gpsimd.tensor_tensor(c3, c3, bc(gates, 2, BLK), ALU.mult).then_inc(s_tb, 1)
                    for y in range(2):
                        after(pool, s_pu[y], (ROUNDS + 1) * (n - 1))
                        pool.wait_ge(s_tb, 2 * n + y + 1)
                        c3 = tc[:, p, y, :].rearrange("p (h t) -> p h t", t=BLK)
                        nc.gpsimd.tensor_tensor(tx[p][:, y].rearrange("p h (k t) -> p h k t", t=BLK),
                                                bc(c3, 2, 8), bc(bc(own_blk[:], 1, H), 3, BLK),
                                                ALU.mult).then_inc(s_tx, 1)
                over_tiles(pool, body)

            @block.tensor
            def _(pe):
                def gram(n, p, j):
                    lo, ro = [(2, 2), (4, 4), (2, 0)][j]
                    after(pe, s_gm, 3 * n + j)
                    for g in range(HQ):
                        for h4 in range(4):
                            q = slice(32 * h4, 32 * h4 + 32)
                            last = nc.tensor.matmul(pg[:, h4, g * 128:(g + 1) * 128],
                                                    ft[q, p, (lo + g) * 128:(lo + g + 1) * 128],
                                                    ft[q, p, (ro + g) * 128:(ro + g + 1) * 128],
                                                    start=True, stop=True)
                    last.then_inc(s_pg, 1)

                def apply_t(n, p, y, k):
                    if k == 0:
                        pe.wait_ge(s_tx, 2 * n + y + 1)
                        after(pe, s_u[y], (ROUNDS + 1) * n)
                    else:
                        pe.wait_ge(s_r[y], ROUNDS * n + k)
                    for h in range(H):
                        hs = slice(h * D, (h + 1) * D)
                        rhs = val[:, p, y * HD + h * D:y * HD + (h + 1) * D] if k == 0 else r[:, y, hs]
                        last = nc.tensor.matmul(pu[:, y, hs], tx[p][:, y, h, :], rhs, start=True, stop=True)
                    last.then_inc(s_pu[y], 1)

                def apply_g(n, p, y, k):
                    pe.wait_ge(s_u[y], (ROUNDS + 1) * n + k + 1)
                    if k == 0:
                        pe.wait_ge(s_gm, 3 * n + y + 1)
                        if y == 0:
                            after(pe, s_z, n)
                    for h in range(H):
                        hs = slice(h * D, (h + 1) * D)
                        last = nc.tensor.matmul(pr[:, y, hs], gm[p][:, y, h % 4, h // 4, :], u[:, p, y, hs],
                                                start=True, stop=True)
                    last.then_inc(s_pr[y], 1)

                def z_of(n, p):
                    pe.wait_ge(s_u[0], (ROUNDS + 1) * (n + 1))
                    pe.wait_ge(s_gm, 3 * n + 3)
                    for h in range(H):
                        q = 32 * (h % 4)
                        c = (h // 4) * 128
                        last = nc.tensor.matmul(pr[q:q + 32, 0, c:c + 128], u[:, p, 0, h * D:(h + 1) * D],
                                                gm[p][:, 2, h % 4, h // 4, :], start=True, stop=True)
                    last.then_inc(s_pz, 1)

                def body(n, p):
                    loaded(pe, n, p)
                    gram(n, p, 0)
                    apply_t(n, p, 0, 0)
                    gram(n, p, 1)
                    apply_t(n, p, 1, 0)
                    for k in range(ROUNDS):
                        for y in range(2):
                            apply_g(n, p, y, k)
                        if k == 0:
                            gram(n, p, 2)
                        for y in range(2):
                            apply_t(n, p, y, k + 1)
                    z_of(n, p)
                over_tiles(pe, body)

            @block.scalar
            def _(act):
                def body(n, p):
                    for k in range(ROUNDS + 1):
                        for y in range(2):
                            act.wait_ge(s_pu[y], (ROUNDS + 1) * n + k + 1)
                            if k == 0:
                                if y == 1:
                                    stored(act, s_uout, n, p)
                                after(act, s_pz, n - 1)
                            nc.scalar.copy(u[:, p, y, :], pu[:, y, 0:HD]).then_inc(s_u[y], 1)
                    act.wait_ge(s_pz, n + 1)
                    stored(act, s_zout, n, p)
                    nc.scalar.copy(zo[:, p, :], pr[:, 0, 0:HQ * 128]).then_inc(s_z, 1)
                over_tiles(act, body)

            @block.vector
            def _(dve):
                dve.wait_ge(s_c, 32)

                def mask(n, p, j):
                    dve.wait_ge(s_pg, 3 * n + j + 1)
                    m = masks[:, 1 if j == 2 else 0, :]
                    nc.vector.tensor_tensor(gm[p][:, j], pg[:, :, 0:HQ * 128].rearrange("p a (g t) -> p a g t", g=HQ),
                                            bc(bc(m, 1, HQ), 1, 4), ALU.mult).then_inc(s_gm, 1)

                def residual(n, p, y, k):
                    dve.wait_ge(s_pr[y], ROUNDS * n + k + 1)
                    nc.vector.tensor_tensor(r[:, y, :], val[:, p, y * HD:(y + 1) * HD], pr[:, y, 0:HD],
                                            ALU.subtract).then_inc(s_r[y], 1)

                def body(n, p):
                    loaded(dve, n, p)
                    after(dve, s_pz, n - 1)
                    after(dve, s_pr[1], ROUNDS * (n - 1))
                    mask(n, p, 0)
                    mask(n, p, 1)
                    for k in range(ROUNDS):
                        for y in range(2):
                            residual(n, p, y, k)
                        if k == 0:
                            mask(n, p, 2)
                over_tiles(dve, body)


def recur(nc, io, hs):
    STREAMS = [(0, 48), (48, B - 48)]
    W = 96
    HALF = S // 2
    with ExitStack() as ctx:
        def tile(name, shape):
            return ctx.enter_context(nc.sbuf_tensor(name, shape, F32))

        def sem(name):
            return ctx.enter_context(nc.semaphore(name))

        def sems(name):
            return [sem(f"r_{name}{i}") for i in range(2)]

        rk = tile("r_rk", [128, HQ, 2, B * HALF])
        u = tile("r_u", [128, 2, B // 4, HD])
        see = tile("r_see", [128, HALF, 16])
        q = [tile(f"r_q{i}", [128, W, 4]) for i in range(2)]
        am = [tile(f"r_am{i}", [128, 2, W, 4]) for i in range(2)]
        hc = [tile(f"r_h{i}", [128, W]) for i in range(2)]
        ht = [tile(f"r_ht{i}", [128, 3, D]) for i in range(2)]
        et = [tile(f"r_et{i}", [128, 3, D]) for i in range(2)]
        st = [tile(f"r_st{i}", [128, 3, 4]) for i in range(2)]
        pa = [ctx.enter_context(nc.psum_tensor(f"r_pa{i}", [128, 2, 512], F32)) for i in range(2)]
        ph = [ctx.enter_context(nc.psum_tensor(f"r_ph{i}", [128, 512], F32)) for i in range(2)]

        s_rk, s_u, s_z, s_see, s_q0 = ([sem(f"r_in_{k}{half}") for half in range(2)] for k in
                                       ("rk", "u", "z", "see", "q0"))
        s_q = sems("q")
        s_a = sems("a")
        s_am = sems("am")
        s_rq = sems("rq")
        s_h = sems("h")
        s_hs = sems("hs")
        s_ht = sems("ht")
        s_mx = sems("mx")
        s_sub = sems("sub")
        s_exp = sems("exp")
        s_sum = sems("sum")
        s_rec = sems("rec")
        s_nrm = sems("nrm")

        with nc.Block() as block:
            @block.sync
            def _(sp):
                for i in range(2):
                    sp.dma_start(q[i][:], io["first_q"]).then_inc(s_q0[i], 16)
                sp.dma_start(see[:], io["see4"]).then_inc(s_see[0], 16)
                for half in range(2):
                    sp.dma_start(rk[:, :, half, :], io["rk"][:, :, half, :]).then_inc(s_rk[half], 16)
                    for b in range(4):
                        n0, r0 = b // 2, (b % 2) * S + half * HALF
                        src = io["u2"][n0:NT:2, r0:r0 + HALF, :].rearrange("n s c -> s n c")
                        sp.dma_start(u[32 * b:32 * b + 32, half], src).then_inc(s_u[half], 16)
                    if half == 0:
                        sp.dma_start(hs[:].rearrange("p g b s -> p (g b s)"),
                                     io["z"][:].rearrange("p g n c -> p (g n c)")).then_inc(s_z[0], 16)

            @block.tensor
            def _(pe):
                def step(t, halves):
                    for i, (b0, nb) in enumerate(STREAMS):
                        pe.wait_ge(s_q[i], t + 1)
                        for half in range(halves):
                            for g in range(HQ):
                                for b in range(0, nb, 4):
                                    c = g * nb + b
                                    w = rk[:, g, half, (b0 + b) * HALF:(b0 + b + 4) * HALF]
                                    last = nc.tensor.matmul(pa[i][:, half, 4 * c:4 * c + 16], w, q[i][:, c:c + 4, :],
                                                            start=True, stop=True)
                            last.then_inc(s_a[i], 1)
                    for i, (b0, nb) in enumerate(STREAMS):
                        pe.wait_ge(s_am[i], t + 1 if halves == 1 else 2 * t + 2 - HALF)
                        for g in range(HQ):
                            for b in range(0, nb, 4):
                                c = g * nb + b
                                for half in range(halves):
                                    last = nc.tensor.matmul(ph[i][:, 4 * c:4 * c + 16],
                                                            u[:, half, (b0 + b) // 4, g * 128:(g + 1) * 128],
                                                            am[i][:, half, c:c + 4, :], start=(half == 0),
                                                            stop=(half == halves - 1))
                        last.then_inc(s_rq[i], 1)

                pe.wait_ge(s_rk[0], 16)
                pe.wait_ge(s_u[0], 64)
                with pe.Fori(0, HALF) as t:
                    step(t, 1)
                pe.wait_ge(s_rk[1], 16)
                pe.wait_ge(s_u[1], 64)
                with pe.Fori(HALF, S) as t:
                    step(t, 2)

            @block.scalar
            def _(act):
                with act.Fori(0, S) as t:
                    for i in range(2):
                        act.wait_ge(s_sub[i], t + 1)
                        nc.scalar.activation(et[i][:], et[i][:], ACT.Exp).then_inc(s_exp[i], 1)

            @block.gpsimd
            def _(pool):
                for i, (b0, nb) in enumerate(STREAMS):
                    nc.gpsimd.memset(hc[i][:], 0.0).then_inc(s_hs[i], 1)
                with pool.Fori(0, S) as t:
                    for i, (b0, nb) in enumerate(STREAMS):
                        pool.wait_ge(s_h[i], t + 1)
                        nc.gpsimd.tensor_copy(hs[:, :, b0:b0 + nb, t],
                                              hc[i][:, 0:HQ * nb].rearrange("p (g b) -> p g b", g=HQ)).then_inc(
                                                  s_hs[i], 1)

            @block.vector
            def _(dve):
                def mask(t, i, half, halves):
                    b0, nb = STREAMS[i]
                    dve.wait_ge(s_a[i], t + 1 if halves == 1 else 2 * t + 1 + half - HALF)
                    k = HQ * nb // 4
                    now = see[:, t, :] if halves == 1 else see[:, t - HALF, :] if half else see[:, HALF - 1, :]
                    nc.vector.tensor_tensor(
                        am[i][:, half, 0:HQ * nb, :].rearrange("p (k w) h -> p k (w h)", w=4),
                        pa[i][:, half, 0:4 * HQ * nb].rearrange("p (k w) -> p k w", k=k),
                        bc(now, 1, k), ALU.mult).then_inc(s_am[i], 1)

                def softmax(t, i):
                    b0, nb = STREAMS[i]
                    dve.wait_ge(s_rq[i], t + 1)
                    dve.wait_ge(s_hs[i], t + 1)
                    for h4 in range(4):
                        r = slice(32 * h4, 32 * h4 + 32)
                        last = nc.vector.tensor_tensor(
                            hc[i][r, 0:HQ * nb].rearrange("p (g b) -> p g b", g=HQ),
                            ph[i][r, 0:4 * HQ * nb].rearrange("p (g b h) -> p g b h", g=HQ, h=4)[:, :, :, h4],
                            hs[r, :, b0:b0 + nb, t], ALU.add)
                    last.then_inc(s_h[i], 1)
                    dve.wait_ge(s_h[i], t + 1)
                    nc.vector.transpose(ht[i][:].rearrange("p k d -> p (k d)"), hc[i][:]).then_inc(s_ht[i], 1)
                    dve.wait_ge(s_ht[i], t + 1)
                    nc.vector.tensor_reduce(st[i][:, :, 0], ht[i][:], AX.X, ALU.max).then_inc(s_mx[i], 1)
                    dve.wait_ge(s_mx[i], t + 1)
                    nc.vector.tensor_tensor(et[i][:], ht[i][:], bc(st[i][:, :, 0], 2, D),
                                            ALU.subtract).then_inc(s_sub[i], 1)

                def spread(t, i):
                    dve.wait_ge(s_exp[i], t + 1)
                    nc.vector.tensor_reduce(st[i][:, :, 1], et[i][:], AX.X, ALU.add).then_inc(s_sum[i], 1)
                    dve.wait_ge(s_sum[i], t + 1)
                    nc.vector.reciprocal(st[i][:, :, 2], st[i][:, :, 1]).then_inc(s_rec[i], 1)
                    dve.wait_ge(s_rec[i], t + 1)
                    nc.vector.tensor_tensor(et[i][:], et[i][:], bc(st[i][:, :, 2], 2, D),
                                            ALU.mult).then_inc(s_nrm[i], 1)
                    dve.wait_ge(s_nrm[i], t + 1)
                    for h4 in range(4):
                        r = slice(32 * h4, 32 * h4 + 32)
                        last = nc.vector.transpose(q[i][r, :, h4], et[i][r].rearrange("p k d -> p (k d)"))
                    last.then_inc(s_q[i], 1)

                def step(t, halves):
                    for i in range(2):
                        for half in range(halves):
                            mask(t, i, half, halves)
                    for i in range(2):
                        softmax(t, i)
                        spread(t, i)

                for i in range(2):
                    dve.wait_ge(s_q0[i], 16)
                    nc.vector.sem_inc(s_q[i], 1)
                dve.wait_ge(s_z[0], 16)
                dve.wait_ge(s_see[0], 16)
                with dve.Fori(0, HALF) as t:
                    step(t, 1)
                with dve.Fori(HALF, S) as t:
                    step(t, 2)


def ffn(nc, io, sb, res, hs):
    with ExitStack() as ctx:
        def tile(name, shape):
            return ctx.enter_context(nc.sbuf_tensor(name, shape, F32))

        def sem(name):
            return ctx.enter_context(nc.semaphore(name))

        ident, rows = sb["ident"], sb["rows"]
        n1 = tile("n1", [128, NT, DM])
        sq = tile("n1_sq", [128, NT, DM])
        nT = tile("n1_T", [DM, NT * 128])
        outw = tile("out_w", [128, HQ, DM])
        wr = tile("wr", [DM, E])
        w1 = tile("w1", [DM, FC, 128])
        b1 = tile("b1", [128, FC])
        w2 = tile("w2", [128, FC, DM])
        b2p = tile("b2p", [128, E, DM])
        earlier = tile("earlier", [128, E, E])
        stat = tile("f_stat", [128, 4, NT])
        mhalf = tile("f_mhalf", [128, NT])
        rw = tile("f_rw", [128, NT, E])
        wts = tile("f_wts", [128, NT, E])

        s_c = sem("p_const")
        s_o = sem("p_out")
        s_cen, s_sq, s_var, s_half, s_rstd, s_n1 = (sem(f"p_{k}") for k in ("cen", "sq", "var", "half", "rstd", "n1"))
        s_tr, s_ev = sem("p_tr"), sem("p_ev")
        s_log, s_sub, s_exp = sem("p_log"), sem("p_sub"), sem("p_exp")
        s_dve = sem("p_dve")

        with ExitStack() as inner:
            def psum(name, shape):
                return inner.enter_context(nc.psum_tensor(name, shape, F32))

            oP = psum("p_oP", [128, 6 * 512])
            tP = psum("p_tP", [64, 2, 512])
            gt = inner.enter_context(nc.sbuf_tensor("f_gt", [128, NT, E, E], F32))
            ge = inner.enter_context(nc.sbuf_tensor("f_ge", [128, NT, E, E], F32))
            PARTS = [(0, 24), (24, NT)]
            with nc.Block() as block:
                @block.sync
                def _(sp):
                    for dst, name in ((outw, "out_w"), (wr, "wr"), (w1, "w1"), (b1, "b1"), (w2, "w2"), (b2p, "b2p"),
                                      (earlier, "earlier")):
                        sp.dma_start(dst[:], io[name]).then_inc(s_c, 16)
                    sp.wait_ge(s_c, 7 * 16)

                @block.tensor
                def _(pe):
                    pe.wait_ge(s_c, 7 * 16)
                    for a, b in PARTS:
                        for n in range(a, b):
                            for g in range(HQ):
                                last = nc.tensor.matmul(oP[:, n * DM:(n + 1) * DM], hs[:, g, 2 * n:2 * n + 2, :],
                                                        outw[:, g, :], start=(g == 0), stop=(g == HQ - 1))
                        last.then_inc(s_o, 1)
                    for k in range((NT + 3) // 4):
                        pe.wait_ge(s_n1, 1 if 4 * k + 4 <= PARTS[0][1] else 2)
                        if k >= 2:
                            pe.wait_ge(s_ev, k - 1)
                        for j in range(min(4, NT - 4 * k)):
                            last = nc.tensor.transpose(tP[:, k % 2, j * 128:(j + 1) * 128], n1[:, 4 * k + j, :],
                                                       ident[:])
                        last.then_inc(s_tr, 1)
                    for n in range(NT):
                        if n % 4 == 0:
                            pe.wait_ge(s_ev, n // 4 + 1)
                        last = nc.tensor.matmul(oP[:, n * E:(n + 1) * E], nT[:, n * 128:(n + 1) * 128], wr[:],
                                                start=True, stop=True)
                    last.then_inc(s_log, 1)

                @block.scalar
                def _(act):
                    for p, (a, b) in enumerate(PARTS):
                        act.wait_ge(s_cen, p + 1)
                        nc.scalar.activation(sq[:, a:b, :], n1[:, a:b, :], ACT.Square).then_inc(s_sq, 1)
                    for k in range((NT + 3) // 4):
                        w = min(4, NT - 4 * k) * 128
                        act.wait_ge(s_tr, k + 1)
                        nc.scalar.copy(nT[:, k * 512:k * 512 + w], tP[:, k % 2, 0:w]).then_inc(s_ev, 1)
                    act.wait_ge(s_sub, 1)
                    nc.scalar.activation(rw[:], rw[:], ACT.Exp).then_inc(s_exp, 1)

                @block.gpsimd
                def _(pool):
                    nc.gpsimd.memset(mhalf[:], -0.5).then_inc(s_half, 1)
                    pool.wait_ge(s_half, 1)
                    for p, (a, b) in enumerate(PARTS):
                        pool.wait_ge(s_var, p + 1)
                        nc.gpsimd.tensor_tensor(stat[:, 3, a:b], stat[:, 2, a:b], mhalf[:, a:b],
                                                ALU.pow).then_inc(s_rstd, 1)

                @block.vector
                def _(dve):
                    own = Chain(s_dve)

                    def then(ins):
                        own.note(ins)
                        dve.wait_ge(s_dve, own.n)

                    for p, (a, b) in enumerate(PARTS):
                        dve.wait_ge(s_o, p + 1)
                        ov = oP[:, a * DM:b * DM].rearrange("p (n d) -> p n d", d=DM)
                        then(nc.vector.tensor_tensor(res[:, a:b, :], res[:, a:b, :], ov, ALU.add))
                        then(nc.vector.tensor_reduce(stat[:, 0, a:b], res[:, a:b, :], AX.X, ALU.add))
                        then(nc.vector.tensor_scalar(stat[:, 1, a:b], stat[:, 0, a:b], -1.0 / DM, None, ALU.mult))
                        nc.vector.tensor_tensor(n1[:, a:b, :], res[:, a:b, :], bc(stat[:, 1, a:b], 2, DM),
                                                ALU.add).then_inc(s_cen, 1)
                    for p, (a, b) in enumerate(PARTS):
                        dve.wait_ge(s_sq, p + 1)
                        then(nc.vector.tensor_reduce(stat[:, 0, a:b], sq[:, a:b, :], AX.X, ALU.add))
                        nc.vector.tensor_scalar(stat[:, 2, a:b], stat[:, 0, a:b], 1.0 / DM, EPS, ALU.mult,
                                                ALU.add).then_inc(s_var, 1)
                    for p, (a, b) in enumerate(PARTS):
                        dve.wait_ge(s_rstd, p + 1)
                        nc.vector.tensor_tensor(n1[:, a:b, :], n1[:, a:b, :], bc(stat[:, 3, a:b], 2, DM),
                                                ALU.mult).then_inc(s_n1, 1)
                    then(nc.vector.tensor_tensor(res[:], res[:], bc(rows[:, 5, :], 1, NT), ALU.add))
                    dve.wait_ge(s_log, 1)
                    lg = oP[:, 0:NT * E].rearrange("p (n e) -> p n e", e=E)
                    then(nc.vector.tensor_reduce(stat[:, 0, :], lg, AX.X, ALU.max))
                    nc.vector.tensor_tensor(rw[:], lg, bc(stat[:, 0, :], 2, E), ALU.subtract).then_inc(s_sub, 1)
                    dve.wait_ge(s_exp, 1)
                    then(nc.vector.tensor_reduce(stat[:, 0, :], rw[:], AX.X, ALU.add))
                    then(nc.vector.reciprocal(stat[:, 1, :], stat[:, 0, :]))
                    then(nc.vector.tensor_tensor(rw[:], rw[:], bc(stat[:, 1, :], 2, E), ALU.mult))
                    mine, other = bc(rw[:], 3, E), bc(rw[:], 2, E)
                    own.note(nc.vector.tensor_tensor(gt[:], other, mine, ALU.is_gt))
                    then(nc.vector.tensor_tensor(ge[:], other, mine, ALU.is_ge))
                    then(nc.vector.tensor_tensor(ge[:], ge[:], gt[:], ALU.subtract))
                    then(nc.vector.tensor_tensor(ge[:], ge[:], bc(earlier[:], 1, NT), ALU.mult))
                    then(nc.vector.tensor_tensor(ge[:], ge[:], gt[:], ALU.add))
                    then(nc.vector.tensor_reduce(wts[:], ge[:], AX.X, ALU.add))
                    then(nc.vector.scalar_tensor_tensor(out=wts[:], in0=wts[:], scalar=1.5, in1=rw[:],
                                                        op0=ALU.is_lt, op1=ALU.mult))
                    then(nc.vector.tensor_reduce(stat[:, 0, :], wts[:], AX.X, ALU.add))
                    then(nc.vector.reciprocal(stat[:, 1, :], stat[:, 0, :]))
                    then(nc.vector.tensor_tensor(wts[:], wts[:], bc(stat[:, 1, :], 2, E), ALU.mult))

        NG = NT // 2
        hg = [tile(f"hidden{i}", [128, 256]) for i in range(2)]
        ng = tile("n1_group", [DM, 2, 256])
        t1 = tile("weighted", [128, 2, E, DM])
        acc = tile("routed", [128, 2, DM])
        fin = tile("final", [128, 2, 2, DM])
        pH = ctx.enter_context(nc.psum_tensor("g_hid", [128, 2, 512], F32))
        pE = [ctx.enter_context(nc.psum_tensor(f"g_exp{i}", [128, 2, 512], F32)) for i in range(2)]
        pS = [ctx.enter_context(nc.psum_tensor(f"g_sh{i}", [128, 512], F32)) for i in range(2)]
        s_ng = sem("g_ng")
        s_hid = sem("g_hid")
        s_act = sem("g_act")
        s_exp2 = sem("g_expr")
        s_b = sem("g_bias")
        s_w = sem("g_weighted")
        s_r = sem("g_routed")
        s_s = sem("g_shared")
        s_f = sem("g_final")
        s_st = [sem(f"g_store{i}") for i in range(2)]

        def over_groups(engine, body):
            body(0, 0)
            body(1, 1)
            with engine.Fori(1, NG // 2) as pair:
                body(2 * pair, 0)
                body(2 * pair + 1, 1)
            body(NG - 1, 0)

        def after(eng, sem_, v):
            if not isinstance(v, int) or v > 0:
                eng.wait_ge(sem_, v)

        with nc.Block() as block:
            @block.tensor
            def _(pe):
                def down(j, p, c):
                    pe.wait_ge(s_act, FC * j + c + 1)
                    for a in range(2):
                        if c < 2 * E:
                            dst = pE[p][:, a, (c // 2) * DM:(c // 2 + 1) * DM]
                        else:
                            dst = pS[p][:, a * DM:(a + 1) * DM]
                        first = c % 2 == 0 and (c < 2 * E or a == 0)
                        last = nc.tensor.matmul(dst, hg[c % 2][:, a * 128:(a + 1) * 128], w2[:, c, :],
                                                start=first, stop=(c % 2 == 1), skip_group_check=c >= 2 * E)
                    return last

                def body(j, p):
                    after(pe, s_f, j - 1)
                    pe.wait_ge(s_ng, j + 1)
                    for c in range(FC):
                        if c >= 2:
                            pe.wait_ge(s_act, FC * j + c - 1)
                        else:
                            after(pe, s_act, FC * j + c - 1)
                        nc.tensor.matmul(pH[:, c % 2, 0:256], w1[:, c, :], ng[:, p, :], start=True,
                                         stop=True).then_inc(s_hid, 1)
                        if c:
                            down(j, p, c - 1)
                    down(j, p, FC - 1).then_inc(s_exp2, 1)
                over_groups(pe, body)

            @block.gpsimd
            def _(pool):
                def body(j, p):
                    after(pool, s_exp2, j - 1)
                    nc.gpsimd.tensor_copy(ng[:, p, :], nT[:, bass.ts(j, 256)]).then_inc(s_ng, 1)
                over_groups(pool, body)

            @block.scalar
            def _(act):
                def body(j, p):
                    for c in range(FC):
                        act.wait_ge(s_hid, FC * j + c + 1)
                        nc.scalar.activation(hg[c % 2][:], pH[:, c % 2, 0:256], ACT.Gelu,
                                             bias=b1[:, c:c + 1]).then_inc(s_act, 1)
                over_groups(act, body)

            @block.vector
            def _(dve):
                def body(j, p):
                    dve.wait_ge(s_exp2, j + 1)
                    for a in range(2):
                        nc.vector.tensor_tensor(t1[:, a], pE[p][:, a, :].rearrange("p (e d) -> p e d", e=E), b2p[:],
                                                ALU.add).then_inc(s_b, 1)
                    for a in range(2):
                        dve.wait_ge(s_b, 2 * j + a + 1)
                        nc.vector.tensor_tensor(t1[:, a], t1[:, a], bc(wts[:, 2 * j + a, :], 2, DM),
                                                ALU.mult).then_inc(s_w, 1)
                    for a in range(2):
                        dve.wait_ge(s_w, 2 * j + a + 1)
                        nc.vector.tensor_reduce(acc[:, a, :], t1[:, a].rearrange("p e d -> p d e"), AX.X,
                                                ALU.add).then_inc(s_r, 1)
                    for a in range(2):
                        dve.wait_ge(s_r, 2 * j + a + 1)
                        nc.vector.tensor_tensor(acc[:, a, :], acc[:, a, :], pS[p][:, a * DM:(a + 1) * DM],
                                                ALU.add).then_inc(s_s, 1)
                    dve.wait_ge(s_s, 2 * j + 2)
                    if isinstance(j, int):
                        after(dve, s_st[p], 32 * (j // 2))
                    else:
                        dve.wait_ge(s_st[p], (j - p) * 16)
                    nc.vector.tensor_tensor(fin[:, p], acc[:], res[:, bass.ts(j, 2), :], ALU.add).then_inc(s_f, 1)
                over_groups(dve, body)

            @block.sync
            def _(sp):
                def body(j, p):
                    sp.wait_ge(s_f, j + 1)
                    dst = io["out"].rearrange("s (j a b) d -> j b s a d", a=2, b=2)
                    for b in range(2):
                        sp.dma_start(dst[j, b], fin[b * S:(b + 1) * S, p]).then_inc(s_st[p], 16)
                over_groups(sp, body)
                sp.wait_ge(s_st[0], 32 * (NG - NG // 2))
                sp.wait_ge(s_st[1], 32 * (NG // 2))


def recur_and_ffn(nc, io, sb, res):
    with nc.sbuf_tensor("hs", [128, HQ, B, S], F32) as hs:
        recur(nc, io, hs)
        ffn(nc, io, sb, res, hs)


def program(nc, io):
    with ExitStack() as ctx:
        def tile(name, shape):
            return ctx.enter_context(nc.sbuf_tensor(name, shape, F32))

        def scratch(name, shape):
            return nc.dram_tensor(name, shape, F32, kind="Internal").ap()

        io["feat"] = scratch("d_feat", [NT, 128, 3 * HD])
        io["val"] = scratch("d_val", [NT, 128, 2 * HD + 2 * H])
        io["diag"] = [scratch(f"d_diag{y}", [NT, 128, HD]) for y in range(2)]
        io["tinv"] = [scratch(f"d_tinv{y}", [NT, 128, H * BLK]) for y in range(2)]
        io["u2"] = scratch("d_u2", [NT, 128, HD])
        io["rk"] = scratch("d_rk", [128, HQ, 2, B * S // 2])
        io["z"] = scratch("d_z", [128, HQ, NT, 128])
        res = tile("res", [128, NT, DM])
        sb = {"rows": tile("rows", [128, 6, DM]), "ident": tile("ident", [128, 128])}
        with nc.sbuf_tensor("oT", [DM, NT * 128], F32) as oT:
            embed(nc, io, sb, res, oT)
            features(nc, io, sb, oT)
        inverses(nc, io)
        solve(nc, io)
        recur_and_ffn(nc, io, sb, res)


OUT = ((S, B, DM), "float32")


def kernel(**inputs):
    import concourse.bacc as _bacc
    from concourse.bass_utils import run_bass_kernel_spmd as _run

    a = {k: np.asarray(v) for k, v in inputs.items()}
    frames = a["x"][:, :NCH * 8, :].reshape(S, NCH, 8 * 16).transpose(2, 1, 0)
    sw = a["L0_attn_slow_W"].reshape(H, 5 * D + 2, DM)
    parts = [sw[:, j * D:(j + 1) * D].reshape(HD, DM) for j in (0, 1, 3, 2, 4)]
    parts[3:3] = [sw[:, 5 * D], sw[:, 5 * D + 1]]
    rows = np.stack([a[k] for k in ("L0_tok_b", "L0_tok_gamma", "L0_tok_beta", "L0_attn_ln_g", "L0_attn_ln_b",
                                    "L0_ffn_b2s")])
    tok = np.arange(128)
    b_, t_ = tok // S, tok % S
    same = b_[:, None] == b_[None, :]
    before = same & (t_[:, None] // BLK < t_[None, :] // BLK)
    causal = same & (t_[:, None] <= t_[None, :])
    step = np.arange(S // 2)
    b4, s4 = tok // 32, tok % 32
    see4 = (s4[:, None, None] <= step[None, :, None]) & (b4[:, None, None] == np.arange(16)[None, None, :] // 4)
    e_ = np.arange(E)
    given = {
        "frames": frames,
        "tok_w": a["L0_tok_W"].T.reshape(2, 128, DM).transpose(1, 0, 2),
        "rows": np.broadcast_to(rows[None], (128, 6, DM)),
        "ident": np.eye(128, dtype=np.float32),
        "slow_w": np.concatenate(parts, 0).T,
        "masks": np.stack([before, causal], 1).astype(np.float32),
        "own_blk": (tok[:, None] // BLK == np.arange(8)[None, :]).astype(np.float32),
        "see4": see4.astype(np.float32),
        "first_q": np.broadcast_to((tok[:, None, None] // 32 == np.arange(4)) / np.float32(D), (128, 96, 4)).astype(np.float32),
        "out_w": a["L0_attn_out_W"].T.reshape(HQ, 128, DM).transpose(1, 0, 2),
        "wr": a["L0_ffn_Wr"],
        "w1": np.concatenate([a["L0_ffn_W1p"].transpose(1, 0, 2), a["L0_ffn_W1s"][:, None]], 1).reshape(DM, FC, 128),
        "b1": np.concatenate([a["L0_ffn_b1p"], a["L0_ffn_b1s"][None]], 0).reshape(FC, 128).T,
        "w2": np.concatenate([a["L0_ffn_W2p"], a["L0_ffn_W2s"][None]], 0).reshape(FC, 128, DM).transpose(1, 0, 2),
        "b2p": np.broadcast_to(a["L0_ffn_b2p"][None], (128, E, DM)),
        "earlier": np.broadcast_to((e_[None, :] < e_[:, None]).astype(np.float32), (128, E, E)),
    }
    nc = _bacc.Bacc("TRN2", target_bir_lowering=False, num_devices=1)
    arrays, io = {}, {}
    for name, v in given.items():
        v = np.ascontiguousarray(v)
        arrays[f"in_{name}"] = v
        io[name] = nc.dram_tensor(f"in_{name}", v.shape, mybir.dt.from_np(v.dtype), kind="ExternalInput").ap()
    io["out"] = nc.dram_tensor("out", OUT[0], F32, kind="ExternalOutput").ap()
    program(nc, io)
    r = _run(nc, [arrays], core_ids=[0])
    return r.results[0]["out"]
```

```python
from contextlib import ExitStack

import numpy as np

import concourse.bass as bass
from concourse import mybir

F32 = mybir.dt.float32
F16 = mybir.dt.float16
ALU = mybir.AluOpType
ACT = mybir.ActivationFunctionType
AX = mybir.AxisListType
RMAX = bass.bass_isa.ReduceOp.max

S = 64
B = 92
DM = 64
H = 8
D = 32
HQ = H // 4
NT = B // 2
HD = H * D
NCH = B + 1
BLK = 16
NB = S // BLK
NP = 3 * HD + 2 * HD + 2 * H
EPS = 1e-5
E = 8

UNIT = 2.0 ** 14
VTOP = 2.0 ** 9
FC = 18


def bc(ap, axis, n):
    v = ap.unsqueeze(axis)
    shape = list(v.shape)
    shape[axis] = n
    return v.broadcast_to(shape)


class Chain:

    def __init__(self, sem):
        self.sem, self.n = sem, 0

    def note(self, ins):
        self.n += 1
        ins.then_inc(self.sem, 1)
        return ins


def over_tiles(engine, body):
    body(0, 0)
    body(1, 1)
    with engine.Fori(1, NT // 2 - 1) as pair:
        body(2 * pair, 0)
        body(2 * pair + 1, 1)
    body(NT - 2, 0)
    body(NT - 1, 1)


def embed(nc, io, sb, res, oT):
    P2 = [(0, 24), (24, NT)]
    with ExitStack() as ctx:
        def tile(name, shape):
            return ctx.enter_context(nc.sbuf_tensor(name, shape, F32))

        def sem(name):
            return ctx.enter_context(nc.semaphore(name))

        frames = tile("frames", [128, NCH, S])
        tokw = tile("tokw", [128, 2, DM])
        x = tile("x_tok", [128, NT, DM])
        xc = tile("x_centred", [128, NT, DM])
        sq = tile("x_squared", [128, NT, DM])
        ssum = tile("row_sum", [128, NT])
        nmean = tile("neg_mean", [128, NT])
        var = tile("row_var", [128, NT])
        rstd = tile("row_rstd", [128, NT])
        mhalf = tile("minus_half", [128, NT])
        rows, ident = sb["rows"], sb["ident"]
        yP = ctx.enter_context(nc.psum_tensor("yP", [128, 6 * 512], F32))
        tP = ctx.enter_context(nc.psum_tensor("tP", [64, 2, 512], F32))

        s_const = sem("e_const")
        s_frames = [sem(f"e_frames{i}") for i in range(2)]
        s_y = sem("e_y")
        s_cen = sem("e_centred")
        s_sq = sem("e_squared")
        s_var = sem("e_var")
        s_rstd = sem("e_rstd")
        s_half = sem("e_half")
        s_o = sem("e_o")
        s_tr = sem("e_tr")
        s_ev = sem("e_ev")
        s_dve = sem("e_dve")

        with nc.Block() as block:
            @block.sync
            def _(sp):
                half = 2 * P2[1][0] + 1
                sp.dma_start(tokw[:], io["tok_w"]).then_inc(s_const, 16)
                sp.dma_start(frames[:, 0:half, :], io["frames"][:, 0:half, :]).then_inc(s_frames[0], 16)
                sp.dma_start(frames[:, half:NCH, :], io["frames"][:, half:NCH, :]).then_inc(s_frames[1], 16)
                sp.dma_start(rows[:], io["rows"]).then_inc(s_const, 16)
                sp.dma_start(ident[:], io["ident"]).then_inc(s_const, 16)

            @block.tensor
            def _(pe):
                pe.wait_ge(s_const, 48)
                pe.wait_ge(s_frames[0], 16)
                for n in range(NT):
                    if n == P2[1][0]:
                        last.then_inc(s_y, 1)
                        pe.wait_ge(s_frames[1], 16)
                    for g in range(2):
                        last = nc.tensor.matmul(yP[:, n * DM:(n + 1) * DM], frames[:, 2 * n + g:2 * n + g + 2, :],
                                                tokw[:, g, :], start=(g == 0), stop=(g == 1))
                last.then_inc(s_y, 1)
                for g in range((NT + 3) // 4):
                    pe.wait_ge(s_o, 1 if 4 * g + 4 <= P2[0][1] else 2)
                    if g >= 2:
                        pe.wait_ge(s_ev, g - 1)
                    for j in range(min(4, NT - 4 * g)):
                        last = nc.tensor.transpose(tP[:, g % 2, j * 128:(j + 1) * 128], xc[:, 4 * g + j, :], ident[:])
                    last.then_inc(s_tr, 1)

            @block.scalar
            def _(act):
                for ln in range(3):
                    for p, (a, b) in enumerate(P2):
                        act.wait_ge(s_cen, 2 * ln + p + 1)
                        nc.scalar.activation(sq[:, a:b, :], xc[:, a:b, :], ACT.Square).then_inc(s_sq, 1)
                for g in range((NT + 3) // 4):
                    w = min(4, NT - 4 * g) * 128
                    act.wait_ge(s_tr, g + 1)
                    nc.scalar.copy(oT[:, g * 512:g * 512 + w], tP[:, g % 2, 0:w]).then_inc(s_ev, 1)

            @block.gpsimd
            def _(pool):
                nc.gpsimd.memset(mhalf[:], -0.5).then_inc(s_half, 1)
                pool.wait_ge(s_half, 1)
                for ln in range(3):
                    for p, (a, b) in enumerate(P2):
                        pool.wait_ge(s_var, 2 * ln + p + 1)
                        nc.gpsimd.tensor_tensor(rstd[:, a:b], var[:, a:b], mhalf[:, a:b], ALU.pow).then_inc(s_rstd, 1)

            @block.vector
            def _(dve):
                own = Chain(s_dve)

                def then(ins):
                    own.note(ins)
                    dve.wait_ge(s_dve, own.n)

                def row(r, a, b):
                    return bc(rows[:, r, :], 1, b - a)

                dve.wait_ge(s_const, 48)
                for p, (a, b) in enumerate(P2):
                    dve.wait_ge(s_y, p + 1)
                    yv = yP[:, a * DM:b * DM].rearrange("p (n d) -> p n d", d=DM)
                    own.note(nc.vector.tensor_tensor(x[:, a:b, :], yv, row(0, a, b), ALU.add))
                for ln in range(3):
                    dve.wait_ge(s_dve, own.n)
                    for p, (a, b) in enumerate(P2):
                        then(nc.vector.tensor_reduce(ssum[:, a:b], x[:, a:b, :], AX.X, ALU.add))
                        then(nc.vector.tensor_scalar(nmean[:, a:b], ssum[:, a:b], -1.0 / DM, None, ALU.mult))
                        nc.vector.tensor_tensor(xc[:, a:b, :], x[:, a:b, :], bc(nmean[:, a:b], 2, DM),
                                                ALU.add).then_inc(s_cen, 1)
                    for p, (a, b) in enumerate(P2):
                        dve.wait_ge(s_sq, 2 * ln + p + 1)
                        then(nc.vector.tensor_reduce(ssum[:, a:b], sq[:, a:b, :], AX.X, ALU.add))
                        nc.vector.tensor_scalar(var[:, a:b], ssum[:, a:b], 1.0 / DM, EPS, ALU.mult,
                                                ALU.add).then_inc(s_var, 1)
                    for p, (a, b) in enumerate(P2):
                        r = bc(rstd[:, a:b], 2, DM)
                        dve.wait_ge(s_rstd, 2 * ln + p + 1)
                        if ln == 0:
                            then(nc.vector.tensor_tensor(xc[:, a:b, :], xc[:, a:b, :], r, ALU.mult))
                            then(nc.vector.tensor_tensor(xc[:, a:b, :], xc[:, a:b, :], row(1, a, b), ALU.mult))
                            then(nc.vector.tensor_tensor(x[:, a:b, :], xc[:, a:b, :], row(2, a, b), ALU.add))
                        elif ln == 1:
                            own.note(nc.vector.tensor_tensor(res[:, a:b, :], xc[:, a:b, :], r, ALU.mult))
                            dve.wait_ge(s_dve, own.n)
                            own.note(nc.vector.tensor_tensor(sq[:, a:b, :], x[:, a:b, :], res[:, a:b, :], ALU.add))
                            dve.wait_ge(s_dve, own.n)
                            own.note(nc.vector.tensor_copy(x[:, a:b, :], res[:, a:b, :]))
                            dve.wait_ge(s_dve, own.n)
                            own.note(nc.vector.tensor_copy(res[:, a:b, :], sq[:, a:b, :]))
                            dve.wait_ge(s_dve, own.n)
                        else:
                            then(nc.vector.tensor_tensor(xc[:, a:b, :], xc[:, a:b, :], r, ALU.mult))
                            then(nc.vector.tensor_tensor(xc[:, a:b, :], xc[:, a:b, :], row(3, a, b), ALU.mult))
                            nc.vector.tensor_tensor(xc[:, a:b, :], xc[:, a:b, :], row(4, a, b),
                                                    ALU.add).then_inc(s_o, 1)


def features(nc, io, sb, oT, rk16, vmax):
    OWN = 3
    with ExitStack() as ctx:
        def tile(name, shape):
            return ctx.enter_context(nc.sbuf_tensor(name, shape, F32))

        def sem(name):
            return ctx.enter_context(nc.semaphore(name))

        ident = sb["ident"]
        w = tile("slow_w", [DM, NP])
        ot = tile("o_tile", [DM, 2, 128])
        low = tile("min_qk", [128, 2 * HD])
        top = tile("max_rk", [128, H])
        feat = tile("feat", [128, 3 * HD])
        tot = tile("feat_sum", [128, 3 * H])
        rtot = tile("feat_rsum", [128, 3 * H])
        gate = tile("gate", [128, 2 * H])
        fn = tile("feat_n", [128, 2, 3 * HD])
        ft = tile("feat_t", [128, 2, 3 * HD])
        f16 = [ctx.enter_context(nc.sbuf_tensor(f"feat_t16_{j}", [128, 2, 3 * HD], F16)) for j in range(2)]
        val = tile("val", [128, 2, 2 * HD + 2 * H])
        diag = tile("diag", [128, 2, 2, HD])
        vtile = tile("vtile", [128, NT])
        pq = ctx.enter_context(nc.psum_tensor("proj", [128, 3, 512], F32))
        pt = ctx.enter_context(nc.psum_tensor("turned", [128, 512], F32))
        pg = ctx.enter_context(nc.psum_tensor("gram", [128, 4, 512], F32))

        s_w = sem("f_w")
        s_ot = sem("f_ot")
        s_proj = sem("f_proj")
        s_low = sem("f_low")
        s_exp = sem("f_exp")
        s_rk0 = sem("f_rk0")
        s_rk1 = sem("f_rk1")
        s_pqdve = sem("f_pqdve")
        s_pqact = sem("f_pqact")
        s_gate = sem("f_gate")
        s_gexp = sem("f_gexp")
        s_rs = sem("f_rs")
        s_fn = sem("f_fn")
        s_val = sem("f_val")
        s_tr = sem("f_tr")
        s_ft = sem("f_ft")
        s_rkc = sem("f_rkc")
        s_vm = sem("f_vm")
        s_vall = sem("f_vall")
        s_alone = sem("f_alone")
        s_f16 = [sem(f"f_f16_{j}") for j in range(2)]
        s_gr = sem("f_gr")
        s_dg = sem("f_dg")
        s_out = [[sem(f"f_out{p}{j}") for j in range(3)] for p in range(2)]
        s_dve = sem("f_dve")

        with nc.Block() as block:
            @block.sync
            def _(sp):
                sp.dma_start(w[:], io["slow_w"]).then_inc(s_w, 16)
                for p in range(2):
                    sp.sem_inc(s_out[p][0], 16)
                    sp.sem_inc(s_out[p][2], 16)

                def body(n, p):
                    for j in range(2):
                        sp.wait_ge(s_f16[j], n + 1)
                        sp.dma_start(io["feat"][j][n], f16[j][:, p, :]).then_inc(s_out[p][0], 16)
                    sp.wait_ge(s_val, n + 1)
                    sp.dma_start(io["val"][n], val[:, p, :]).then_inc(s_out[p][1], 16)
                    sp.wait_ge(s_dg, n + 1)
                    for y in range(2):
                        sp.dma_start(io["diag"][y][n], diag[:, p, y, :]).then_inc(s_out[p][2], 16)

                over_tiles(sp, body)
                for p in range(2):
                    sp.wait_ge(s_out[p][0], 32 * (NT // 2) + 16)
                    sp.wait_ge(s_out[p][1], 16 * (NT // 2))
                    sp.wait_ge(s_out[p][2], 32 * (NT // 2) + 16)

            def stored(eng, n, p, which, per=16):
                if isinstance(n, int):
                    if n < 2:
                        return
                    eng.wait_ge(s_out[p][which], per * (n // 2))
                else:
                    eng.wait_ge(s_out[p][which], (n - p) * (per // 2))

            def after(eng, sem_, v):
                if not isinstance(v, int) or v > 0:
                    eng.wait_ge(sem_, v)

            @block.gpsimd
            def _(pool):
                def body(n, p):
                    after(pool, s_proj, n - 1)
                    nc.gpsimd.tensor_copy(ot[:, p, :], oT[:, bass.ts(n, 128)]).then_inc(s_ot, 1)
                    pool.wait_ge(s_rs, n + 1)
                    after(pool, s_tr, 2 * n - 2)
                    f3 = feat[:].rearrange("p (g d) -> p g d", d=D)
                    nc.gpsimd.tensor_tensor(fn[:, p, :].rearrange("p (g d) -> p g d", d=D), f3,
                                            bc(rtot[:], 2, D), ALU.mult).then_inc(s_fn, 1)
                over_tiles(pool, body)
                pool.wait_ge(s_vall, 1)
                nc.gpsimd.partition_all_reduce(vmax[:, 1:2], vmax[:, 0:1], 128, RMAX).then_inc(s_vall, 1)

            @block.tensor
            def _(pe):
                def project(n, p):
                    pe.wait_ge(s_ot, n + 1)
                    after(pe, s_pqdve, n)
                    after(pe, s_pqact, n)
                    nc.tensor.matmul(pq[:, 0, :], ot[:, p, :], w[:, 0:512], start=True, stop=True)
                    nc.tensor.matmul(pq[:, 1, 0:HD + 2 * H], ot[:, p, :], w[:, 2 * HD:3 * HD + 2 * H], start=True,
                                     stop=True)
                    nc.tensor.matmul(pq[:, 2, :], ot[:, p, :], w[:, 3 * HD + 2 * H:NP], start=True,
                                     stop=True).then_inc(s_proj, 1)

                def grams(n, p):
                    pe.wait_ge(s_fn, n + 1)
                    after(pe, s_ft, 2 * n)
                    after(pe, s_dg, n)
                    for j in range(4):
                        last = nc.tensor.transpose(pt[:, j * 128:(j + 1) * 128],
                                                   fn[:, p, j * 128:(j + 1) * 128], ident[:])
                    last.then_inc(s_tr, 1)
                    for j in range(2):
                        last = nc.tensor.transpose(pg[:, j, 256:384], fn[:, p, (4 + j) * 128:(5 + j) * 128], ident[:])
                    last.then_inc(s_tr, 1)
                    pe.wait_ge(s_ft, 2 * n + 2)
                    nc.tensor.sem_inc(s_alone, 1)
                    for y in range(2):
                        for g in range(HQ):
                            c = (2 + 2 * y + g) * 128
                            for tb in range(4):
                                for h4 in range(4):
                                    q = slice(32 * h4, 32 * h4 + 32)
                                    cc = c + 32 * tb
                                    o = (y * HQ + g) * 32
                                    last = nc.tensor.matmul(pg[32 * tb:32 * tb + 32, h4, o:o + 32],
                                                            ft[q, p, cc:cc + 32], ft[q, p, cc:cc + 32],
                                                            start=True, stop=True)
                    last.then_inc(s_gr, 1)

                pe.wait_ge(s_w, 16)
                project(0, 0)

                def body(n, p):
                    if isinstance(n, int) and n == NT - 1:
                        grams(n, p)
                        return
                    project(n + 1, 1 - p)
                    grams(n, p)
                over_tiles(pe, body)

            def copy_rk(eng, copy, n, p, j):
                for g in range(HQ):
                    src = f16[j][:, p, (4 + g) * 128:(5 + g) * 128].rearrange("p (b a s) -> p a b s", b=2, a=2)
                    dst = rk16[j][:, g].rearrange("p a (b s) -> p a b s", s=S // 2)[:, :, bass.ts(n, 2), :]
                    copy(dst, src).then_inc(s_rkc, 1)

            @block.scalar
            def _(act):
                def body(n, p):
                    act.wait_ge(s_proj, n + 1)
                    stored(act, n, p, 1)
                    after(act, s_vm, n - 1)
                    nc.scalar.copy(val[:, p, 0:2 * HD], pq[:, 2, :]).then_inc(s_pqact, 1)
                    act.wait_ge(s_low, n + 1)
                    nc.scalar.activation(low[:], low[:], ACT.Exp).then_inc(s_exp, 1)
                    act.wait_ge(s_gate, n + 1)
                    nc.scalar.activation(gate[:], gate[:], ACT.Exp, scale=-1.0).then_inc(s_gexp, 1)
                    act.wait_ge(s_rk0, n + 1)
                    nc.scalar.activation(feat[:, 2 * HD:3 * HD], feat[:, 2 * HD:3 * HD], ACT.Exp).then_inc(s_rk1, 1)
                    act.wait_ge(s_tr, 2 * n + 1)
                    after(act, s_f16[1], n - 1)
                    nc.scalar.copy(ft[:, p, 0:512], pt[:]).then_inc(s_ft, 1)
                    act.wait_ge(s_tr, 2 * n + 2)
                    nc.scalar.copy(ft[:, p, 512:768].rearrange("p (a b) -> p a b", a=2),
                                   pg[:, 0:2, 256:384]).then_inc(s_ft, 1)
                    act.wait_ge(s_ft, 2 * n + 2)
                    if not isinstance(n, int):
                        act.wait_ge(s_out[p][0], (n - p) * 16 + 16)
                    elif n >= 2:
                        act.wait_ge(s_out[p][0], 32 * (n // 2) + 16)
                    nc.scalar.mul(f16[0][:, p, :], ft[:, p, :], UNIT).then_inc(s_f16[0], 1)
                    act.wait_ge(s_f16[0], n + 1)
                    copy_rk(act, nc.scalar.copy, n, p, 0)
                over_tiles(act, body)

            @block.vector
            def _(dve):
                def stored_late(n, p, which):
                    if not isinstance(n, int):
                        dve.wait_ge(s_out[p][which], (n - p) * 16 + 16)
                    elif n >= 2:
                        dve.wait_ge(s_out[p][which], 32 * (n // 2) + 16)

                def scale_diag(n, p):
                    dve.wait_ge(s_gr, n + 1)
                    stored_late(n, p, 2)
                    for y in range(2):
                        for g in range(HQ):
                            o = (y * HQ + g) * 32
                            b4 = val[:, p, 2 * HD + y * H + 4 * g:2 * HD + y * H + 4 * g + 4]
                            last = nc.vector.tensor_tensor(
                                diag[:, p, y, g * 128:(g + 1) * 128].rearrange("p (h s) -> p h s", s=32),
                                pg[:, :, o:o + 32], bc(b4, 2, 32), ALU.mult)
                    last.then_inc(s_dg, 1)
                    dve.wait_ge(s_f16[0], n + 1)
                    stored_late(n, p, 0)
                    nc.vector.scalar_tensor_tensor(out=f16[1][:, p, :], in0=ft[:, p, :], scalar=UNIT,
                                                   in1=f16[0][:, p, :], op0=ALU.mult,
                                                   op1=ALU.subtract).then_inc(s_f16[1], 1)
                    nc.vector.tensor_reduce(vtile[:, bass.ts(n, 1)], val[:, p, 0:2 * HD], AX.X, ALU.max,
                                            apply_absolute_value=True).then_inc(s_vm, 1)
                    dve.wait_ge(s_f16[1], n + 1)
                    copy_rk(dve, nc.vector.tensor_copy, n, p, 1)

                def body(n, p):
                    f3 = feat[:].rearrange("p (g d) -> p g d", d=D)
                    dve.wait_ge(s_proj, n + 1)
                    after(dve, s_exp, n)
                    nc.vector.tensor_scalar(low[:], pq[:, 0, :], 0.0, None, ALU.min).then_inc(s_low, 1)
                    r3 = pq[:, 1, 0:HD].rearrange("p (g d) -> p g d", d=D)
                    nc.vector.tensor_reduce(top[:], r3, AX.X, ALU.max).then_inc(s_dve, 1)
                    nc.vector.tensor_copy(gate[:], pq[:, 1, HD:HD + 2 * H]).then_inc(s_gate, 1)
                    after(dve, s_fn, n)
                    dve.wait_ge(s_dve, OWN * n + 1)
                    nc.vector.tensor_tensor(f3[:, 2 * H:3 * H, :], r3, bc(top[:], 2, D),
                                            ALU.subtract).then_inc(s_rk0, 1)
                    dve.wait_ge(s_exp, n + 1)
                    nc.vector.scalar_tensor_tensor(out=feat[:, 0:2 * HD], in0=pq[:, 0, :], scalar=0.0, in1=low[:],
                                                   op0=ALU.max, op1=ALU.add).then_inc(s_pqdve, 1)
                    dve.wait_ge(s_gexp, n + 1)
                    nc.vector.tensor_scalar(gate[:], gate[:], 1.0, None, ALU.add).then_inc(s_dve, 1)
                    dve.wait_ge(s_rk1, n + 1)
                    dve.wait_ge(s_pqdve, n + 1)
                    nc.vector.tensor_reduce(tot[:], f3, AX.X, ALU.add).then_inc(s_dve, 1)
                    dve.wait_ge(s_dve, OWN * n + 2)
                    dve.wait_ge(s_pqact, n + 1)
                    stored(dve, n, p, 1)
                    nc.vector.reciprocal(val[:, p, 2 * HD:2 * HD + 2 * H], gate[:]).then_inc(s_val, 1)
                    dve.wait_ge(s_dve, OWN * n + 3)
                    nc.vector.reciprocal(rtot[:], tot[:]).then_inc(s_rs, 1)
                    if not (isinstance(n, int) and n == 0):
                        scale_diag(n - 1, 1 - p)
                over_tiles(dve, body)
                scale_diag(NT - 1, (NT - 1) % 2)
                dve.wait_ge(s_vm, NT)
                nc.vector.tensor_reduce(vmax[:, 0:1], vtile[:], AX.X, ALU.max).then_inc(s_vall, 1)
                dve.wait_ge(s_vall, 2)
                nc.vector.tensor_scalar(vmax[:, 1:2], vmax[:, 1:2], 1e-30, 1.0 / VTOP, ALU.max,
                                        ALU.mult).then_inc(s_vall, 1)
                dve.wait_ge(s_vall, 3)
                nc.vector.tensor_scalar(vmax[:, 2:3], vmax[:, 1:2], 1.0 / UNIT, None, ALU.mult).then_inc(s_vall, 1)
                dve.wait_ge(s_vall, 4)
                nc.vector.reciprocal(vmax[:, 1:2], vmax[:, 1:2]).then_inc(s_vall, 1)


def inverses(nc, io):
    with ExitStack() as ctx:
        def tile(name, shape):
            return ctx.enter_context(nc.sbuf_tensor(name, shape, F32))

        def sem(name):
            return ctx.enter_context(nc.semaphore(name))

        HS = S // 2
        a = tile("a_half", [B, 2, HS, HD])
        tt = tile("t_transposed", [B, 2, S, H * BLK])
        prod = tile("products", [B, 2, H * (BLK - 1) * (BLK - 1)])
        s_in = [sem(f"i_in{j}") for j in range(2)]
        s_init = sem("i_init")
        s_done = sem("i_done")
        s_out = sem("i_out")
        s_dve = sem("i_dve")
        parts = [(y, half) for y in range(2) for half in range(2)]

        with nc.Block() as block:
            @block.sync
            def _(sp):
                for k, (y, half) in enumerate(parts):
                    if k >= 2:
                        sp.wait_ge(s_done, k - 1)
                    src = io["diag"][y][:].rearrange("n (b t) c -> (n b) t c", b=2)
                    sp.dma_start(a[:, k % 2], src[:, half * HS:(half + 1) * HS, :]).then_inc(s_in[k % 2], 16)
                    if k >= 1:
                        yy, hh = parts[k - 1]
                        sp.wait_ge(s_done, k)
                        dst = io["tinv"][yy][:].rearrange("n (b t) c -> (n b) t c", b=2)
                        sp.dma_start(dst[:, hh * HS:(hh + 1) * HS, :],
                                     tt[:, yy, hh * HS:(hh + 1) * HS, :]).then_inc(s_out, 16)
                yy, hh = parts[-1]
                sp.wait_ge(s_done, len(parts))
                dst = io["tinv"][yy][:].rearrange("n (b t) c -> (n b) t c", b=2)
                sp.dma_start(dst[:, hh * HS:(hh + 1) * HS, :],
                             tt[:, yy, hh * HS:(hh + 1) * HS, :]).then_inc(s_out, 16)
                sp.wait_ge(s_out, 16 * len(parts))

            @block.gpsimd
            def _(pool):
                nc.gpsimd.memset(tt[:], 0.0).then_inc(s_init, 1)
                pool.wait_ge(s_init, 1)
                for x in range(BLK):
                    diag = tt[:].rearrange("p y (k x) (h t) -> p (y k) x h t", x=BLK, t=BLK)[:, :, x, :, x]
                    last = nc.gpsimd.memset(diag, 1.0)
                last.then_inc(s_init, 1)

            @block.vector
            def _(dve):
                own = Chain(s_dve)
                dve.wait_ge(s_init, 2)
                for k, (y, half) in enumerate(parts):
                    dve.wait_ge(s_in[k % 2], 16 * (k // 2 + 1))
                    for t in range(1, BLK):
                        n = H * t * t
                        for blk in range(2):
                            rows_ = a[:, k % 2, blk * BLK + t, :].rearrange("p (h s) -> p h s", s=2 * BLK)
                            arow = bc(rows_[:, :, blk * BLK:blk * BLK + t], 2, t)
                            x0 = (half * 2 + blk) * BLK
                            tprev = tt[:, y, x0:x0 + t, :].rearrange("p x (h t) -> p h x t", t=BLK)[:, :, :, 0:t]
                            dve.wait_ge(s_dve, own.n)
                            pr = prod[:, blk, 0:n].rearrange("p (h x s) -> p h x s", x=t, s=t)
                            own.note(nc.vector.tensor_tensor(pr, arow, tprev, ALU.mult))
                        for blk in range(2):
                            x0 = (half * 2 + blk) * BLK
                            pr = prod[:, blk, 0:n].rearrange("p (h x s) -> p h x s", x=t, s=t)
                            dst = tt[:, y, x0:x0 + t, :].rearrange("p x (h t) -> p h x t", t=BLK)[:, :, :, t]
                            dve.wait_ge(s_dve, own.n - (1 if blk == 0 else 1))
                            last = own.note(nc.vector.tensor_reduce(dst, pr, AX.X, ALU.add, negate=True))
                    dve.wait_ge(s_dve, own.n)
                    nc.vector.sem_inc(s_done, 1)


def solve(nc, io, vscale):
    with ExitStack() as ctx:
        def tile(name, shape, dt=F32):
            return ctx.enter_context(nc.sbuf_tensor(name, shape, dt))

        def sem(name):
            return ctx.enter_context(nc.semaphore(name))

        ROUNDS = NB - 1
        R1 = ROUNDS + 1
        ft = tile("s_ft", [128, 2, 2, 3 * HD], F16)
        val = tile("s_val", [128, 2, 2 * HD + 2 * H])
        vs = tile("s_vs", [128, 2, 2 * HD])
        v16 = tile("s_v16", [128, 2, 2, 2 * HD], F16)
        tc = tile("s_tc", [128, 2, 2, H * BLK])
        tb = tile("s_tb", [128, 2, H * BLK])
        t16 = tile("s_t16", [128, 2, 2, H * BLK], F16)
        masks = tile("s_masks", [128, 2, 128])
        own32 = tile("s_own32", [128, 128])
        own16 = tile("s_own16", [128, 128], F16)
        tx = [tile(f"s_tx{p}", [128, 2, 2, H, 128], F16) for p in range(2)]
        g32 = tile("s_g32", [128, 2, 4 * HQ * 128])
        gm = [tile(f"s_gm{p}", [128, 3, 2, 4, HQ, 128], F16) for p in range(2)]
        u16 = tile("s_u16", [128, 2, 2, 2, HD], F16)
        r32 = tile("s_r32", [128, 2, HD])
        r16 = tile("s_r16", [128, 2, 2, HD], F16)
        zo = tile("s_z", [128, 2, HQ * 128])
        pg = ctx.enter_context(nc.psum_tensor("s_gram", [128, 4, 512], F32))
        pu = ctx.enter_context(nc.psum_tensor("s_pu", [128, 2, 512], F32))
        pr = ctx.enter_context(nc.psum_tensor("s_pr", [128, 2, 512], F32))

        s_c = sem("s_const")
        s_own = sem("s_own")
        s_in = [sem(f"s_in{p}") for p in range(2)]
        s_vs = sem("s_vsr")
        s_v1 = sem("s_v1")
        s_v2 = sem("s_v2")
        s_tb = sem("s_tbr")
        s_t1 = sem("s_t1")
        s_t2 = sem("s_t2")
        s_tx = sem("s_txr")
        s_pg = sem("s_pg")
        s_g32 = sem("s_g32r")
        s_g1 = sem("s_g1")
        s_g2 = sem("s_g2")
        s_pu = [sem(f"s_pu{y}") for y in range(2)]
        s_u1 = [sem(f"s_u1_{y}") for y in range(2)]
        s_u2 = [sem(f"s_u2_{y}") for y in range(2)]
        s_pr = [sem(f"s_pr{y}") for y in range(2)]
        s_r = [sem(f"s_r{y}") for y in range(2)]
        s_r1 = [sem(f"s_r1_{y}") for y in range(2)]
        s_r2 = [sem(f"s_r2_{y}") for y in range(2)]
        s_pz = sem("s_pz")
        s_z = sem("s_zr")
        s_zout = [sem(f"s_zout{p}") for p in range(2)]
        s_uout = [sem(f"s_uout{p}") for p in range(2)]

        def after(eng, sem_, v):
            if not isinstance(v, int) or v > 0:
                eng.wait_ge(sem_, v)

        def loaded(eng, n, p):
            if isinstance(n, int):
                eng.wait_ge(s_in[p], 80 * (n // 2 + 1))
            else:
                eng.wait_ge(s_in[p], (n - p) * 40 + 80)

        def stored(eng, sems, n, p, per):
            if isinstance(n, int):
                if n >= 2:
                    eng.wait_ge(sems[p], per * (n // 2))
            else:
                eng.wait_ge(sems[p], (n - p) * (per // 2))

        with nc.Block() as block:
            @block.sync
            def _(sp):
                sp.dma_start(masks[:], io["masks"]).then_inc(s_c, 16)
                sp.dma_start(own32[:], io["own_blk"]).then_inc(s_c, 16)

                def load(n, p):
                    after(sp, s_r[0], ROUNDS * (n - 1))
                    after(sp, s_r[1], ROUNDS * (n - 1))
                    after(sp, s_pg, 3 * (n - 1))
                    for j in range(2):
                        sp.dma_start(ft[:, p, j, :], io["feat"][j][n]).then_inc(s_in[p], 16)
                    sp.dma_start(val[:, p, :], io["val"][n]).then_inc(s_in[p], 16)
                    for y in range(2):
                        sp.dma_start(tc[:, p, y, :], io["tinv"][y][n]).then_inc(s_in[p], 16)

                def store(n, p):
                    sp.wait_ge(s_u2[1], R1 * (n + 1))
                    for j in range(2):
                        sp.dma_start(io["u2"][j][n], u16[:, p, 1, j, :]).then_inc(s_uout[p], 16)
                    sp.wait_ge(s_z, n + 1)
                    sp.dma_start(io["z"][:, :, n, :], zo[:, p, :].rearrange("p (a b) -> p a b", a=HQ)).then_inc(
                        s_zout[p], 16)

                load(0, 0)
                load(1, 1)

                def body(n, p):
                    if not (isinstance(n, int) and n < 2):
                        load(n, p)
                        store(n - 2, p)
                over_tiles(sp, body)
                store(NT - 2, 0)
                store(NT - 1, 1)
                for p in range(2):
                    sp.wait_ge(s_uout[p], 32 * (NT // 2))
                    sp.wait_ge(s_zout[p], 16 * (NT // 2))

            @block.gpsimd
            def _(pool):
                pool.wait_ge(s_c, 32)
                nc.gpsimd.tensor_copy(own16[:], own32[:]).then_inc(s_own, 1)
                pool.wait_ge(s_own, 1)

                def body(n, p):
                    loaded(pool, n, p)
                    nc.gpsimd.tensor_tensor(vs[:, p, :], val[:, p, 0:2 * HD],
                                            vscale[:, 1:2].broadcast_to([128, 2 * HD]), ALU.mult).then_inc(s_vs, 1)
                    after(pool, s_t2, n)
                    for y in range(2):
                        c3 = tc[:, p, y, :].rearrange("p (h t) -> p h t", t=BLK)
                        gates = val[:, p, 2 * HD + y * H:2 * HD + (y + 1) * H]
                        nc.gpsimd.tensor_tensor(tb[:, y, :].rearrange("p (h t) -> p h t", t=BLK), c3,
                                                bc(gates, 2, BLK), ALU.mult).then_inc(s_tb, 1)
                    pool.wait_ge(s_v1, n + 1)
                    nc.gpsimd.tensor_tensor(v16[:, p, 1, :], vs[:, p, :], v16[:, p, 0, :],
                                            ALU.subtract).then_inc(s_v2, 1)
                    pool.wait_ge(s_t2, n + 1)
                    for j in range(2):
                        for y in range(2):
                            after(pool, s_pu[y], R1 * (n - 1))
                            c3 = t16[:, j, y, :].rearrange("p (h t) -> p h t", t=BLK)
                            o3 = own16[:].rearrange("p (k t) -> p k t", t=BLK)
                            nc.gpsimd.tensor_tensor(tx[p][:, y, j].rearrange("p h (k t) -> p h k t", t=BLK),
                                                    bc(c3, 2, 8), bc(o3, 1, H), ALU.mult).then_inc(s_tx, 1)
                over_tiles(pool, body)

            @block.tensor
            def _(pe):
                PRODUCTS = ((0, 0), (0, 1), (1, 0))

                def gram(n, p, j):
                    lo, ro = [(2, 2), (4, 4), (2, 0)][j]
                    after(pe, s_g32, 3 * n + j)
                    for g in range(HQ):
                        for m, (a, b) in enumerate(PRODUCTS):
                            for h4 in range(4):
                                q = slice(32 * h4, 32 * h4 + 32)
                                last = nc.tensor.matmul(pg[:, h4, g * 128:(g + 1) * 128],
                                                        ft[q, p, a, (lo + g) * 128:(lo + g + 1) * 128],
                                                        ft[q, p, b, (ro + g) * 128:(ro + g + 1) * 128],
                                                        start=(m == 0), stop=(m == 2))
                    last.then_inc(s_pg, 1)

                def apply_t(n, p, y, k):
                    if k == 0:
                        pe.wait_ge(s_tx, 4 * n + 4)
                        pe.wait_ge(s_v2, n + 1)
                        after(pe, s_u2[y], R1 * n)
                    else:
                        pe.wait_ge(s_r2[y], ROUNDS * n + k)
                    for h in range(H):
                        hs = slice(h * D, (h + 1) * D)
                        for m, (a, b) in enumerate(PRODUCTS):
                            rhs = v16[:, p, b, y * HD + h * D:y * HD + (h + 1) * D] if k == 0 else r16[:, y, b, hs]
                            last = nc.tensor.matmul(pu[:, y, hs], tx[p][:, y, a, h, :], rhs, start=(m == 0),
                                                    stop=(m == 2))
                    last.then_inc(s_pu[y], 1)

                def apply_g(n, p, y, k):
                    if k == 0:
                        pe.wait_ge(s_g2, 3 * n + y + 1)
                        if y == 0:
                            after(pe, s_z, n)
                    pe.wait_ge(s_u2[y], R1 * n + k + 1)
                    for h in range(H):
                        hs = slice(h * D, (h + 1) * D)
                        for m, (a, b) in enumerate(PRODUCTS):
                            last = nc.tensor.matmul(pr[:, y, hs], gm[p][:, y, a, h % 4, h // 4, :],
                                                    u16[:, p, y, b, hs], start=(m == 0), stop=(m == 2))
                    last.then_inc(s_pr[y], 1)

                def z_of(n, p):
                    pe.wait_ge(s_g2, 3 * n + 3)
                    pe.wait_ge(s_u2[0], R1 * (n + 1))
                    for h in range(H):
                        q = 32 * (h % 4)
                        c = (h // 4) * 128
                        for m, (a, b) in enumerate(PRODUCTS):
                            last = nc.tensor.matmul(pr[q:q + 32, 0, c:c + 128], u16[:, p, 0, a, h * D:(h + 1) * D],
                                                    gm[p][:, 2, b, h % 4, h // 4, :], start=(m == 0), stop=(m == 2))
                    last.then_inc(s_pz, 1)

                loaded(pe, 0, 0)
                for j in range(3):
                    gram(0, 0, j)

                def body(n, p):
                    ends = isinstance(n, int) and n == NT - 1
                    if not ends:
                        loaded(pe, n + 1, 1 - p)
                    for y in range(2):
                        apply_t(n, p, y, 0)
                    for k in range(ROUNDS):
                        for y in range(2):
                            apply_g(n, p, y, k)
                        if not ends:
                            gram(n + 1, 1 - p, k)
                        for y in range(2):
                            apply_t(n, p, y, k + 1)
                    z_of(n, p)

                over_tiles(pe, body)

            @block.scalar
            def _(act):
                def gram_high(n, p, j):
                    act.wait_ge(s_g32, 3 * n + j + 1)
                    nc.scalar.copy(gm[p][:, j, 0].rearrange("p a g t -> p (a g t)"),
                                   g32[:, (j + p) % 2, :]).then_inc(s_g1, 1)

                def splits(n, p):
                    act.wait_ge(s_vs, n + 1)
                    nc.scalar.copy(v16[:, p, 0, :], vs[:, p, :]).then_inc(s_v1, 1)
                    act.wait_ge(s_tb, 2 * n + 2)
                    after(act, s_tx, 4 * n)
                    nc.scalar.mul(t16[:, 0], tb[:], UNIT).then_inc(s_t1, 1)

                splits(0, 0)
                for j in range(3):
                    gram_high(0, 0, j)

                def body(n, p):
                    ends = isinstance(n, int) and n == NT - 1
                    for k in range(R1):
                        for y in range(2):
                            act.wait_ge(s_pu[y], R1 * n + k + 1)
                            if k == 0 and y == 0:
                                stored(act, s_uout, n, p, 32)
                            nc.scalar.mul(u16[:, p, y, 0, :], pu[:, y, 0:HD], 1.0 / UNIT).then_inc(s_u1[y], 1)
                        if k < ROUNDS:
                            for y in range(2):
                                act.wait_ge(s_r[y], ROUNDS * n + k + 1)
                                nc.scalar.copy(r16[:, y, 0, :], r32[:, y, :]).then_inc(s_r1[y], 1)
                            if not ends:
                                if k == 0:
                                    splits(n + 1, 1 - p)
                                gram_high(n + 1, 1 - p, k)
                    act.wait_ge(s_pz, n + 1)
                    stored(act, s_zout, n, p, 16)
                    nc.scalar.mul(zo[:, p, :], pr[:, 0, 0:HQ * 128], vscale[:, 2:3]).then_inc(s_z, 1)
                over_tiles(act, body)

            @block.vector
            def _(dve):
                dve.wait_ge(s_c, 32)

                def mask(n, p, j):
                    dve.wait_ge(s_pg, 3 * n + j + 1)
                    after(dve, s_g1, 3 * n + j - 1)
                    m = masks[:, 1 if j == 2 else 0, :]
                    nc.vector.tensor_tensor(g32[:, (j + p) % 2, :].rearrange("p (a g t) -> p a g t", a=4, g=HQ),
                                            pg[:, :, 0:HQ * 128].rearrange("p a (g t) -> p a g t", g=HQ),
                                            bc(bc(m, 1, HQ), 1, 4), ALU.mult).then_inc(s_g32, 1)

                def gram_low(n, p, j):
                    dve.wait_ge(s_g1, 3 * n + j + 1)
                    nc.vector.tensor_tensor(gm[p][:, j, 1].rearrange("p a g t -> p (a g t)"), g32[:, (j + p) % 2, :],
                                            gm[p][:, j, 0].rearrange("p a g t -> p (a g t)"),
                                            ALU.subtract).then_inc(s_g2, 1)

                def u_low(n, p, y, k):
                    dve.wait_ge(s_u1[y], R1 * n + k + 1)
                    nc.vector.scalar_tensor_tensor(out=u16[:, p, y, 1, :], in0=pu[:, y, 0:HD], scalar=1.0 / UNIT,
                                                   in1=u16[:, p, y, 0, :], op0=ALU.mult,
                                                   op1=ALU.subtract).then_inc(s_u2[y], 1)

                def residual(n, p, y, k):
                    dve.wait_ge(s_pr[y], ROUNDS * n + k + 1)
                    nc.vector.scalar_tensor_tensor(out=r32[:, y, :], in0=pr[:, y, 0:HD], scalar=-1.0 / UNIT,
                                                   in1=vs[:, p, y * HD:(y + 1) * HD], op0=ALU.mult,
                                                   op1=ALU.add).then_inc(s_r[y], 1)

                def r_low(n, p, y, k):
                    dve.wait_ge(s_r1[y], ROUNDS * n + k + 1)
                    nc.vector.tensor_tensor(r16[:, y, 1, :], r32[:, y, :], r16[:, y, 0, :],
                                            ALU.subtract).then_inc(s_r2[y], 1)

                def t_low(n, p):
                    dve.wait_ge(s_t1, n + 1)
                    nc.vector.scalar_tensor_tensor(out=t16[:, 1].rearrange("p y c -> p (y c)"),
                                                   in0=tb[:].rearrange("p y c -> p (y c)"), scalar=UNIT,
                                                   in1=t16[:, 0].rearrange("p y c -> p (y c)"), op0=ALU.mult,
                                                   op1=ALU.subtract).then_inc(s_t2, 1)

                t_low(0, 0)
                for j in range(3):
                    mask(0, 0, j)
                    gram_low(0, 0, j)

                def body(n, p):
                    ends = isinstance(n, int) and n == NT - 1
                    for y in range(2):
                        u_low(n, p, y, 0)
                    for k in range(ROUNDS):
                        for y in range(2):
                            residual(n, p, y, k)
                        for y in range(2):
                            r_low(n, p, y, k)
                        if not ends:
                            if k == 0:
                                t_low(n + 1, 1 - p)
                            mask(n + 1, 1 - p, k)
                        for y in range(2):
                            u_low(n, p, y, k + 1)
                        if not ends:
                            gram_low(n + 1, 1 - p, k)
                over_tiles(dve, body)


def recur(nc, io, hs, rk16, vscale):
    STREAMS = [(0, 48), (48, B - 48)]
    W = 96
    HALF = S // 2
    with ExitStack() as ctx:
        def tile(name, shape, dt=F32):
            return ctx.enter_context(nc.sbuf_tensor(name, shape, dt))

        def sem(name):
            return ctx.enter_context(nc.semaphore(name))

        def sems(name):
            return [sem(f"r_{name}{i}") for i in range(2)]

        u16 = [tile(f"r_u{j}", [128, 2, B // 4, HD], F16) for j in range(2)]
        see = tile("r_see", [128, HALF, 16])
        q = [[tile(f"r_q{i}{j}", [128, W, 4], F16) for j in range(2)] for i in range(2)]
        a32 = [tile(f"r_a32{i}", [128, 2, W * 4]) for i in range(2)]
        am = [[tile(f"r_am{i}{j}", [128, 2, W * 4], F16) for j in range(2)] for i in range(2)]
        hc = [tile(f"r_h{i}", [128, W]) for i in range(2)]
        ht = [tile(f"r_ht{i}", [128, 3, D]) for i in range(2)]
        et = [tile(f"r_et{i}", [128, 3, D]) for i in range(2)]
        e16 = [[tile(f"r_e{i}{j}", [128, 3 * D], F16) for j in range(2)] for i in range(2)]
        st = [tile(f"r_st{i}", [128, 3, 4]) for i in range(2)]
        pa = [ctx.enter_context(nc.psum_tensor(f"r_pa{i}", [128, 2, 512], F32)) for i in range(2)]
        ph = [ctx.enter_context(nc.psum_tensor(f"r_ph{i}", [128, 512], F32)) for i in range(2)]

        s_z, s_see, s_q0 = (sem(f"r_in_{k}") for k in ("z", "see", "q0"))
        s_u = [sem(f"r_in_u{half}") for half in range(2)]
        s_q = sems("q")
        s_a = sems("a")
        s_a32 = sems("a32")
        s_am1 = sems("am1")
        s_am = sems("am")
        s_rq = sems("rq")
        s_h = sems("h")
        s_hs = sems("hs")
        s_ht = sems("ht")
        s_mx = sems("mx")
        s_sub = sems("sub")
        s_exp = sems("exp")
        s_sum = sems("sum")
        s_rec = sems("rec")
        s_nrm = sems("nrm")
        s_n1 = sems("n1")
        s_n2 = sems("n2")

        with nc.Block() as block:
            @block.sync
            def _(sp):
                sp.dma_start(see[:], io["see4"]).then_inc(s_see, 16)
                for half in range(2):
                    for j in range(2):
                        for b in range(4):
                            n0, r0 = b // 2, (b % 2) * S + half * HALF
                            src = io["u2"][j][n0:NT:2, r0:r0 + HALF, :].rearrange("n s c -> s n c")
                            sp.dma_start(u16[j][32 * b:32 * b + 32, half], src).then_inc(s_u[half], 16)
                    if half == 0:
                        sp.dma_start(hs[:].rearrange("p g b s -> p (g b s)"),
                                     io["z"][:].rearrange("p g n c -> p (g n c)")).then_inc(s_z, 16)
                sp.wait_ge(s_u[1], 128)

            @block.tensor
            def _(pe):
                PRODUCTS = ((0, 0), (0, 1), (1, 0))

                def step(t, halves):
                    for i, (b0, nb) in enumerate(STREAMS):
                        pe.wait_ge(s_q[i], t + 1)
                        for half in range(halves):
                            for g in range(HQ):
                                for b in range(0, nb, 4):
                                    c = g * nb + b
                                    rows_ = slice((b0 + b) * HALF, (b0 + b + 4) * HALF)
                                    for m, (x, y) in enumerate(PRODUCTS):
                                        last = nc.tensor.matmul(pa[i][:, half, 4 * c:4 * c + 16],
                                                                rk16[x][:, g, half, rows_], q[i][y][:, c:c + 4, :],
                                                                start=(m == 0), stop=(m == 2))
                            last.then_inc(s_a[i], 1)
                    for i, (b0, nb) in enumerate(STREAMS):
                        pe.wait_ge(s_am[i], t + 1 if halves == 1 else 2 * t + 2 - HALF)
                        for g in range(HQ):
                            for b in range(0, nb, 4):
                                c = g * nb + b
                                for half in range(halves):
                                    for m, (x, y) in enumerate(PRODUCTS):
                                        last = nc.tensor.matmul(ph[i][:, 4 * c:4 * c + 16],
                                                                u16[x][:, half, (b0 + b) // 4, g * 128:(g + 1) * 128],
                                                                am[i][y][:, half, 4 * c:4 * c + 16],
                                                                start=(half == 0 and m == 0),
                                                                stop=(half == halves - 1 and m == 2))
                        last.then_inc(s_rq[i], 1)

                pe.wait_ge(s_u[0], 128)
                with pe.Fori(0, HALF) as t:
                    step(t, 1)
                pe.wait_ge(s_u[1], 128)
                with pe.Fori(HALF, S) as t:
                    step(t, 2)

            @block.scalar
            def _(act):
                def step(t, halves):
                    for i, (b0, nb) in enumerate(STREAMS):
                        cols = slice(0, 4 * HQ * nb)
                        for half in range(halves):
                            act.wait_ge(s_a32[i], t + 1 if halves == 1 else 2 * t + 1 + half - HALF)
                            nc.scalar.copy(am[i][0][:, half, cols], a32[i][:, half, cols]).then_inc(s_am1[i], 1)
                    for i in range(2):
                        act.wait_ge(s_sub[i], t + 1)
                        nc.scalar.activation(et[i][:], et[i][:], ACT.Exp).then_inc(s_exp[i], 1)

                with act.Fori(0, HALF) as t:
                    step(t, 1)
                with act.Fori(HALF, S) as t:
                    step(t, 2)

            @block.gpsimd
            def _(pool):
                for i, (b0, nb) in enumerate(STREAMS):
                    nc.gpsimd.memset(hc[i][:], 0.0).then_inc(s_hs[i], 1)
                    for j in range(2):
                        nc.gpsimd.memset(q[i][j][:], 0.0).then_inc(s_q0, 1)
                pool.wait_ge(s_q0, 4)
                for i in range(2):
                    for h4 in range(4):
                        last = nc.gpsimd.memset(q[i][0][32 * h4:32 * h4 + 32, :, h4], UNIT / D)
                    last.then_inc(s_q[i], 1)
                with pool.Fori(0, S) as t:
                    for i, (b0, nb) in enumerate(STREAMS):
                        pool.wait_ge(s_h[i], t + 1)
                        nc.gpsimd.tensor_copy(hs[:, :, b0:b0 + nb, t],
                                              hc[i][:, 0:HQ * nb].rearrange("p (g b) -> p g b", g=HQ)).then_inc(
                                                  s_hs[i], 1)

            @block.vector
            def _(dve):
                def mask(t, i, half, halves):
                    b0, nb = STREAMS[i]
                    dve.wait_ge(s_a[i], t + 1 if halves == 1 else 2 * t + 1 + half - HALF)
                    k = HQ * nb // 4
                    now = see[:, t, :] if halves == 1 else see[:, t - HALF, :] if half else see[:, HALF - 1, :]
                    nc.vector.tensor_tensor(
                        a32[i][:, half, 0:4 * HQ * nb].rearrange("p (k w) -> p k w", k=k),
                        pa[i][:, half, 0:4 * HQ * nb].rearrange("p (k w) -> p k w", k=k),
                        bc(now, 1, k), ALU.mult).then_inc(s_a32[i], 1)

                def mask_low(t, i, half, halves):
                    cols = slice(0, 4 * HQ * STREAMS[i][1])
                    dve.wait_ge(s_am1[i], t + 1 if halves == 1 else 2 * t + 1 + half - HALF)
                    nc.vector.tensor_tensor(am[i][1][:, half, cols], a32[i][:, half, cols], am[i][0][:, half, cols],
                                            ALU.subtract).then_inc(s_am[i], 1)

                def softmax(t, i):
                    b0, nb = STREAMS[i]
                    dve.wait_ge(s_rq[i], t + 1)
                    dve.wait_ge(s_hs[i], t + 1)
                    for h4 in range(4):
                        r = slice(32 * h4, 32 * h4 + 32)
                        last = nc.vector.scalar_tensor_tensor(
                            out=hc[i][r, 0:HQ * nb].rearrange("p (g b) -> p g b", g=HQ),
                            in0=ph[i][r, 0:4 * HQ * nb].rearrange("p (g b h) -> p g b h", g=HQ, h=4)[:, :, :, h4],
                            scalar=vscale[r, 2:3], in1=hs[r, :, b0:b0 + nb, t], op0=ALU.mult, op1=ALU.add)
                    last.then_inc(s_h[i], 1)
                    dve.wait_ge(s_h[i], t + 1)
                    nc.vector.transpose(ht[i][:].rearrange("p k d -> p (k d)"), hc[i][:]).then_inc(s_ht[i], 1)
                    dve.wait_ge(s_ht[i], t + 1)
                    nc.vector.tensor_reduce(st[i][:, :, 0], ht[i][:], AX.X, ALU.max).then_inc(s_mx[i], 1)
                    dve.wait_ge(s_mx[i], t + 1)
                    nc.vector.tensor_tensor(et[i][:], ht[i][:], bc(st[i][:, :, 0], 2, D),
                                            ALU.subtract).then_inc(s_sub[i], 1)

                def spread(t, i):
                    dve.wait_ge(s_exp[i], t + 1)
                    nc.vector.tensor_reduce(st[i][:, :, 1], et[i][:], AX.X, ALU.add).then_inc(s_sum[i], 1)
                    dve.wait_ge(s_sum[i], t + 1)
                    nc.vector.reciprocal(st[i][:, :, 2], st[i][:, :, 1]).then_inc(s_rec[i], 1)
                    dve.wait_ge(s_rec[i], t + 1)
                    nc.vector.scalar_tensor_tensor(out=et[i][:], in0=et[i][:], scalar=UNIT,
                                                   in1=bc(st[i][:, :, 2], 2, D), op0=ALU.mult,
                                                   op1=ALU.mult).then_inc(s_nrm[i], 1)
                    ef = et[i][:].rearrange("p k d -> p (k d)")
                    dve.wait_ge(s_nrm[i], t + 1)
                    nc.vector.tensor_copy(e16[i][0][:], ef).then_inc(s_n1[i], 1)
                    dve.wait_ge(s_n1[i], t + 1)
                    nc.vector.tensor_tensor(e16[i][1][:], ef, e16[i][0][:], ALU.subtract).then_inc(s_n2[i], 1)
                    for j in range(2):
                        if j == 1:
                            dve.wait_ge(s_n2[i], t + 1)
                        for h4 in range(4):
                            r = slice(32 * h4, 32 * h4 + 32)
                            last = nc.vector.transpose(q[i][j][r, :, h4], e16[i][j][r])
                    last.then_inc(s_q[i], 1)

                def step(t, halves):
                    for i in range(2):
                        for half in range(halves):
                            mask(t, i, half, halves)
                        for half in range(halves):
                            mask_low(t, i, half, halves)
                    for i in range(2):
                        softmax(t, i)
                        spread(t, i)

                dve.wait_ge(s_z, 16)
                dve.wait_ge(s_see, 16)
                with dve.Fori(0, HALF) as t:
                    step(t, 1)
                with dve.Fori(HALF, S) as t:
                    step(t, 2)


def ffn(nc, io, sb, res, hs):
    with ExitStack() as ctx:
        def tile(name, shape):
            return ctx.enter_context(nc.sbuf_tensor(name, shape, F32))

        def sem(name):
            return ctx.enter_context(nc.semaphore(name))

        ident, rows = sb["ident"], sb["rows"]
        n1 = tile("n1", [128, NT, DM])
        sq = tile("n1_sq", [128, NT, DM])
        nT = tile("n1_T", [DM, NT * 128])
        outw = tile("out_w", [128, HQ, DM])
        wr = tile("wr", [DM, E])
        w1 = tile("w1", [DM, FC, 128])
        b1 = tile("b1", [128, FC])
        w2 = tile("w2", [128, FC, DM])
        b2p = tile("b2p", [128, E, DM])
        earlier = tile("earlier", [128, E, E])
        stat = tile("f_stat", [128, 4, NT])
        mhalf = tile("f_mhalf", [128, NT])
        rw = tile("f_rw", [128, NT, E])
        wts = tile("f_wts", [128, NT, E])

        s_c = sem("p_const")
        s_o = sem("p_out")
        s_cen, s_sq, s_var, s_half, s_rstd, s_n1 = (sem(f"p_{k}") for k in ("cen", "sq", "var", "half", "rstd", "n1"))
        s_tr, s_ev = sem("p_tr"), sem("p_ev")
        s_log, s_sub, s_exp = sem("p_log"), sem("p_sub"), sem("p_exp")
        s_dve = sem("p_dve")

        with ExitStack() as inner:
            def psum(name, shape):
                return inner.enter_context(nc.psum_tensor(name, shape, F32))

            oP = psum("p_oP", [128, 6 * 512])
            tP = psum("p_tP", [64, 2, 512])
            gt = inner.enter_context(nc.sbuf_tensor("f_gt", [128, NT, E, E], F32))
            ge = inner.enter_context(nc.sbuf_tensor("f_ge", [128, NT, E, E], F32))
            PARTS = [(0, 24), (24, NT)]
            with nc.Block() as block:
                @block.sync
                def _(sp):
                    for dst, name in ((outw, "out_w"), (wr, "wr"), (w1, "w1"), (b1, "b1"), (w2, "w2"), (b2p, "b2p"),
                                      (earlier, "earlier")):
                        sp.dma_start(dst[:], io[name]).then_inc(s_c, 16)
                    sp.wait_ge(s_c, 7 * 16)

                @block.tensor
                def _(pe):
                    pe.wait_ge(s_c, 7 * 16)
                    for a, b in PARTS:
                        for n in range(a, b):
                            for g in range(HQ):
                                last = nc.tensor.matmul(oP[:, n * DM:(n + 1) * DM], hs[:, g, 2 * n:2 * n + 2, :],
                                                        outw[:, g, :], start=(g == 0), stop=(g == HQ - 1))
                        last.then_inc(s_o, 1)
                    for k in range((NT + 3) // 4):
                        pe.wait_ge(s_n1, 1 if 4 * k + 4 <= PARTS[0][1] else 2)
                        if k >= 2:
                            pe.wait_ge(s_ev, k - 1)
                        for j in range(min(4, NT - 4 * k)):
                            last = nc.tensor.transpose(tP[:, k % 2, j * 128:(j + 1) * 128], n1[:, 4 * k + j, :],
                                                       ident[:])
                        last.then_inc(s_tr, 1)
                    for n in range(NT):
                        if n % 4 == 0:
                            pe.wait_ge(s_ev, n // 4 + 1)
                        last = nc.tensor.matmul(oP[:, n * E:(n + 1) * E], nT[:, n * 128:(n + 1) * 128], wr[:],
                                                start=True, stop=True)
                    last.then_inc(s_log, 1)

                @block.scalar
                def _(act):
                    for p, (a, b) in enumerate(PARTS):
                        act.wait_ge(s_cen, p + 1)
                        nc.scalar.activation(sq[:, a:b, :], n1[:, a:b, :], ACT.Square).then_inc(s_sq, 1)
                    for k in range((NT + 3) // 4):
                        w = min(4, NT - 4 * k) * 128
                        act.wait_ge(s_tr, k + 1)
                        nc.scalar.copy(nT[:, k * 512:k * 512 + w], tP[:, k % 2, 0:w]).then_inc(s_ev, 1)
                    act.wait_ge(s_sub, 1)
                    nc.scalar.activation(rw[:], rw[:], ACT.Exp).then_inc(s_exp, 1)

                @block.gpsimd
                def _(pool):
                    nc.gpsimd.memset(mhalf[:], -0.5).then_inc(s_half, 1)
                    pool.wait_ge(s_half, 1)
                    for p, (a, b) in enumerate(PARTS):
                        pool.wait_ge(s_var, p + 1)
                        nc.gpsimd.tensor_tensor(stat[:, 3, a:b], stat[:, 2, a:b], mhalf[:, a:b],
                                                ALU.pow).then_inc(s_rstd, 1)

                @block.vector
                def _(dve):
                    own = Chain(s_dve)

                    def then(ins):
                        own.note(ins)
                        dve.wait_ge(s_dve, own.n)

                    for p, (a, b) in enumerate(PARTS):
                        dve.wait_ge(s_o, p + 1)
                        ov = oP[:, a * DM:b * DM].rearrange("p (n d) -> p n d", d=DM)
                        then(nc.vector.tensor_tensor(res[:, a:b, :], res[:, a:b, :], ov, ALU.add))
                        then(nc.vector.tensor_reduce(stat[:, 0, a:b], res[:, a:b, :], AX.X, ALU.add))
                        then(nc.vector.tensor_scalar(stat[:, 1, a:b], stat[:, 0, a:b], -1.0 / DM, None, ALU.mult))
                        nc.vector.tensor_tensor(n1[:, a:b, :], res[:, a:b, :], bc(stat[:, 1, a:b], 2, DM),
                                                ALU.add).then_inc(s_cen, 1)
                    for p, (a, b) in enumerate(PARTS):
                        dve.wait_ge(s_sq, p + 1)
                        then(nc.vector.tensor_reduce(stat[:, 0, a:b], sq[:, a:b, :], AX.X, ALU.add))
                        nc.vector.tensor_scalar(stat[:, 2, a:b], stat[:, 0, a:b], 1.0 / DM, EPS, ALU.mult,
                                                ALU.add).then_inc(s_var, 1)
                    for p, (a, b) in enumerate(PARTS):
                        dve.wait_ge(s_rstd, p + 1)
                        nc.vector.tensor_tensor(n1[:, a:b, :], n1[:, a:b, :], bc(stat[:, 3, a:b], 2, DM),
                                                ALU.mult).then_inc(s_n1, 1)
                    then(nc.vector.tensor_tensor(res[:], res[:], bc(rows[:, 5, :], 1, NT), ALU.add))
                    dve.wait_ge(s_log, 1)
                    lg = oP[:, 0:NT * E].rearrange("p (n e) -> p n e", e=E)
                    then(nc.vector.tensor_reduce(stat[:, 0, :], lg, AX.X, ALU.max))
                    nc.vector.tensor_tensor(rw[:], lg, bc(stat[:, 0, :], 2, E), ALU.subtract).then_inc(s_sub, 1)
                    dve.wait_ge(s_exp, 1)
                    then(nc.vector.tensor_reduce(stat[:, 0, :], rw[:], AX.X, ALU.add))
                    then(nc.vector.reciprocal(stat[:, 1, :], stat[:, 0, :]))
                    then(nc.vector.tensor_tensor(rw[:], rw[:], bc(stat[:, 1, :], 2, E), ALU.mult))
                    mine, other = bc(rw[:], 3, E), bc(rw[:], 2, E)
                    own.note(nc.vector.tensor_tensor(gt[:], other, mine, ALU.is_gt))
                    then(nc.vector.tensor_tensor(ge[:], other, mine, ALU.is_ge))
                    then(nc.vector.tensor_tensor(ge[:], ge[:], gt[:], ALU.subtract))
                    then(nc.vector.tensor_tensor(ge[:], ge[:], bc(earlier[:], 1, NT), ALU.mult))
                    then(nc.vector.tensor_tensor(ge[:], ge[:], gt[:], ALU.add))
                    then(nc.vector.tensor_reduce(wts[:], ge[:], AX.X, ALU.add))
                    then(nc.vector.scalar_tensor_tensor(out=wts[:], in0=wts[:], scalar=1.5, in1=rw[:],
                                                        op0=ALU.is_lt, op1=ALU.mult))
                    then(nc.vector.tensor_reduce(stat[:, 0, :], wts[:], AX.X, ALU.add))
                    then(nc.vector.reciprocal(stat[:, 1, :], stat[:, 0, :]))
                    then(nc.vector.tensor_tensor(wts[:], wts[:], bc(stat[:, 1, :], 2, E), ALU.mult))

        NG = NT // 2
        hg = [tile(f"hidden{i}", [128, 256]) for i in range(2)]
        ng = tile("n1_group", [DM, 2, 256])
        t1 = tile("weighted", [128, 2, E, DM])
        acc = tile("routed", [128, 2, DM])
        fin = tile("final", [128, 2, 2, DM])
        pH = ctx.enter_context(nc.psum_tensor("g_hid", [128, 2, 512], F32))
        pE = [ctx.enter_context(nc.psum_tensor(f"g_exp{i}", [128, 2, 512], F32)) for i in range(2)]
        pS = [ctx.enter_context(nc.psum_tensor(f"g_sh{i}", [128, 512], F32)) for i in range(2)]
        s_ng = sem("g_ng")
        s_hid = sem("g_hid")
        s_act = sem("g_act")
        s_exp2 = sem("g_expr")
        s_b = sem("g_bias")
        s_w = sem("g_weighted")
        s_r = sem("g_routed")
        s_s = sem("g_shared")
        s_f = sem("g_final")
        s_st = [sem(f"g_store{i}") for i in range(2)]

        def over_groups(engine, body):
            body(0, 0)
            body(1, 1)
            with engine.Fori(1, NG // 2) as pair:
                body(2 * pair, 0)
                body(2 * pair + 1, 1)
            body(NG - 1, 0)

        def after(eng, sem_, v):
            if not isinstance(v, int) or v > 0:
                eng.wait_ge(sem_, v)

        with nc.Block() as block:
            @block.tensor
            def _(pe):
                def down(j, p, c):
                    pe.wait_ge(s_act, FC * j + c + 1)
                    for a in range(2):
                        if c < 2 * E:
                            dst = pE[p][:, a, (c // 2) * DM:(c // 2 + 1) * DM]
                        else:
                            dst = pS[p][:, a * DM:(a + 1) * DM]
                        first = c % 2 == 0 and (c < 2 * E or a == 0)
                        last = nc.tensor.matmul(dst, hg[c % 2][:, a * 128:(a + 1) * 128], w2[:, c, :],
                                                start=first, stop=(c % 2 == 1), skip_group_check=c >= 2 * E)
                    return last

                def body(j, p):
                    after(pe, s_f, j - 1)
                    pe.wait_ge(s_ng, j + 1)
                    for c in range(FC):
                        if c >= 2:
                            pe.wait_ge(s_act, FC * j + c - 1)
                        else:
                            after(pe, s_act, FC * j + c - 1)
                        nc.tensor.matmul(pH[:, c % 2, 0:256], w1[:, c, :], ng[:, p, :], start=True,
                                         stop=True).then_inc(s_hid, 1)
                        if c:
                            down(j, p, c - 1)
                    down(j, p, FC - 1).then_inc(s_exp2, 1)
                over_groups(pe, body)

            @block.gpsimd
            def _(pool):
                def body(j, p):
                    after(pool, s_exp2, j - 1)
                    nc.gpsimd.tensor_copy(ng[:, p, :], nT[:, bass.ts(j, 256)]).then_inc(s_ng, 1)
                over_groups(pool, body)

            @block.scalar
            def _(act):
                def body(j, p):
                    for c in range(FC):
                        act.wait_ge(s_hid, FC * j + c + 1)
                        nc.scalar.activation(hg[c % 2][:], pH[:, c % 2, 0:256], ACT.Gelu,
                                             bias=b1[:, c:c + 1]).then_inc(s_act, 1)
                over_groups(act, body)

            @block.vector
            def _(dve):
                def body(j, p):
                    dve.wait_ge(s_exp2, j + 1)
                    for a in range(2):
                        nc.vector.tensor_tensor(t1[:, a], pE[p][:, a, :].rearrange("p (e d) -> p e d", e=E), b2p[:],
                                                ALU.add).then_inc(s_b, 1)
                    for a in range(2):
                        dve.wait_ge(s_b, 2 * j + a + 1)
                        nc.vector.tensor_tensor(t1[:, a], t1[:, a], bc(wts[:, 2 * j + a, :], 2, DM),
                                                ALU.mult).then_inc(s_w, 1)
                    for a in range(2):
                        dve.wait_ge(s_w, 2 * j + a + 1)
                        nc.vector.tensor_reduce(acc[:, a, :], t1[:, a].rearrange("p e d -> p d e"), AX.X,
                                                ALU.add).then_inc(s_r, 1)
                    for a in range(2):
                        dve.wait_ge(s_r, 2 * j + a + 1)
                        nc.vector.tensor_tensor(acc[:, a, :], acc[:, a, :], pS[p][:, a * DM:(a + 1) * DM],
                                                ALU.add).then_inc(s_s, 1)
                    dve.wait_ge(s_s, 2 * j + 2)
                    if isinstance(j, int):
                        after(dve, s_st[p], 32 * (j // 2))
                    else:
                        dve.wait_ge(s_st[p], (j - p) * 16)
                    nc.vector.tensor_tensor(fin[:, p], acc[:], res[:, bass.ts(j, 2), :], ALU.add).then_inc(s_f, 1)
                over_groups(dve, body)

            @block.sync
            def _(sp):
                def body(j, p):
                    sp.wait_ge(s_f, j + 1)
                    dst = io["out"].rearrange("s (j a b) d -> j b s a d", a=2, b=2)
                    for b in range(2):
                        sp.dma_start(dst[j, b], fin[b * S:(b + 1) * S, p]).then_inc(s_st[p], 16)
                over_groups(sp, body)
                sp.wait_ge(s_st[0], 32 * (NG - NG // 2))
                sp.wait_ge(s_st[1], 32 * (NG // 2))


def recur_and_ffn(nc, io, sb, res, rk16, vscale):
    with nc.sbuf_tensor("hs", [128, HQ, B, S], F32) as hs:
        recur(nc, io, hs, rk16, vscale)
        ffn(nc, io, sb, res, hs)


def program(nc, io):
    with ExitStack() as ctx:
        def tile(name, shape):
            return ctx.enter_context(nc.sbuf_tensor(name, shape, F32))

        def scratch(name, shape, dt=F32):
            return nc.dram_tensor(name, shape, dt, kind="Internal").ap()

        io["feat"] = [scratch(f"d_feat{j}", [NT, 128, 3 * HD], F16) for j in range(2)]
        io["val"] = scratch("d_val", [NT, 128, 2 * HD + 2 * H])
        io["diag"] = [scratch(f"d_diag{y}", [NT, 128, HD]) for y in range(2)]
        io["tinv"] = [scratch(f"d_tinv{y}", [NT, 128, H * BLK]) for y in range(2)]
        io["u2"] = [scratch(f"d_u2{j}", [NT, 128, HD], F16) for j in range(2)]
        io["z"] = scratch("d_z", [128, HQ, NT, 128])
        res = tile("res", [128, NT, DM])
        vscale = tile("vscale", [128, 3])
        sb = {"rows": tile("rows", [128, 6, DM]), "ident": tile("ident", [128, 128])}
        rk16 = [ctx.enter_context(nc.sbuf_tensor(f"rk16_{j}", [128, HQ, 2, B * S // 2], F16)) for j in range(2)]
        with nc.sbuf_tensor("oT", [DM, NT * 128], F32) as oT:
            embed(nc, io, sb, res, oT)
            features(nc, io, sb, oT, rk16, vscale)
        inverses(nc, io)
        solve(nc, io, vscale)
        recur_and_ffn(nc, io, sb, res, rk16, vscale)


OUT = ((S, B, DM), "float32")


def kernel(**inputs):
    import concourse.bacc as _bacc
    from concourse.bass_utils import run_bass_kernel_spmd as _run

    a = {k: np.asarray(v) for k, v in inputs.items()}
    frames = a["x"][:, :NCH * 8, :].reshape(S, NCH, 8 * 16).transpose(2, 1, 0)
    sw = a["L0_attn_slow_W"].reshape(H, 5 * D + 2, DM)
    parts = [sw[:, j * D:(j + 1) * D].reshape(HD, DM) for j in (0, 1, 3, 2, 4)]
    parts[3:3] = [sw[:, 5 * D], sw[:, 5 * D + 1]]
    rows = np.stack([a[k] for k in ("L0_tok_b", "L0_tok_gamma", "L0_tok_beta", "L0_attn_ln_g", "L0_attn_ln_b",
                                    "L0_ffn_b2s")])
    tok = np.arange(128)
    b_, t_ = tok // S, tok % S
    same = b_[:, None] == b_[None, :]
    before = same & (t_[:, None] // BLK < t_[None, :] // BLK)
    causal = same & (t_[:, None] <= t_[None, :])
    step = np.arange(S // 2)
    b4, s4 = tok // 32, tok % 32
    see4 = (s4[:, None, None] <= step[None, :, None]) & (b4[:, None, None] == np.arange(16)[None, None, :] // 4)
    e_ = np.arange(E)
    given = {
        "frames": frames,
        "tok_w": a["L0_tok_W"].T.reshape(2, 128, DM).transpose(1, 0, 2),
        "rows": np.broadcast_to(rows[None], (128, 6, DM)),
        "ident": np.eye(128, dtype=np.float32),
        "slow_w": np.concatenate(parts, 0).T,
        "masks": np.stack([before, causal], 1).astype(np.float32) / np.float32(UNIT),
        "own_blk": (tok[:, None] // BLK == tok[None, :] // BLK).astype(np.float32),
        "see4": see4.astype(np.float32) / np.float32(UNIT),
        "out_w": a["L0_attn_out_W"].T.reshape(HQ, 128, DM).transpose(1, 0, 2),
        "wr": a["L0_ffn_Wr"],
        "w1": np.concatenate([a["L0_ffn_W1p"].transpose(1, 0, 2), a["L0_ffn_W1s"][:, None]], 1).reshape(DM, FC, 128),
        "b1": np.concatenate([a["L0_ffn_b1p"], a["L0_ffn_b1s"][None]], 0).reshape(FC, 128).T,
        "w2": np.concatenate([a["L0_ffn_W2p"], a["L0_ffn_W2s"][None]], 0).reshape(FC, 128, DM).transpose(1, 0, 2),
        "b2p": np.broadcast_to(a["L0_ffn_b2p"][None], (128, E, DM)),
        "earlier": np.broadcast_to((e_[None, :] < e_[:, None]).astype(np.float32), (128, E, E)),
    }
    nc = _bacc.Bacc("TRN2", target_bir_lowering=False, num_devices=1)
    arrays, io = {}, {}
    for name, v in given.items():
        v = np.ascontiguousarray(v)
        arrays[f"in_{name}"] = v
        io[name] = nc.dram_tensor(f"in_{name}", v.shape, mybir.dt.from_np(v.dtype), kind="ExternalInput").ap()
    io["out"] = nc.dram_tensor("out", OUT[0], F32, kind="ExternalOutput").ap()
    program(nc, io)
    r = _run(nc, [arrays], core_ids=[0])
    return r.results[0]["out"]
```

```python
from contextlib import ExitStack

import numpy as np

import concourse.bass as bass
from concourse import mybir

F32 = mybir.dt.float32
F16 = mybir.dt.float16
I32 = mybir.dt.int32
ALU = mybir.AluOpType
ACT = mybir.ActivationFunctionType
AX = mybir.AxisListType
RMAX = bass.bass_isa.ReduceOp.max

S = 64
B = 92
DM = 64
H = 8
D = 32
HQ = H // 4
NT = B // 2
HD = H * D
NCH = B + 1
BLK = 16
NB = S // BLK
NP = 3 * HD + 2 * HD + 2 * H
EPS = 1e-5
E = 8

UNIT = 2.0 ** 14
VTOP = 2.0 ** 9
FC = 18


def bc(ap, axis, n):
    v = ap.unsqueeze(axis)
    shape = list(v.shape)
    shape[axis] = n
    return v.broadcast_to(shape)


class Chain:

    def __init__(self, sem):
        self.sem, self.n = sem, 0

    def note(self, ins):
        self.n += 1
        ins.then_inc(self.sem, 1)
        return ins


def over_tiles(engine, body):
    body(0, 0)
    body(1, 1)
    with engine.Fori(1, NT // 2 - 1) as pair:
        body(2 * pair, 0)
        body(2 * pair + 1, 1)
    body(NT - 2, 0)
    body(NT - 1, 1)


def embed(nc, io, sb, res, oT, w16, pback):
    OTOP = 2.0 ** 14
    WTOP = 2.0 ** 13
    P2 = [(0, 24), (24, NT)]
    with ExitStack() as ctx:
        def tile(name, shape, dt=F32):
            return ctx.enter_context(nc.sbuf_tensor(name, shape, dt))

        def sem(name):
            return ctx.enter_context(nc.semaphore(name))

        w = tile("slow_w", [128, NP])
        o16 = tile("o_parts", [128, NT, 2, DM], F16)
        ident16 = tile("e_ident16", [128, 128], F16)
        big = tile("e_top", [128, 4])
        fac = tile("e_factor", [128, 2])
        frames = tile("frames", [128, NCH, S])
        tokw = tile("tokw", [128, 2, DM])
        x = tile("x_tok", [128, NT, DM])
        xc = tile("x_centred", [128, NT, DM])
        a0 = tile("a0", [128, NT, DM])
        sq = tile("x_squared", [128, NT, DM])
        ssum = tile("row_sum", [128, NT])
        nmean = tile("neg_mean", [128, NT])
        var = tile("row_var", [128, NT])
        rstd = tile("row_rstd", [128, NT])
        mhalf = tile("minus_half", [128, NT])
        rows, ident = sb["rows"], sb["ident"]
        yP = ctx.enter_context(nc.psum_tensor("yP", [128, 6 * 512], F32))
        tP = ctx.enter_context(nc.psum_tensor("tP", [128, 2, 1024], F16))

        s_w = sem("e_w")
        s_top, s_all = sem("e_tops"), sem("e_all")
        s_const = sem("e_const")
        s_frames = [sem(f"e_frames{i}") for i in range(2)]
        s_y = sem("e_y")
        s_cen = sem("e_centred")
        s_sq = sem("e_squared")
        s_var = sem("e_var")
        s_rstd = sem("e_rstd")
        s_half = sem("e_half")
        s_o = sem("e_o")
        s_tr = sem("e_tr")
        s_ev = sem("e_ev")
        s_dve = sem("e_dve")

        with nc.Block() as block:
            @block.sync
            def _(sp):
                half = 2 * P2[1][0] + 1
                sp.dma_start(tokw[:], io["tok_w"]).then_inc(s_const, 16)
                sp.dma_start(frames[:, 0:half, :], io["frames"][:, 0:half, :]).then_inc(s_frames[0], 16)
                for j in range(2):
                    sp.dma_start(w[j * DM:(j + 1) * DM], io["slow_w"]).then_inc(s_w, 16)
                sp.dma_start(frames[:, half:NCH, :], io["frames"][:, half:NCH, :]).then_inc(s_frames[1], 16)
                sp.dma_start(rows[:], io["rows"]).then_inc(s_const, 16)
                sp.dma_start(ident[:], io["ident"]).then_inc(s_const, 16)

            @block.tensor
            def _(pe):
                pe.wait_ge(s_const, 48)
                pe.wait_ge(s_frames[0], 16)
                for n in range(NT):
                    if n == P2[1][0]:
                        last.then_inc(s_y, 1)
                        pe.wait_ge(s_frames[1], 16)
                    for g in range(2):
                        last = nc.tensor.matmul(yP[:, n * DM:(n + 1) * DM], frames[:, 2 * n + g:2 * n + g + 2, :],
                                                tokw[:, g, :], start=(g == 0), stop=(g == 1))
                last.then_inc(s_y, 1)
                for g in range((NT + 7) // 8):
                    pe.wait_ge(s_o, 1 if 8 * g + 8 <= P2[0][1] else 2)
                    if g >= 2:
                        pe.wait_ge(s_ev, g - 1)
                    for j in range(min(8, NT - 8 * g)):
                        last = nc.tensor.transpose(tP[:, g % 2, j * 128:(j + 1) * 128],
                                                   o16[:, 8 * g + j].rearrange("p j d -> p (j d)"), ident16[:])
                    last.then_inc(s_tr, 1)

            @block.scalar
            def _(act):
                for ln in range(3):
                    for p, (a, b) in enumerate(P2):
                        act.wait_ge(s_cen, 2 * ln + p + 1)
                        nc.scalar.activation(sq[:, a:b, :], xc[:, a:b, :], ACT.Square).then_inc(s_sq, 1)
                for g in range((NT + 7) // 8):
                    c = min(8, NT - 8 * g) * 128
                    act.wait_ge(s_tr, g + 1)
                    nc.scalar.copy(oT[:, g * 1024:g * 1024 + c], tP[:, g % 2, 0:c]).then_inc(s_ev, 1)

            @block.gpsimd
            def _(pool):
                nc.gpsimd.memset(mhalf[:], -0.5).then_inc(s_half, 1)
                pool.wait_ge(s_half, 1)
                pool.wait_ge(s_top, 1)
                nc.gpsimd.partition_all_reduce(big[:, 0:1], big[:, 0:1], 128, RMAX).then_inc(s_all, 1)
                for ln in range(3):
                    for p, (a, b) in enumerate(P2):
                        pool.wait_ge(s_var, 2 * ln + p + 1)
                        nc.gpsimd.tensor_tensor(rstd[:, a:b], var[:, a:b], mhalf[:, a:b], ALU.pow).then_inc(s_rstd, 1)

            @block.vector
            def _(dve):
                own = Chain(s_dve)

                def then(ins):
                    own.note(ins)
                    dve.wait_ge(s_dve, own.n)

                def row(r, a, b):
                    return bc(rows[:, r, :], 1, b - a)

                dve.wait_ge(s_const, 48)
                own.note(nc.vector.tensor_copy(ident16[:], ident[:]))
                for k in range(2):
                    own.note(nc.vector.tensor_reduce(big[:, 1 + k:2 + k], rows[:, 3 + k, :], AX.X, ALU.max,
                                                     apply_absolute_value=True))
                dve.wait_ge(s_w, 32)
                nc.vector.tensor_reduce(big[:, 0:1], w[:], AX.X, ALU.max, apply_absolute_value=True).then_inc(s_top, 1)
                dve.wait_ge(s_dve, own.n)
                then(nc.vector.scalar_tensor_tensor(out=big[:, 3:4], in0=big[:, 1:2], scalar=float(DM) ** 0.5,
                                                    in1=big[:, 2:3], op0=ALU.mult, op1=ALU.add))
                then(nc.vector.tensor_scalar(big[:, 3:4], big[:, 3:4], 1e-30, 1.0 / OTOP, ALU.max, ALU.mult))
                dve.wait_ge(s_all, 1)
                then(nc.vector.tensor_scalar(big[:, 0:1], big[:, 0:1], 1e-30, 1.0 / WTOP, ALU.max, ALU.mult))
                own.note(nc.vector.reciprocal(fac[:, 0:1], big[:, 0:1]))
                own.note(nc.vector.reciprocal(fac[:, 1:2], big[:, 3:4]))
                then(nc.vector.tensor_tensor(pback[:, 0:1], big[:, 0:1], big[:, 3:4], ALU.mult))
                then(nc.vector.tensor_scalar(pback[:, 1:2], pback[:, 0:1], -1.0, None, ALU.mult))
                then(nc.vector.tensor_scalar(w16[0][:], w[:], fac[:, 0:1], None, ALU.mult))
                then(nc.vector.scalar_tensor_tensor(out=w16[1][:], in0=w[:], scalar=fac[:, 0:1], in1=w16[0][:],
                                                    op0=ALU.mult, op1=ALU.subtract))
                for p, (a, b) in enumerate(P2):
                    dve.wait_ge(s_y, p + 1)
                    yv = yP[:, a * DM:b * DM].rearrange("p (n d) -> p n d", d=DM)
                    own.note(nc.vector.tensor_tensor(x[:, a:b, :], yv, row(0, a, b), ALU.add))
                for ln in range(3):
                    src = a0 if ln == 2 else x
                    dve.wait_ge(s_dve, own.n)
                    for p, (a, b) in enumerate(P2):
                        then(nc.vector.tensor_reduce(ssum[:, a:b], src[:, a:b, :], AX.X, ALU.add))
                        then(nc.vector.tensor_scalar(nmean[:, a:b], ssum[:, a:b], -1.0 / DM, None, ALU.mult))
                        nc.vector.tensor_tensor(xc[:, a:b, :], src[:, a:b, :], bc(nmean[:, a:b], 2, DM),
                                                ALU.add).then_inc(s_cen, 1)
                    for p, (a, b) in enumerate(P2):
                        dve.wait_ge(s_sq, 2 * ln + p + 1)
                        then(nc.vector.tensor_reduce(ssum[:, a:b], sq[:, a:b, :], AX.X, ALU.add))
                        nc.vector.tensor_scalar(var[:, a:b], ssum[:, a:b], 1.0 / DM, EPS, ALU.mult,
                                                ALU.add).then_inc(s_var, 1)
                    for p, (a, b) in enumerate(P2):
                        r = bc(rstd[:, a:b], 2, DM)
                        dve.wait_ge(s_rstd, 2 * ln + p + 1)
                        if ln == 0:
                            then(nc.vector.tensor_tensor(xc[:, a:b, :], xc[:, a:b, :], r, ALU.mult))
                            then(nc.vector.tensor_tensor(xc[:, a:b, :], xc[:, a:b, :], row(1, a, b), ALU.mult))
                            then(nc.vector.tensor_tensor(x[:, a:b, :], xc[:, a:b, :], row(2, a, b), ALU.add))
                        elif ln == 1:
                            then(nc.vector.tensor_tensor(a0[:, a:b, :], xc[:, a:b, :], r, ALU.mult))
                            own.note(nc.vector.tensor_tensor(res[:, a:b, :], x[:, a:b, :], a0[:, a:b, :], ALU.add))
                        else:
                            then(nc.vector.tensor_tensor(xc[:, a:b, :], xc[:, a:b, :], r, ALU.mult))
                            then(nc.vector.tensor_tensor(xc[:, a:b, :], xc[:, a:b, :], row(3, a, b), ALU.mult))
                            then(nc.vector.tensor_tensor(xc[:, a:b, :], xc[:, a:b, :], row(4, a, b), ALU.add))
                            then(nc.vector.tensor_scalar(o16[:, a:b, 0, :], xc[:, a:b, :], fac[:, 1:2], None, ALU.mult))
                            nc.vector.scalar_tensor_tensor(out=o16[:, a:b, 1, :], in0=xc[:, a:b, :],
                                                           scalar=fac[:, 1:2], in1=o16[:, a:b, 0, :], op0=ALU.mult,
                                                           op1=ALU.subtract).then_inc(s_o, 1)


def features(nc, io, sb, oT, w16, pback, rk16, vmax):
    OWN = 3
    with ExitStack() as ctx:
        def tile(name, shape):
            return ctx.enter_context(nc.sbuf_tensor(name, shape, F32))

        def sem(name):
            return ctx.enter_context(nc.semaphore(name))

        ident = sb["ident"]
        ot = ctx.enter_context(nc.sbuf_tensor("o_tile", [128, 2, 128], F16))
        one = tile("elu_x", [128, 2 * HD])
        low = tile("min_qk", [128, 2 * HD])
        top = tile("max_rk", [128, H])
        feat = tile("feat", [128, 3 * HD])
        tot = tile("feat_sum", [128, 3 * H])
        rtot = tile("feat_rsum", [128, 3 * H])
        gate = tile("gate", [128, 2 * H])
        fn = tile("feat_n", [128, 2, 3 * HD])
        ft = tile("feat_t", [128, 2, 3 * HD])
        f16 = [ctx.enter_context(nc.sbuf_tensor(f"feat_t16_{j}", [128, 2, 3 * HD], F16)) for j in range(2)]
        val = tile("val", [128, 2, 2 * HD + 2 * H])
        diag = tile("diag", [128, 2, 2, HD])
        vtile = tile("vtile", [128, NT])
        pq = ctx.enter_context(nc.psum_tensor("proj", [128, 3, 512], F32))
        pt = ctx.enter_context(nc.psum_tensor("turned", [128, 512], F32))
        pg = ctx.enter_context(nc.psum_tensor("gram", [128, 4, 512], F32))

        s_ot = sem("f_ot")
        s_proj = sem("f_proj")
        s_low = sem("f_low")
        s_exp = sem("f_exp")
        s_one = sem("f_one")
        s_rk0 = sem("f_rk0")
        s_rk1 = sem("f_rk1")
        s_pqdve = sem("f_pqdve")
        s_pqact = sem("f_pqact")
        s_gate = sem("f_gate")
        s_gexp = sem("f_gexp")
        s_rs = sem("f_rs")
        s_fn = sem("f_fn")
        s_val = sem("f_val")
        s_tr = sem("f_tr")
        s_ft = sem("f_ft")
        s_rkc = sem("f_rkc")
        s_vm = sem("f_vm")
        s_vall = sem("f_vall")
        s_alone = sem("f_alone")
        s_f16 = [sem(f"f_f16_{j}") for j in range(2)]
        s_gr = sem("f_gr")
        s_dg = sem("f_dg")
        s_out = [[sem(f"f_out{p}{j}") for j in range(3)] for p in range(2)]
        s_dve = sem("f_dve")

        with nc.Block() as block:
            @block.sync
            def _(sp):
                for p in range(2):
                    sp.sem_inc(s_out[p][0], 16)
                    sp.sem_inc(s_out[p][2], 16)

                def body(n, p):
                    sp.wait_ge(s_val, n + 1)
                    sp.dma_start(io["val"][n], val[:, p, :]).then_inc(s_out[p][1], 16)
                    for j in range(2):
                        sp.wait_ge(s_f16[j], n + 1)
                        sp.dma_start(io["feat"][j][n], f16[j][:, p, :]).then_inc(s_out[p][0], 16)
                    sp.wait_ge(s_dg, n + 1)
                    for y in range(2):
                        sp.dma_start(io["diag"][y][n], diag[:, p, y, :]).then_inc(s_out[p][2], 16)

                over_tiles(sp, body)
                for p in range(2):
                    sp.wait_ge(s_out[p][0], 32 * (NT // 2) + 16)
                    sp.wait_ge(s_out[p][1], 16 * (NT // 2))
                    sp.wait_ge(s_out[p][2], 32 * (NT // 2) + 16)

            def stored(eng, n, p, which, per=16):
                if isinstance(n, int):
                    if n < 2:
                        return
                    eng.wait_ge(s_out[p][which], per * (n // 2))
                else:
                    eng.wait_ge(s_out[p][which], (n - p) * (per // 2))

            def after(eng, sem_, v):
                if not isinstance(v, int) or v > 0:
                    eng.wait_ge(sem_, v)

            @block.gpsimd
            def _(pool):
                def fetch(n, p):
                    after(pool, s_proj, n - 1)
                    nc.gpsimd.tensor_copy(ot[:, p, :], oT[:, bass.ts(n, 128)]).then_inc(s_ot, 1)

                def body(n, p):
                    if not (isinstance(n, int) and n == NT - 1):
                        fetch(n + 1, 1 - p)
                    pool.wait_ge(s_rs, n + 1)
                    after(pool, s_tr, 2 * n - 2)
                    f3 = feat[:].rearrange("p (g d) -> p g d", d=D)
                    nc.gpsimd.tensor_tensor(fn[:, p, :].rearrange("p (g d) -> p g d", d=D), f3,
                                            bc(rtot[:], 2, D), ALU.mult).then_inc(s_fn, 1)
                fetch(0, 0)
                over_tiles(pool, body)
                pool.wait_ge(s_vall, 1)
                nc.gpsimd.partition_all_reduce(vmax[:, 1:2], vmax[:, 0:1], 128, RMAX).then_inc(s_vall, 1)

            @block.tensor
            def _(pe):
                def project(n, p):
                    pe.wait_ge(s_ot, n + 1)
                    after(pe, s_pqdve, n)
                    after(pe, s_pqact, n)
                    for k, (a, b) in enumerate(((0, 2 * HD), (2 * HD, 3 * HD + 2 * H), (3 * HD + 2 * H, NP))):
                        for j in range(2):
                            last = nc.tensor.matmul(pq[:, k, 0:b - a], ot[:, p, :], w16[j][:, a:b], start=(j == 0),
                                                    stop=(j == 1))
                    last.then_inc(s_proj, 1)

                def grams(n, p):
                    pe.wait_ge(s_fn, n + 1)
                    after(pe, s_ft, 2 * n)
                    after(pe, s_dg, n)
                    for j in range(4):
                        last = nc.tensor.transpose(pt[:, j * 128:(j + 1) * 128],
                                                   fn[:, p, j * 128:(j + 1) * 128], ident[:])
                    last.then_inc(s_tr, 1)
                    for j in range(2):
                        last = nc.tensor.transpose(pg[:, j, 256:384], fn[:, p, (4 + j) * 128:(5 + j) * 128], ident[:])
                    last.then_inc(s_tr, 1)
                    pe.wait_ge(s_ft, 2 * n + 2)
                    nc.tensor.sem_inc(s_alone, 1)
                    for y in range(2):
                        for g in range(HQ):
                            c = (2 + 2 * y + g) * 128
                            for tb in range(4):
                                for h4 in range(4):
                                    q = slice(32 * h4, 32 * h4 + 32)
                                    cc = c + 32 * tb
                                    o = (y * HQ + g) * 32
                                    last = nc.tensor.matmul(pg[32 * tb:32 * tb + 32, h4, o:o + 32],
                                                            ft[q, p, cc:cc + 32], ft[q, p, cc:cc + 32],
                                                            start=True, stop=True)
                    last.then_inc(s_gr, 1)

                project(0, 0)

                def body(n, p):
                    if isinstance(n, int) and n == NT - 1:
                        grams(n, p)
                        return
                    project(n + 1, 1 - p)
                    grams(n, p)
                over_tiles(pe, body)

            def copy_rk(eng, copy, n, p, j):
                for g in range(HQ):
                    src = f16[j][:, p, (4 + g) * 128:(5 + g) * 128].rearrange("p (b a s) -> p a b s", b=2, a=2)
                    dst = rk16[j][:, g].rearrange("p a (b s) -> p a b s", s=S // 2)[:, :, bass.ts(n, 2), :]
                    copy(dst, src).then_inc(s_rkc, 1)

            @block.scalar
            def _(act):
                def split(n, p):
                    act.wait_ge(s_ft, 2 * n + 2)
                    if not isinstance(n, int):
                        act.wait_ge(s_out[p][0], (n - p) * 16 + 16)
                    elif n >= 2:
                        act.wait_ge(s_out[p][0], 32 * (n // 2) + 16)
                    nc.scalar.mul(f16[0][:, p, :], ft[:, p, :], UNIT).then_inc(s_f16[0], 1)
                    act.wait_ge(s_f16[0], n + 1)
                    copy_rk(act, nc.scalar.copy, n, p, 0)

                def body(n, p):
                    act.wait_ge(s_proj, n + 1)
                    stored(act, n, p, 1)
                    after(act, s_vm, n - 1)
                    nc.scalar.mul(val[:, p, 0:2 * HD], pq[:, 2, :], pback[:, 0:1]).then_inc(s_pqact, 1)
                    after(act, s_pqdve, n)
                    act.wait_ge(s_low, n + 1)
                    nc.scalar.activation(one[:], pq[:, 0, :], ACT.Copy, bias=1.0,
                                         scale=pback[:, 0:1]).then_inc(s_one, 1)
                    nc.scalar.activation(low[:], low[:], ACT.Exp).then_inc(s_exp, 1)
                    act.wait_ge(s_gate, n + 1)
                    nc.scalar.activation(gate[:], gate[:], ACT.Exp, scale=pback[:, 1:2]).then_inc(s_gexp, 1)
                    act.wait_ge(s_rk0, n + 1)
                    nc.scalar.activation(feat[:, 2 * HD:3 * HD], feat[:, 2 * HD:3 * HD], ACT.Exp,
                                         scale=pback[:, 0:1]).then_inc(s_rk1, 1)
                    if not (isinstance(n, int) and n == 0):
                        split(n - 1, 1 - p)
                    act.wait_ge(s_tr, 2 * n + 1)
                    after(act, s_f16[1], n - 1)
                    nc.scalar.copy(ft[:, p, 0:512], pt[:]).then_inc(s_ft, 1)
                    act.wait_ge(s_tr, 2 * n + 2)
                    nc.scalar.copy(ft[:, p, 512:768].rearrange("p (a b) -> p a b", a=2),
                                   pg[:, 0:2, 256:384]).then_inc(s_ft, 1)
                over_tiles(act, body)
                split(NT - 1, (NT - 1) % 2)

            @block.vector
            def _(dve):
                def stored_late(n, p, which):
                    if not isinstance(n, int):
                        dve.wait_ge(s_out[p][which], (n - p) * 16 + 16)
                    elif n >= 2:
                        dve.wait_ge(s_out[p][which], 32 * (n // 2) + 16)

                def scale_diag(n, p):
                    dve.wait_ge(s_gr, n + 1)
                    stored_late(n, p, 2)
                    for y in range(2):
                        for g in range(HQ):
                            o = (y * HQ + g) * 32
                            b4 = val[:, p, 2 * HD + y * H + 4 * g:2 * HD + y * H + 4 * g + 4]
                            last = nc.vector.tensor_tensor(
                                diag[:, p, y, g * 128:(g + 1) * 128].rearrange("p (h s) -> p h s", s=32),
                                pg[:, :, o:o + 32], bc(b4, 2, 32), ALU.mult)
                    last.then_inc(s_dg, 1)
                    dve.wait_ge(s_f16[0], n + 1)
                    stored_late(n, p, 0)
                    nc.vector.scalar_tensor_tensor(out=f16[1][:, p, :], in0=ft[:, p, :], scalar=UNIT,
                                                   in1=f16[0][:, p, :], op0=ALU.mult,
                                                   op1=ALU.subtract).then_inc(s_f16[1], 1)
                    nc.vector.tensor_reduce(vtile[:, bass.ts(n, 1)], val[:, p, 0:2 * HD], AX.X, ALU.max,
                                            apply_absolute_value=True).then_inc(s_vm, 1)
                    dve.wait_ge(s_f16[1], n + 1)
                    copy_rk(dve, nc.vector.tensor_copy, n, p, 1)

                def body(n, p):
                    f3 = feat[:].rearrange("p (g d) -> p g d", d=D)
                    dve.wait_ge(s_proj, n + 1)
                    after(dve, s_exp, n)
                    nc.vector.tensor_scalar(low[:], pq[:, 0, :], pback[:, 0:1], 0.0, ALU.mult,
                                            ALU.min).then_inc(s_low, 1)
                    r3 = pq[:, 1, 0:HD].rearrange("p (g d) -> p g d", d=D)
                    nc.vector.tensor_reduce(top[:], r3, AX.X, ALU.max).then_inc(s_dve, 1)
                    after(dve, s_val, n)
                    nc.vector.tensor_copy(gate[:], pq[:, 1, HD:HD + 2 * H]).then_inc(s_gate, 1)
                    after(dve, s_fn, n)
                    dve.wait_ge(s_dve, OWN * n + 1)
                    nc.vector.tensor_tensor(f3[:, 2 * H:3 * H, :], r3, bc(top[:], 2, D),
                                            ALU.subtract).then_inc(s_rk0, 1)
                    dve.wait_ge(s_exp, n + 1)
                    dve.wait_ge(s_one, n + 1)
                    nc.vector.tensor_tensor(feat[:, 0:2 * HD], one[:], low[:], ALU.max).then_inc(s_pqdve, 1)
                    dve.wait_ge(s_gexp, n + 1)
                    nc.vector.tensor_scalar(gate[:], gate[:], 1.0, None, ALU.add).then_inc(s_dve, 1)
                    dve.wait_ge(s_rk1, n + 1)
                    dve.wait_ge(s_pqdve, n + 1)
                    nc.vector.tensor_reduce(tot[:], f3, AX.X, ALU.add).then_inc(s_dve, 1)
                    dve.wait_ge(s_dve, OWN * n + 2)
                    dve.wait_ge(s_pqact, n + 1)
                    stored(dve, n, p, 1)
                    nc.vector.reciprocal(val[:, p, 2 * HD:2 * HD + 2 * H], gate[:]).then_inc(s_val, 1)
                    dve.wait_ge(s_dve, OWN * n + 3)
                    nc.vector.reciprocal(rtot[:], tot[:]).then_inc(s_rs, 1)
                    if not (isinstance(n, int) and n == 0):
                        scale_diag(n - 1, 1 - p)
                over_tiles(dve, body)
                scale_diag(NT - 1, (NT - 1) % 2)
                dve.wait_ge(s_vm, NT)
                nc.vector.tensor_reduce(vmax[:, 0:1], vtile[:], AX.X, ALU.max).then_inc(s_vall, 1)
                dve.wait_ge(s_vall, 2)
                nc.vector.tensor_scalar(vmax[:, 1:2], vmax[:, 1:2], 1e-30, 1.0 / VTOP, ALU.max,
                                        ALU.mult).then_inc(s_vall, 1)
                dve.wait_ge(s_vall, 3)
                nc.vector.tensor_scalar(vmax[:, 2:3], vmax[:, 1:2], 1.0 / UNIT, None, ALU.mult).then_inc(s_vall, 1)
                dve.wait_ge(s_vall, 4)
                nc.vector.reciprocal(vmax[:, 1:2], vmax[:, 1:2]).then_inc(s_vall, 1)


def inverses(nc, io):
    with ExitStack() as ctx:
        def tile(name, shape):
            return ctx.enter_context(nc.sbuf_tensor(name, shape, F32))

        def sem(name):
            return ctx.enter_context(nc.semaphore(name))

        HS = S // 2
        a = tile("a_half", [B, 2, HS, HD])
        tt = tile("t_transposed", [B, 2, S, H * BLK])
        prod = tile("products", [B, 2, H * (BLK - 1) * (BLK - 1)])
        s_in = [sem(f"i_in{j}") for j in range(2)]
        s_init = sem("i_init")
        s_done = sem("i_done")
        s_out = sem("i_out")
        s_dve = sem("i_dve")
        s_pool = sem("i_pool")
        HV = 3

        def count(k, t):
            return 4 * ((BLK - 1) * k + t)

        parts = [(y, half) for y in range(2) for half in range(2)]

        with nc.Block() as block:
            @block.sync
            def _(sp):
                for k, (y, half) in enumerate(parts):
                    if k >= 2:
                        sp.wait_ge(s_done, k - 1)
                    src = io["diag"][y][:].rearrange("n (b t) c -> (n b) t c", b=2)
                    sp.dma_start(a[:, k % 2], src[:, half * HS:(half + 1) * HS, :]).then_inc(s_in[k % 2], 16)
                    if k >= 1:
                        yy, hh = parts[k - 1]
                        sp.wait_ge(s_done, k)
                        dst = io["tinv"][yy][:].rearrange("n (b t) c -> (n b) t c", b=2)
                        sp.dma_start(dst[:, hh * HS:(hh + 1) * HS, :],
                                     tt[:, yy, hh * HS:(hh + 1) * HS, :]).then_inc(s_out, 16)
                yy, hh = parts[-1]
                sp.wait_ge(s_done, len(parts))
                dst = io["tinv"][yy][:].rearrange("n (b t) c -> (n b) t c", b=2)
                sp.dma_start(dst[:, hh * HS:(hh + 1) * HS, :],
                             tt[:, yy, hh * HS:(hh + 1) * HS, :]).then_inc(s_out, 16)
                sp.wait_ge(s_out, 16 * len(parts))

            def views(k, blk, t, h0, h1):
                y, half = parts[k]
                x0 = (half * 2 + blk) * BLK
                row = a[:, k % 2, blk * BLK + t, :].rearrange("p (h s) -> p h s", s=2 * BLK)
                row = bc(row[:, h0:h1, blk * BLK:blk * BLK + t], 2, t)
                t3 = tt[:, y, x0:x0 + t, :].rearrange("p x (h t) -> p h x t", t=BLK)[:, h0:h1]
                room = prod[:, blk, h0 * t * t:h1 * t * t].rearrange("p (h x s) -> p h x s", x=t, s=t)
                return row, t3[:, :, :, 0:t], room, t3[:, :, :, t]

            @block.gpsimd
            def _(pool):
                for k, (y, half) in enumerate(parts):
                    own = tt[:, y, half * HS:(half + 1) * HS, :]
                    nc.gpsimd.memset(own, 0.0).then_inc(s_init, 1)
                    pool.wait_ge(s_init, 2 * k + 1)
                    for x in range(BLK):
                        diag = own.rearrange("p (k x) (h t) -> p k x h t", x=BLK, t=BLK)[:, :, x, :, x]
                        last = nc.gpsimd.memset(diag, 1.0)
                    last.then_inc(s_init, 1)
                for k in range(len(parts)):
                    pool.wait_ge(s_in[k % 2], 16 * (k // 2 + 1))
                    for t in range(1, BLK):
                        for blk in range(2):
                            if k or t > 1:
                                pool.wait_ge(s_dve, count(k, t - 1) - 1 + blk)
                            row, before, room, _ = views(k, blk, t, HV, H)
                            nc.gpsimd.tensor_tensor(room, row, before, ALU.mult).then_inc(s_pool, 1)

            @block.vector
            def _(dve):
                own = Chain(s_dve)
                for k in range(len(parts)):
                    dve.wait_ge(s_init, 2 * k + 2)
                    dve.wait_ge(s_in[k % 2], 16 * (k // 2 + 1))
                    for t in range(1, BLK):
                        for blk in range(2):
                            if own.n:
                                dve.wait_ge(s_dve, own.n)
                            row, before, room, _ = views(k, blk, t, 0, HV)
                            own.note(nc.vector.tensor_tensor(room, row, before, ALU.mult))
                        for blk in range(2):
                            dve.wait_ge(s_dve, own.n - 1)
                            dve.wait_ge(s_pool, 2 * ((BLK - 1) * k + t - 1) + blk + 1)
                            _, _, room, now = views(k, blk, t, 0, H)
                            own.note(nc.vector.tensor_reduce(now, room, AX.X, ALU.add, negate=True))
                    dve.wait_ge(s_dve, own.n)
                    nc.vector.sem_inc(s_done, 1)


def solve(nc, io, vscale, past):
    with ExitStack() as ctx:
        def tile(name, shape, dt=F32):
            return ctx.enter_context(nc.sbuf_tensor(name, shape, dt))

        def sem(name):
            return ctx.enter_context(nc.semaphore(name))

        LOADS = 9
        ROUNDS = NB - 1
        R1 = ROUNDS + 1
        left = tile("s_left", [3 * D, 2, 4, 2 * HQ * 128], F16)
        right = tile("s_right", [3 * D, 2, 4, 3 * HQ * 128], F16)
        val = tile("s_val", [128, 2, 2 * HD + 2 * H])
        vs = tile("s_vs", [128, 2, 2 * HD])
        v16 = tile("s_v16", [128, 2, 2, 2 * HD], F16)
        tc = tile("s_tc", [128, 2, 2, H * BLK])
        tb = tile("s_tb", [128, 2, H * BLK])
        t16 = tile("s_t16", [128, 2, 2, H * BLK], F16)
        masks = tile("s_masks", [128, 2, 128])
        own32 = tile("s_own32", [128, 128])
        own16 = tile("s_own16", [128, 128], F16)
        tx = [tile(f"s_tx{p}", [128, 2, 2, H, 128], F16) for p in range(2)]
        g32 = tile("s_g32", [128, 3, 4 * HQ * 128])
        gm = [tile(f"s_gm{p}", [128, 3, 2, 4, HQ, 128], F16) for p in range(2)]
        u16 = tile("s_u16", [128, 2, 2, 2, HD], F16)
        r32 = tile("s_r32", [128, 2, HD])
        r16 = tile("s_r16", [128, 2, 2, HD], F16)
        zo = tile("s_z", [128, 2, HQ * 128])
        pg = ctx.enter_context(nc.psum_tensor("s_gram", [128, 4, 512], F32))
        pu = ctx.enter_context(nc.psum_tensor("s_pu", [128, 2, 512], F32))
        pr = ctx.enter_context(nc.psum_tensor("s_pr", [128, 2, 512], F32))

        s_c = sem("s_const")
        s_own = sem("s_own")
        s_in = [sem(f"s_in{p}") for p in range(2)]
        s_prep = sem("s_prep")
        s_v1 = sem("s_v1")
        s_v2 = sem("s_v2")
        s_t1 = sem("s_t1")
        s_t2 = sem("s_t2")
        s_tx = sem("s_txr")
        s_pg = sem("s_pg")
        s_g32 = sem("s_g32r")
        s_g1 = sem("s_g1")
        s_g2 = sem("s_g2")
        s_pu = [sem(f"s_pu{y}") for y in range(2)]
        s_u1 = [sem(f"s_u1_{y}") for y in range(2)]
        s_u2 = [sem(f"s_u2_{y}") for y in range(2)]
        s_pr = [sem(f"s_pr{y}") for y in range(2)]
        s_r = [sem(f"s_r{y}") for y in range(2)]
        s_r1 = [sem(f"s_r1_{y}") for y in range(2)]
        s_r2 = [sem(f"s_r2_{y}") for y in range(2)]
        s_pz = sem("s_pz")
        s_z = sem("s_zr")
        s_zout = [sem(f"s_zout{p}") for p in range(2)]
        s_uout = [sem(f"s_uout{p}") for p in range(2)]

        def after(eng, sem_, v):
            if not isinstance(v, int) or v > 0:
                eng.wait_ge(sem_, v)

        def loaded(eng, n, p):
            if isinstance(n, int):
                eng.wait_ge(s_in[p], 16 * LOADS * (n // 2 + 1))
            else:
                eng.wait_ge(s_in[p], (n - p) * (8 * LOADS) + 16 * LOADS)

        def stored(eng, sems, n, p, per):
            if isinstance(n, int):
                if n >= 2:
                    eng.wait_ge(sems[p], per * (n // 2))
            else:
                eng.wait_ge(sems[p], (n - p) * (per // 2))

        with nc.Block() as block:
            @block.sync
            def _(sp):
                sp.dma_start(masks[:], io["masks"]).then_inc(s_c, 16)
                sp.dma_start(own32[:], io["own_blk"]).then_inc(s_c, 16)

                def load(n, p):
                    after(sp, s_prep, 3 * (n - 1))
                    after(sp, s_pg, 3 * (n - 1))
                    for c in range(3):
                        rows_ = slice(c * D, (c + 1) * D)
                        fl, fr = (io["feat"][j][n].rearrange("(h d) c -> d h c", d=D)
                                  for j in ((0, 0, 1)[c], (0, 1, 0)[c]))
                        sp.dma_start(left[rows_, p], fl[:, :, HD:3 * HD]).then_inc(s_in[p], 16)
                        sp.dma_start(right[rows_, p], fr).then_inc(s_in[p], 16)
                    sp.dma_start(val[:, p, :], io["val"][n]).then_inc(s_in[p], 16)
                    for y in range(2):
                        sp.dma_start(tc[:, p, y, :], io["tinv"][y][n]).then_inc(s_in[p], 16)

                def store(n, p):
                    sp.wait_ge(s_u2[1], R1 * (n + 1))
                    for b in range(2):
                        for half in range(2):
                            r0 = b * S + half * (S // 2)
                            q0 = (2 * p + b) * 32
                            sp.dma_start(past[q0:q0 + 32, :, half, bass.ds((n - p) // 2, 1), :],
                                         u16[r0:r0 + 32, p, 1, :, :].unsqueeze(2)).then_inc(s_uout[p], 16)
                    sp.wait_ge(s_z, n + 1)
                    sp.dma_start(io["z"][:, :, n, :], zo[:, p, :].rearrange("p (a b) -> p a b", a=HQ)).then_inc(
                        s_zout[p], 16)

                load(0, 0)
                load(1, 1)

                def body(n, p):
                    if not (isinstance(n, int) and n < 2):
                        load(n, p)
                        store(n - 2, p)
                over_tiles(sp, body)
                store(NT - 2, 0)
                store(NT - 1, 1)
                for p in range(2):
                    sp.wait_ge(s_uout[p], 64 * (NT // 2))
                    sp.wait_ge(s_zout[p], 16 * (NT // 2))

            @block.gpsimd
            def _(pool):
                pool.wait_ge(s_c, 32)
                nc.gpsimd.tensor_copy(own16[:], own32[:]).then_inc(s_own, 1)

                def body(n, p):
                    for y in range(2):
                        after(pool, s_r[y], ROUNDS * (n - 1))
                    loaded(pool, n, p)
                    nc.gpsimd.tensor_tensor(vs[:, p, :], val[:, p, 0:2 * HD],
                                            vscale[:, 1:2].broadcast_to([128, 2 * HD]), ALU.mult).then_inc(s_prep, 1)
                    after(pool, s_t2, n)
                    for y in range(2):
                        c3 = tc[:, p, y, :].rearrange("p (h t) -> p h t", t=BLK)
                        gates = val[:, p, 2 * HD + y * H:2 * HD + (y + 1) * H]
                        nc.gpsimd.tensor_tensor(tb[:, y, :].rearrange("p (h t) -> p h t", t=BLK), c3,
                                                bc(gates, 2, BLK), ALU.mult).then_inc(s_prep, 1)
                    pool.wait_ge(s_v1, n + 1)
                    nc.gpsimd.tensor_tensor(v16[:, p, 1, :], vs[:, p, :], v16[:, p, 0, :],
                                            ALU.subtract).then_inc(s_v2, 1)
                    for j in range(3):
                        pool.wait_ge(s_g1, 3 * n + j + 1)
                        nc.gpsimd.tensor_tensor(gm[p][:, j, 1].rearrange("p a g t -> p (a g t)"), g32[:, j, :],
                                                gm[p][:, j, 0].rearrange("p a g t -> p (a g t)"),
                                                ALU.subtract).then_inc(s_g2, 1)
                over_tiles(pool, body)

            @block.tensor
            def _(pe):
                PRODUCTS = ((0, 0), (0, 1), (1, 0))

                def gram(n, p, j):
                    lo, ro = [(0, 2), (2, 4), (0, 0)][j]
                    after(pe, s_g32, 3 * n + j)
                    for g in range(HQ):
                        for h4 in range(4):
                            last = nc.tensor.matmul(pg[:, h4, g * 128:(g + 1) * 128],
                                                    left[:, p, h4, (lo + g) * 128:(lo + g + 1) * 128],
                                                    right[:, p, h4, (ro + g) * 128:(ro + g + 1) * 128],
                                                    start=True, stop=True)
                    last.then_inc(s_pg, 1)

                def apply_t(n, p, y, k):
                    if k == 0:
                        pe.wait_ge(s_tx, 4 * n + 2 * y + 2)
                        pe.wait_ge(s_v2, n + 1)
                        after(pe, s_u2[y], R1 * n)
                    else:
                        pe.wait_ge(s_r2[y], ROUNDS * n + k)
                    for h in range(H):
                        hs = slice(h * D, (h + 1) * D)
                        for m, (a, b) in enumerate(PRODUCTS):
                            rhs = v16[:, p, b, y * HD + h * D:y * HD + (h + 1) * D] if k == 0 else r16[:, y, b, hs]
                            last = nc.tensor.matmul(pu[:, y, hs], tx[p][:, y, a, h, :], rhs, start=(m == 0),
                                                    stop=(m == 2))
                    last.then_inc(s_pu[y], 1)

                def apply_g(n, p, y, k):
                    if k == 0:
                        pe.wait_ge(s_g2, 3 * n + y + 1)
                        if y == 0:
                            after(pe, s_z, n)
                    pe.wait_ge(s_u2[y], R1 * n + k + 1)
                    for h in range(H):
                        hs = slice(h * D, (h + 1) * D)
                        for m, (a, b) in enumerate(PRODUCTS):
                            last = nc.tensor.matmul(pr[:, y, hs], gm[p][:, y, a, h % 4, h // 4, :],
                                                    u16[:, p, y, b, hs], start=(m == 0), stop=(m == 2))
                    last.then_inc(s_pr[y], 1)

                def z_of(n, p):
                    pe.wait_ge(s_g2, 3 * n + 3)
                    pe.wait_ge(s_u2[0], R1 * (n + 1))
                    for h in range(H):
                        q = 32 * (h % 4)
                        c = (h // 4) * 128
                        for m, (a, b) in enumerate(PRODUCTS):
                            last = nc.tensor.matmul(pr[q:q + 32, 0, c:c + 128], u16[:, p, 0, a, h * D:(h + 1) * D],
                                                    gm[p][:, 2, b, h % 4, h // 4, :], start=(m == 0), stop=(m == 2))
                    last.then_inc(s_pz, 1)

                loaded(pe, 0, 0)
                for j in range(3):
                    gram(0, 0, j)

                def body(n, p):
                    ends = isinstance(n, int) and n == NT - 1
                    if not ends:
                        loaded(pe, n + 1, 1 - p)
                    for y in range(2):
                        apply_t(n, p, y, 0)
                    for k in range(ROUNDS):
                        for y in range(2):
                            apply_g(n, p, y, k)
                        if not ends:
                            gram(n + 1, 1 - p, k)
                        for y in range(2):
                            apply_t(n, p, y, k + 1)
                    z_of(n, p)

                over_tiles(pe, body)

            @block.scalar
            def _(act):
                def gram_high(n, p, j):
                    act.wait_ge(s_g32, 3 * n + j + 1)
                    nc.scalar.copy(gm[p][:, j, 0].rearrange("p a g t -> p (a g t)"),
                                   g32[:, j, :]).then_inc(s_g1, 1)

                def splits(n, p):
                    act.wait_ge(s_prep, 3 * n + 1)
                    nc.scalar.copy(v16[:, p, 0, :], vs[:, p, :]).then_inc(s_v1, 1)
                    act.wait_ge(s_prep, 3 * n + 3)
                    after(act, s_tx, 4 * n)
                    nc.scalar.mul(t16[:, 0], tb[:], UNIT).then_inc(s_t1, 1)

                splits(0, 0)
                for j in range(3):
                    gram_high(0, 0, j)

                def body(n, p):
                    ends = isinstance(n, int) and n == NT - 1
                    for k in range(R1):
                        for y in range(2):
                            act.wait_ge(s_pu[y], R1 * n + k + 1)
                            if k == 0 and y == 0:
                                stored(act, s_uout, n, p, 64)
                            nc.scalar.mul(u16[:, p, y, 0, :], pu[:, y, 0:HD], 1.0 / UNIT).then_inc(s_u1[y], 1)
                        if not ends:
                            if k == 0:
                                splits(n + 1, 1 - p)
                            else:
                                gram_high(n + 1, 1 - p, k - 1)
                        if k < ROUNDS:
                            for y in range(2):
                                act.wait_ge(s_r[y], ROUNDS * n + k + 1)
                                nc.scalar.copy(r16[:, y, 0, :], r32[:, y, :]).then_inc(s_r1[y], 1)
                    act.wait_ge(s_pz, n + 1)
                    stored(act, s_zout, n, p, 16)
                    nc.scalar.mul(zo[:, p, :], pr[:, 0, 0:HQ * 128], vscale[:, 2:3]).then_inc(s_z, 1)
                over_tiles(act, body)

            @block.vector
            def _(dve):
                dve.wait_ge(s_c, 32)
                dve.wait_ge(s_own, 1)

                def mask(n, p, j):
                    dve.wait_ge(s_pg, 3 * n + j + 1)
                    after(dve, s_g1, 3 * (n - 1) + j + 1)
                    after(dve, s_g2, 3 * (n - 1) + j + 1)
                    m = masks[:, 1 if j == 2 else 0, :]
                    nc.vector.tensor_tensor(g32[:, j, :].rearrange("p (a g t) -> p a g t", a=4, g=HQ),
                                            pg[:, :, 0:HQ * 128].rearrange("p a (g t) -> p a g t", g=HQ),
                                            bc(bc(m, 1, HQ), 1, 4), ALU.mult).then_inc(s_g32, 1)

                def u_low(n, p, y, k):
                    dve.wait_ge(s_u1[y], R1 * n + k + 1)
                    nc.vector.scalar_tensor_tensor(out=u16[:, p, y, 1, :], in0=pu[:, y, 0:HD], scalar=1.0 / UNIT,
                                                   in1=u16[:, p, y, 0, :], op0=ALU.mult,
                                                   op1=ALU.subtract).then_inc(s_u2[y], 1)

                def residual(n, p, y, k):
                    dve.wait_ge(s_pr[y], ROUNDS * n + k + 1)
                    nc.vector.scalar_tensor_tensor(out=r32[:, y, :], in0=pr[:, y, 0:HD], scalar=-1.0 / UNIT,
                                                   in1=vs[:, p, y * HD:(y + 1) * HD], op0=ALU.mult,
                                                   op1=ALU.add).then_inc(s_r[y], 1)

                def r_low(n, p, y, k):
                    dve.wait_ge(s_r1[y], ROUNDS * n + k + 1)
                    nc.vector.tensor_tensor(r16[:, y, 1, :], r32[:, y, :], r16[:, y, 0, :],
                                            ALU.subtract).then_inc(s_r2[y], 1)

                def t_low(n, p):
                    dve.wait_ge(s_t1, n + 1)
                    nc.vector.scalar_tensor_tensor(out=t16[:, 1].rearrange("p y c -> p (y c)"),
                                                   in0=tb[:].rearrange("p y c -> p (y c)"), scalar=UNIT,
                                                   in1=t16[:, 0].rearrange("p y c -> p (y c)"), op0=ALU.mult,
                                                   op1=ALU.subtract).then_inc(s_t2, 1)

                def expand(n, p, y, j):
                    dve.wait_ge(s_t2, n + 1)
                    c3 = t16[:, j, y, :].rearrange("p (h t) -> p h t", t=BLK)
                    o3 = own16[:].rearrange("p (k t) -> p k t", t=BLK)
                    nc.vector.tensor_tensor(tx[p][:, y, j].rearrange("p h (k t) -> p h k t", t=BLK),
                                            bc(c3, 2, 8), bc(o3, 1, H), ALU.mult).then_inc(s_tx, 1)

                t_low(0, 0)
                for y in range(2):
                    for j in range(2):
                        expand(0, 0, y, j)
                for j in range(3):
                    mask(0, 0, j)

                def body(n, p):
                    ends = isinstance(n, int) and n == NT - 1
                    for y in range(2):
                        u_low(n, p, y, 0)
                    for k in range(ROUNDS):
                        for y in range(2):
                            residual(n, p, y, k)
                        for y in range(2):
                            r_low(n, p, y, k)
                        if not ends:
                            mask(n + 1, 1 - p, k)
                        for y in range(2):
                            u_low(n, p, y, k + 1)
                        if not ends:
                            if k == 0:
                                t_low(n + 1, 1 - p)
                            else:
                                expand(n + 1, 1 - p, 0, k - 1)
                    if not ends:
                        for j in range(2):
                            expand(n + 1, 1 - p, 1, j)
                over_tiles(dve, body)


def recur(nc, io, hs, rk16, vscale, past):
    STREAMS = [(0, 48), (48, B - 48)]
    W = 96
    HALF = S // 2
    with ExitStack() as ctx:
        def tile(name, shape, dt=F32):
            return ctx.enter_context(nc.sbuf_tensor(name, shape, dt))

        def sem(name):
            return ctx.enter_context(nc.semaphore(name))

        def sems(name):
            return [sem(f"r_{name}{i}") for i in range(2)]

        see = tile("r_see", [128, HALF, 16])
        q = [tile(f"r_q{i}", [128, W, 4, 2], F16) for i in range(2)]
        a32 = [tile(f"r_a32{i}", [128, 2, W * 4]) for i in range(2)]
        am = [[tile(f"r_am{i}{j}", [128, 2, W * 4], F16) for j in range(2)] for i in range(2)]
        hc = [tile(f"r_h{i}", [128, W]) for i in range(2)]
        ht = [tile(f"r_ht{i}", [128, 3, D]) for i in range(2)]
        et = [tile(f"r_et{i}", [128, 3, D]) for i in range(2)]
        nrm = [tile(f"r_nrm{i}", [128, 3, D]) for i in range(2)]
        e16 = [tile(f"r_e{i}", [128, 3 * D, 2], F16) for i in range(2)]
        st = [tile(f"r_st{i}", [128, 3, 3]) for i in range(2)]
        pa = [ctx.enter_context(nc.psum_tensor(f"r_pa{i}", [128, 2, 512], F32)) for i in range(2)]
        ph = [ctx.enter_context(nc.psum_tensor(f"r_ph{i}", [128, 512], F32)) for i in range(2)]

        s_see, s_q0 = (sem(f"r_in_{k}") for k in ("see", "q0"))
        s_z = sems("in_z")
        s_q = sems("q")
        s_a = sems("a")
        s_a32 = sems("a32")
        s_am1 = sems("am1")
        s_am = sems("am")
        s_rq = sems("rq")
        s_h = sems("h")
        s_hs = sems("hs")
        s_ht = sems("ht")
        s_mx = sems("mx")
        s_exp = sems("exp")
        s_rec = sems("rec")
        s_nrm = sems("nrm")
        s_n1 = sems("n1")
        s_n2 = sems("n2")

        with nc.Block() as block:
            @block.sync
            def _(sp):
                sp.dma_start(see[:], io["see4"]).then_inc(s_see, 16)
                for i, (b0, nb) in enumerate(STREAMS):
                    sp.dma_start(hs[:, :, b0:b0 + nb, :].rearrange("p g b s -> p g (b s)"),
                                 io["z"][:, :, b0 // 2:(b0 + nb) // 2, :].rearrange("p g n c -> p g (n c)")).then_inc(
                                     s_z[i], 16)

            @block.tensor
            def _(pe):
                PRODUCTS = ((0, 0), (0, 1), (1, 0))

                def step(t, halves):
                    for i, (b0, nb) in enumerate(STREAMS):
                        pe.wait_ge(s_q[i], t + 1)
                        for half in range(halves):
                            for g in range(HQ):
                                for b in range(0, nb, 4):
                                    c = g * nb + b
                                    rows_ = slice((b0 + b) * HALF, (b0 + b + 4) * HALF)
                                    for m, (x, y) in enumerate(PRODUCTS):
                                        last = nc.tensor.matmul(pa[i][:, half, 4 * c:4 * c + 16],
                                                                rk16[x][:, g, half, rows_], q[i][:, c:c + 4, :, y],
                                                                start=(m == 0), stop=(m == 2))
                            last.then_inc(s_a[i], 1)
                    for i, (b0, nb) in enumerate(STREAMS):
                        pe.wait_ge(s_am[i], t + 1 if halves == 1 else 2 * t + 2 - HALF)
                        for g in range(HQ):
                            for b in range(0, nb, 4):
                                c = g * nb + b
                                for half in range(halves):
                                    for m, (x, y) in enumerate(PRODUCTS):
                                        last = nc.tensor.matmul(ph[i][:, 4 * c:4 * c + 16],
                                                                past[:, x, half, (b0 + b) // 4, g * 128:(g + 1) * 128],
                                                                am[i][y][:, half, 4 * c:4 * c + 16],
                                                                start=(half == 0 and m == 0),
                                                                stop=(half == halves - 1 and m == 2))
                        last.then_inc(s_rq[i], 1)

                with pe.Fori(0, HALF) as t:
                    step(t, 1)
                with pe.Fori(HALF, S) as t:
                    step(t, 2)

            @block.scalar
            def _(act):
                def step(t, halves):
                    for i, (b0, nb) in enumerate(STREAMS):
                        cols = slice(0, 4 * HQ * nb)
                        for half in range(halves):
                            act.wait_ge(s_a32[i], t + 1 if halves == 1 else 2 * t + 1 + half - HALF)
                            nc.scalar.copy(am[i][0][:, half, cols], a32[i][:, half, cols]).then_inc(s_am1[i], 1)
                    for i in range(2):
                        act.wait_ge(s_mx[i], t + 1)
                        for k in range(3):
                            nc.scalar.activation(et[i][:, k], ht[i][:, k], ACT.Exp, bias=st[i][:, k, 0:1],
                                                 accum_out=st[i][:, k, 1:2]).then_inc(s_exp[i], 1)

                with act.Fori(0, HALF) as t:
                    step(t, 1)
                with act.Fori(HALF, S) as t:
                    step(t, 2)

            @block.gpsimd
            def _(pool):
                for i, (b0, nb) in enumerate(STREAMS):
                    nc.gpsimd.memset(hc[i][:], 0.0).then_inc(s_hs[i], 1)
                    nc.gpsimd.memset(q[i][:], 0.0).then_inc(s_q0, 1)
                pool.wait_ge(s_q0, 2)
                for i in range(2):
                    for h4 in range(4):
                        last = nc.gpsimd.memset(q[i][32 * h4:32 * h4 + 32, :, h4, 0], UNIT / D)
                    last.then_inc(s_q[i], 1)
                with pool.Fori(0, S) as t:
                    for i, (b0, nb) in enumerate(STREAMS):
                        pool.wait_ge(s_h[i], t + 1)
                        nc.gpsimd.tensor_copy(hs[:, :, b0:b0 + nb, t],
                                              hc[i][:, 0:HQ * nb].rearrange("p (g b) -> p g b", g=HQ)).then_inc(
                                                  s_hs[i], 1)

            @block.vector
            def _(dve):
                def mask(t, i, half, halves):
                    b0, nb = STREAMS[i]
                    dve.wait_ge(s_a[i], t + 1 if halves == 1 else 2 * t + 1 + half - HALF)
                    k = HQ * nb // 4
                    now = see[:, t, :] if halves == 1 else see[:, t - HALF, :] if half else see[:, HALF - 1, :]
                    nc.vector.tensor_tensor(
                        a32[i][:, half, 0:4 * HQ * nb].rearrange("p (k w) -> p k w", k=k),
                        pa[i][:, half, 0:4 * HQ * nb].rearrange("p (k w) -> p k w", k=k),
                        bc(now, 1, k), ALU.mult).then_inc(s_a32[i], 1)

                def mask_low(t, i, half, halves):
                    cols = slice(0, 4 * HQ * STREAMS[i][1])
                    dve.wait_ge(s_am1[i], t + 1 if halves == 1 else 2 * t + 1 + half - HALF)
                    nc.vector.tensor_tensor(am[i][1][:, half, cols], a32[i][:, half, cols], am[i][0][:, half, cols],
                                            ALU.subtract).then_inc(s_am[i], 1)

                def softmax(t, i):
                    b0, nb = STREAMS[i]
                    dve.wait_ge(s_z[i], 16)
                    dve.wait_ge(s_rq[i], t + 1)
                    dve.wait_ge(s_hs[i], t + 1)
                    for h4 in range(4):
                        r = slice(32 * h4, 32 * h4 + 32)
                        last = nc.vector.scalar_tensor_tensor(
                            out=hc[i][r, 0:HQ * nb].rearrange("p (g b) -> p g b", g=HQ),
                            in0=ph[i][r, 0:4 * HQ * nb].rearrange("p (g b h) -> p g b h", g=HQ, h=4)[:, :, :, h4],
                            scalar=vscale[r, 2:3], in1=hs[r, :, b0:b0 + nb, t], op0=ALU.mult, op1=ALU.add)
                    last.then_inc(s_h[i], 1)
                    dve.wait_ge(s_h[i], t + 1)
                    nc.vector.transpose(ht[i][:].rearrange("p k d -> p (k d)"), hc[i][:]).then_inc(s_ht[i], 1)
                    dve.wait_ge(s_ht[i], t + 1)
                    nc.vector.tensor_reduce(st[i][:, :, 0], ht[i][:], AX.X, ALU.max, negate=True).then_inc(s_mx[i], 1)

                def spread(t, i):
                    dve.wait_ge(s_exp[i], 3 * t + 3)
                    nc.vector.reciprocal(st[i][:, :, 2], st[i][:, :, 1]).then_inc(s_rec[i], 1)
                    dve.wait_ge(s_rec[i], t + 1)
                    parts = e16[i][:].rearrange("p (k d) j -> p k d j", d=D)
                    inv = bc(st[i][:, :, 2], 2, D)
                    nc.vector.scalar_tensor_tensor(out=parts[:, :, :, 0], in0=et[i][:], scalar=UNIT, in1=inv,
                                                   op0=ALU.mult, op1=ALU.mult).then_inc(s_n1[i], 1)
                    nc.vector.scalar_tensor_tensor(out=nrm[i][:], in0=et[i][:], scalar=UNIT, in1=inv, op0=ALU.mult,
                                                   op1=ALU.mult).then_inc(s_nrm[i], 1)
                    dve.wait_ge(s_n1[i], t + 1)
                    dve.wait_ge(s_nrm[i], t + 1)
                    nc.vector.tensor_tensor(parts[:, :, :, 1], nrm[i][:], parts[:, :, :, 0],
                                            ALU.subtract).then_inc(s_n2[i], 1)
                    dve.wait_ge(s_n2[i], t + 1)
                    both = e16[i][:].rearrange("p k j -> p (k j)").bitcast(I32)
                    q32 = q[i][:].rearrange("p w h j -> p (w h j)").bitcast(I32).rearrange("p (w h) -> p w h", h=4)
                    for h4 in range(4):
                        r = slice(32 * h4, 32 * h4 + 32)
                        last = nc.vector.transpose(q32[r, :, h4], both[r])
                    last.then_inc(s_q[i], 1)

                def step(t, halves):
                    for i in range(2):
                        for half in range(halves):
                            mask(t, i, half, halves)
                        for half in range(halves):
                            mask_low(t, i, half, halves)
                    for i in range(2):
                        softmax(t, i)
                        if halves == 2:
                            spread(t, i)
                    if halves == 1:
                        for i in range(2):
                            spread(t, i)

                dve.wait_ge(s_see, 16)
                with dve.Fori(0, HALF) as t:
                    step(t, 1)
                with dve.Fori(HALF, S) as t:
                    step(t, 2)


def ffn(nc, io, sb, res, hs, past):
    NSCALE = 2.0 ** 10
    WTOP = 2.0 ** 13
    HTOP = 2.0 ** 14
    with ExitStack() as ctx:
        def tile(name, shape, dt=F32):
            return ctx.enter_context(nc.sbuf_tensor(name, shape, dt))

        def sem(name):
            return ctx.enter_context(nc.semaphore(name))

        ident, rows = sb["ident"], sb["rows"]
        n1 = tile("n1", [128, NT, DM])
        sq = tile("n1_sq", [128, NT, DM])
        room = past[:].rearrange("p j a k c -> p (j a k c)")
        n16 = room[:, 0:NT * 128].rearrange("p (n j d) -> p n j d", j=2, d=DM)
        nT = room[:, NT * 128:2 * NT * 128]
        ident16 = tile("ident16", [128, 128], F16)
        outw = tile("out_w", [128, HQ, DM])
        wr = tile("wr", [128, E])
        w1 = tile("w1", [128, FC, 128])
        b1 = tile("b1", [128, FC])
        w2 = tile("w2", [128, FC, DM])
        b2p = tile("b2p", [128, E, DM])
        earlier = tile("earlier", [128, E, E])
        stat = tile("f_stat", [128, 4, NT])
        mhalf = tile("f_mhalf", [128, NT])
        rw = tile("f_rw", [128, NT, E])
        wts = tile("f_wts", [128, NT, E])
        wr16 = tile("wr16", [128, 2, E], F16)
        w116 = [tile(f"w1_16_{j}", [128, FC, 128], F16) for j in range(2)]
        w216 = [room[:, (2 * NT + 4 * FC) * 128 + j * FC * DM:(2 * NT + 4 * FC) * 128 + (j + 1) * FC * DM].rearrange(
            "p (c d) -> p c d", c=FC) for j in range(2)]
        top = tile("f_top", [128, 4])
        scl = tile("f_scale", [128, 3])
        hid = tile("f_hid", [128, 2])
        back = tile("f_back", [128, 3])

        s_c = sem("p_const")
        s_o = sem("p_out")
        s_cen, s_sq, s_var, s_half, s_rstd = (sem(f"p_{k}") for k in ("cen", "sq", "var", "half", "rstd"))
        s_tr, s_ev = sem("p_tr"), sem("p_ev")
        s_log, s_sub, s_exp = sem("p_log"), sem("p_sub"), sem("p_exp")
        s_dve = sem("p_dve")
        s_top, s_all = sem("p_top"), sem("p_all")
        s_w = sem("p_w16")
        s_n16 = sem("p_n16")

        with ExitStack() as inner:
            def psum(name, shape):
                return inner.enter_context(nc.psum_tensor(name, shape, F32))

            oP = psum("p_oP", [128, 6 * 512])
            tP = inner.enter_context(nc.psum_tensor("p_tP", [128, 2, 1024], F16))
            gt, ge = (hs[:, k].rearrange("p b s -> p (b s)")[:, 0:NT * E * E].rearrange("p (n e o) -> p n e o",
                                                                                        e=E, o=E) for k in range(2))
            PARTS = [(0, 24), (24, NT)]
            LOADS = 16 * 9
            with nc.Block() as block:
                @block.sync
                def _(sp):
                    for dst, name in ((outw, "out_w"), (b1, "b1"), (w2, "w2"), (b2p, "b2p"), (earlier, "earlier")):
                        sp.dma_start(dst[:], io[name]).then_inc(s_c, 16)
                    for j in range(2):
                        for dst, name in ((wr, "wr"), (w1, "w1")):
                            sp.dma_start(dst[j * DM:(j + 1) * DM], io[name]).then_inc(s_c, 16)
                    sp.wait_ge(s_c, LOADS)

                @block.tensor
                def _(pe):
                    pe.wait_ge(s_c, LOADS)
                    for a, b in PARTS:
                        for n in range(a, b):
                            for g in range(HQ):
                                last = nc.tensor.matmul(oP[:, n * DM:(n + 1) * DM], hs[:, g, 2 * n:2 * n + 2, :],
                                                        outw[:, g, :], start=(g == 0), stop=(g == HQ - 1))
                        last.then_inc(s_o, 1)
                    for k in range((NT + 7) // 8):
                        pe.wait_ge(s_n16, 1 if 8 * k + 8 <= PARTS[0][1] else 2)
                        if k >= 2:
                            pe.wait_ge(s_ev, k - 1)
                        for j in range(min(8, NT - 8 * k)):
                            last = nc.tensor.transpose(tP[:, k % 2, j * 128:(j + 1) * 128],
                                                       n16[:, 8 * k + j].rearrange("p j d -> p (j d)"), ident16[:])
                        last.then_inc(s_tr, 1)
                    pe.wait_ge(s_w, 1)
                    for n in range(NT):
                        if n % 8 == 0:
                            pe.wait_ge(s_ev, n // 8 + 1)
                        for j in range(2):
                            last = nc.tensor.matmul(oP[:, n * E:(n + 1) * E], nT[:, n * 128:(n + 1) * 128],
                                                    wr16[:, j, :], start=(j == 0), stop=(j == 1))
                    last.then_inc(s_log, 1)

                @block.scalar
                def _(act):
                    for p, (a, b) in enumerate(PARTS):
                        act.wait_ge(s_cen, p + 1)
                        nc.scalar.activation(sq[:, a:b, :], n1[:, a:b, :], ACT.Square).then_inc(s_sq, 1)
                    for k in range((NT + 7) // 8):
                        w = min(8, NT - 8 * k) * 128
                        act.wait_ge(s_tr, k + 1)
                        nc.scalar.copy(nT[:, k * 1024:k * 1024 + w], tP[:, k % 2, 0:w]).then_inc(s_ev, 1)
                    act.wait_ge(s_sub, 1)
                    nc.scalar.activation(rw[:], rw[:], ACT.Exp, scale=back[:, 2:3]).then_inc(s_exp, 1)

                @block.gpsimd
                def _(pool):
                    nc.gpsimd.memset(mhalf[:], -0.5).then_inc(s_half, 1)
                    pool.wait_ge(s_half, 1)
                    pool.wait_ge(s_top, 1)
                    nc.gpsimd.partition_all_reduce(top[:], top[:], 128, RMAX).then_inc(s_all, 1)
                    for p, (a, b) in enumerate(PARTS):
                        pool.wait_ge(s_var, p + 1)
                        nc.gpsimd.tensor_tensor(stat[:, 3, a:b], stat[:, 2, a:b], mhalf[:, a:b],
                                                ALU.pow).then_inc(s_rstd, 1)

                @block.vector
                def _(dve):
                    own = Chain(s_dve)

                    def then(ins):
                        own.note(ins)
                        dve.wait_ge(s_dve, own.n)

                    dve.wait_ge(s_c, LOADS)
                    for k, x in enumerate((w1[:].rearrange("p c f -> p (c f)"), w2[:].rearrange("p c f -> p (c f)"),
                                           wr[:], b1[:])):
                        last = own.note(nc.vector.tensor_reduce(top[:, k:k + 1], x, AX.X, ALU.max,
                                                                apply_absolute_value=True))
                    dve.wait_ge(s_dve, own.n)
                    nc.vector.sem_inc(s_top, 1)
                    then(nc.vector.tensor_copy(ident16[:], ident[:]))
                    dve.wait_ge(s_all, 1)
                    then(nc.vector.tensor_scalar(top[:, 0:3], top[:, 0:3], 1e-30, None, ALU.max))
                    then(nc.vector.reciprocal(scl[:], top[:, 0:3]))
                    then(nc.vector.tensor_scalar(scl[:], scl[:], WTOP, None, ALU.mult))
                    then(nc.vector.scalar_tensor_tensor(out=hid[:, 0:1], in0=top[:, 0:1], scalar=float(DM),
                                                        in1=top[:, 3:4], op0=ALU.mult, op1=ALU.add))
                    then(nc.vector.reciprocal(hid[:, 1:2], hid[:, 0:1]))
                    then(nc.vector.tensor_scalar(hid[:, 1:2], hid[:, 1:2], HTOP, None, ALU.mult))
                    then(nc.vector.tensor_scalar(back[:], top[:, 0:3], 1.0 / WTOP / NSCALE, None, ALU.mult))
                    then(nc.vector.scalar_tensor_tensor(out=back[:, 1:2], in0=back[:, 1:2], scalar=NSCALE / HTOP,
                                                        in1=hid[:, 0:1], op0=ALU.mult, op1=ALU.mult))
                    for k, x, parts in ((2, wr[:], (wr16[:, 0], wr16[:, 1])), (0, w1[:], (w116[0][:], w116[1][:])),
                                        (1, w2[:], (w216[0], w216[1]))):
                        then(nc.vector.tensor_scalar(parts[0], x, scl[:, k:k + 1], None, ALU.mult))
                        then(nc.vector.scalar_tensor_tensor(out=parts[1], in0=x, scalar=scl[:, k:k + 1],
                                                            in1=parts[0], op0=ALU.mult, op1=ALU.subtract))
                    nc.vector.sem_inc(s_w, 1)
                    for p, (a, b) in enumerate(PARTS):
                        dve.wait_ge(s_o, p + 1)
                        ov = oP[:, a * DM:b * DM].rearrange("p (n d) -> p n d", d=DM)
                        then(nc.vector.tensor_tensor(res[:, a:b, :], res[:, a:b, :], ov, ALU.add))
                        then(nc.vector.tensor_reduce(stat[:, 0, a:b], res[:, a:b, :], AX.X, ALU.add))
                        then(nc.vector.tensor_scalar(stat[:, 1, a:b], stat[:, 0, a:b], -1.0 / DM, None, ALU.mult))
                        nc.vector.tensor_tensor(n1[:, a:b, :], res[:, a:b, :], bc(stat[:, 1, a:b], 2, DM),
                                                ALU.add).then_inc(s_cen, 1)
                    for p, (a, b) in enumerate(PARTS):
                        dve.wait_ge(s_sq, p + 1)
                        then(nc.vector.tensor_reduce(stat[:, 0, a:b], sq[:, a:b, :], AX.X, ALU.add))
                        nc.vector.tensor_scalar(stat[:, 2, a:b], stat[:, 0, a:b], 1.0 / DM, EPS, ALU.mult,
                                                ALU.add).then_inc(s_var, 1)
                    for p, (a, b) in enumerate(PARTS):
                        dve.wait_ge(s_rstd, p + 1)
                        then(nc.vector.tensor_tensor(n1[:, a:b, :], n1[:, a:b, :], bc(stat[:, 3, a:b], 2, DM),
                                                     ALU.mult))
                        then(nc.vector.tensor_scalar(n16[:, a:b, 0, :], n1[:, a:b, :], NSCALE, None, ALU.mult))
                        nc.vector.scalar_tensor_tensor(out=n16[:, a:b, 1, :], in0=n1[:, a:b, :], scalar=NSCALE,
                                                       in1=n16[:, a:b, 0, :], op0=ALU.mult,
                                                       op1=ALU.subtract).then_inc(s_n16, 1)
                    then(nc.vector.tensor_tensor(res[:], res[:], bc(rows[:, 5, :], 1, NT), ALU.add))
                    dve.wait_ge(s_log, 1)
                    lg = oP[:, 0:NT * E].rearrange("p (n e) -> p n e", e=E)
                    then(nc.vector.tensor_reduce(stat[:, 0, :], lg, AX.X, ALU.max))
                    nc.vector.tensor_tensor(rw[:], lg, bc(stat[:, 0, :], 2, E), ALU.subtract).then_inc(s_sub, 1)
                    dve.wait_ge(s_exp, 1)
                    then(nc.vector.tensor_reduce(stat[:, 0, :], rw[:], AX.X, ALU.add))
                    then(nc.vector.reciprocal(stat[:, 1, :], stat[:, 0, :]))
                    then(nc.vector.tensor_tensor(rw[:], rw[:], bc(stat[:, 1, :], 2, E), ALU.mult))
                    mine, other = bc(rw[:], 3, E), bc(rw[:], 2, E)
                    own.note(nc.vector.tensor_tensor(gt, other, mine, ALU.is_gt))
                    then(nc.vector.tensor_tensor(ge, other, mine, ALU.is_ge))
                    then(nc.vector.tensor_tensor(ge, ge, gt, ALU.subtract))
                    then(nc.vector.tensor_tensor(ge, ge, bc(earlier[:], 1, NT), ALU.mult))
                    then(nc.vector.tensor_tensor(ge, ge, gt, ALU.add))
                    then(nc.vector.tensor_reduce(wts[:], ge, AX.X, ALU.add))
                    then(nc.vector.scalar_tensor_tensor(out=wts[:], in0=wts[:], scalar=1.5, in1=rw[:],
                                                        op0=ALU.is_lt, op1=ALU.mult))
                    then(nc.vector.tensor_reduce(stat[:, 0, :], wts[:], AX.X, ALU.add))
                    then(nc.vector.reciprocal(stat[:, 1, :], stat[:, 0, :]))
                    then(nc.vector.tensor_tensor(wts[:], wts[:], bc(stat[:, 1, :], 2, E), ALU.mult))

        NG = NT // 2
        NBUF = FC
        LAG = 8
        hg = hs[:, 0].rearrange("p b s -> p (b s)")[:, 0:NBUF * 256].rearrange("p (c n) -> p c n", c=NBUF)
        t1 = hs[:, 1].rearrange("p b s -> p (b s)")[:, 0:2 * E * DM].rearrange("p (a e d) -> p a e d", a=2, e=E)
        h16 = [room[:, 2 * NT * 128 + j * NBUF * 256:2 * NT * 128 + (j + 1) * NBUF * 256].rearrange(
            "p (c n) -> p c n", c=NBUF) for j in range(2)]
        ng = tile("n1_group", [128, 2, 256], F16)
        acc = tile("routed", [128, 2, DM])
        fin = tile("final", [128, 2, 2, DM])
        pH = ctx.enter_context(nc.psum_tensor("g_hid", [128, 2, 512], F32))
        pE = [ctx.enter_context(nc.psum_tensor(f"g_exp{i}", [128, 2, 512], F32)) for i in range(2)]
        pS = [ctx.enter_context(nc.psum_tensor(f"g_sh{i}", [128, 512], F32)) for i in range(2)]
        s_ng = sem("g_ng")
        s_hid = sem("g_hid")
        s_act = sem("g_act")
        s_h1 = [sem(f"g_h1_{k}") for k in range(2)]
        s_h2 = sem("g_h2")
        s_down = sem("g_down")
        s_b = sem("g_bias")
        s_wt = sem("g_weighted")
        s_r = sem("g_routed")
        s_s = sem("g_shared")
        s_f = sem("g_final")
        s_st = [sem(f"g_store{i}") for i in range(2)]

        POOL, SCALAR = range(2)
        NPAIR = FC // 2
        maker = [(POOL, POOL, SCALAR)[k % 3] for k in range(NPAIR)]

        def high_done(j, k):
            return s_h1[maker[k]], maker.count(maker[k]) * j + maker[:k + 1].count(maker[k])

        def high(engine, j, k):
            after(engine, s_down, FC * (j - 1) + 2 * k + 2)
            out, src = h16[0][:, 2 * k:2 * k + 2, :], hg[:, 2 * k:2 * k + 2, :]
            engine.wait_ge(s_act, FC * j + 2 * k + 2)
            if maker[k] == POOL:
                ins = nc.gpsimd.tensor_tensor(out, src, bc(hid[:, 1:2].broadcast_to([128, 256]), 1, 2), ALU.mult)
            else:
                ins = nc.scalar.activation(out, src, ACT.Copy, scale=hid[:, 1:2])
            ins.then_inc(s_h1[maker[k]], 1)

        def over_groups(engine, body):
            body(0, 0)
            body(1, 1)
            with engine.Fori(1, NG // 2) as pair:
                body(2 * pair, 0)
                body(2 * pair + 1, 1)
            body(NG - 1, 0)

        def after(eng, sem_, v):
            if not isinstance(v, int) or v > 0:
                eng.wait_ge(sem_, v)

        with nc.Block() as block:
            @block.tensor
            def _(pe):
                def down(j, p, c):
                    if c == 0:
                        after(pe, s_f, j - 1)
                    pe.wait_ge(s_h2, NPAIR * j + c // 2 + 1)
                    for a in range(2):
                        if c < 2 * E:
                            dst = pE[p][:, a, (c // 2) * DM:(c // 2 + 1) * DM]
                        else:
                            dst = pS[p][:, a * DM:(a + 1) * DM]
                        first = c % 2 == 0 and (c < 2 * E or a == 0)
                        for m, (x, y) in enumerate(((0, 0), (0, 1), (1, 0))):
                            last = nc.tensor.matmul(dst, h16[x][:, c % NBUF, a * 128:(a + 1) * 128], w216[y][:, c, :],
                                                    start=first and m == 0, stop=(c % 2 == 1 and m == 2),
                                                    skip_group_check=c >= 2 * E)
                    last.then_inc(s_down, 1)

                def body(j, p):
                    pe.wait_ge(s_ng, j + 1)
                    for c in range(FC):
                        after(pe, s_act, FC * j + c - 1)
                        for m in range(2):
                            last = nc.tensor.matmul(pH[:, c % 2, 0:256], w116[m][:, c, :], ng[:, p, :], start=(m == 0),
                                                    stop=(m == 1))
                        last.then_inc(s_hid, 1)
                        if c >= LAG:
                            down(j, p, c - LAG)
                        elif not (isinstance(j, int) and j == 0):
                            down(j - 1, 1 - p, FC + c - LAG)
                over_groups(pe, body)
                for c in range(LAG):
                    down(NG - 1, (NG - 1) % 2, FC + c - LAG)

            @block.gpsimd
            def _(pool):
                def weigh(j, a):
                    pool.wait_ge(s_b, 2 * j + a + 1)
                    nc.gpsimd.tensor_tensor(t1[:, a], t1[:, a], bc(wts[:, 2 * j + a, :], 2, DM),
                                            ALU.mult).then_inc(s_wt, 1)

                def body(j, p):
                    for k in range(NPAIR):
                        if maker[k] == POOL:
                            high(pool, j, k)
                        if k >= NPAIR - 2 and not (isinstance(j, int) and j == 0):
                            weigh(j - 1, k - (NPAIR - 2))
                        if k == 3 and not (isinstance(j, int) and j == NG - 1):
                            after(pool, s_hid, FC * j)
                            nc.gpsimd.tensor_copy(ng[:, 1 - p, :], nT[:, bass.ts(j + 1, 256)]).then_inc(s_ng, 1)
                nc.gpsimd.tensor_copy(ng[:, 0, :], nT[:, bass.ts(0, 256)]).then_inc(s_ng, 1)
                over_groups(pool, body)
                for a in range(2):
                    weigh(NG - 1, a)

            @block.scalar
            def _(act):
                def body(j, p):
                    for c in range(FC):
                        if c % 2 == 0:
                            after(act, s_h2, NPAIR * (j - 1) + c // 2 + 1)
                        act.wait_ge(s_hid, FC * j + c + 1)
                        nc.scalar.activation(hg[:, c % NBUF, :], pH[:, c % 2, 0:256], ACT.Gelu, bias=b1[:, c:c + 1],
                                             scale=back[:, 0:1]).then_inc(s_act, 1)
                        if c % 2 == 0 and c and maker[c // 2 - 1] == SCALAR:
                            high(act, j, c // 2 - 1)
                    if maker[NPAIR - 1] == SCALAR:
                        high(act, j, NPAIR - 1)
                over_groups(act, body)

            @block.vector
            def _(dve):
                def low(j, k):
                    dve.wait_ge(*high_done(j, k))
                    pair = slice(2 * k, 2 * k + 2)
                    nc.vector.scalar_tensor_tensor(out=h16[1][:, pair, :], in0=hg[:, pair, :], scalar=hid[:, 1:2],
                                                   in1=h16[0][:, pair, :], op0=ALU.mult,
                                                   op1=ALU.subtract).then_inc(s_h2, 1)

                def weigh(j, p, step):
                    kind, a = divmod(step, 2)
                    if kind == 0:
                        if a == 0:
                            dve.wait_ge(s_down, FC * (j + 1))
                        nc.vector.scalar_tensor_tensor(out=t1[:, a].rearrange("p e d -> p (e d)"), in0=pE[p][:, a, :],
                                                       scalar=back[:, 1:2], in1=b2p[:].rearrange("p e d -> p (e d)"),
                                                       op0=ALU.mult, op1=ALU.add).then_inc(s_b, 1)
                    elif kind == 1:
                        return
                    elif kind == 2:
                        dve.wait_ge(s_wt, 2 * j + a + 1)
                        nc.vector.tensor_reduce(acc[:, a, :], t1[:, a].rearrange("p e d -> p d e"), AX.X,
                                                ALU.add).then_inc(s_r, 1)
                    elif kind == 3:
                        dve.wait_ge(s_r, 2 * j + a + 1)
                        nc.vector.scalar_tensor_tensor(out=acc[:, a, :], in0=pS[p][:, a * DM:(a + 1) * DM],
                                                       scalar=back[:, 1:2], in1=acc[:, a, :], op0=ALU.mult,
                                                       op1=ALU.add).then_inc(s_s, 1)
                    elif a == 0:
                        dve.wait_ge(s_s, 2 * j + 2)
                        if isinstance(j, int):
                            after(dve, s_st[p], 32 * (j // 2))
                        else:
                            dve.wait_ge(s_st[p], (j - p) * 16)
                        nc.vector.tensor_tensor(fin[:, p], acc[:], res[:, bass.ts(j, 2), :], ALU.add).then_inc(s_f, 1)

                def body(j, p):
                    for c in range(FC):
                        if c % 2:
                            low(j, c // 2)
                        if c >= FC - 9 and not (isinstance(j, int) and j == 0):
                            weigh(j - 1, 1 - p, c - (FC - 9))
                over_groups(dve, body)
                for step in range(9):
                    weigh(NG - 1, (NG - 1) % 2, step)

            @block.sync
            def _(sp):
                def body(j, p):
                    sp.wait_ge(s_f, j + 1)
                    dst = io["out"].rearrange("s (j a b) d -> j b s a d", a=2, b=2)
                    for b in range(2):
                        sp.dma_start(dst[j, b], fin[b * S:(b + 1) * S, p]).then_inc(s_st[p], 16)
                over_groups(sp, body)
                sp.wait_ge(s_st[0], 32 * (NG - NG // 2))
                sp.wait_ge(s_st[1], 32 * (NG // 2))


def recur_and_ffn(nc, io, sb, res, rk16, vscale, past):
    with nc.sbuf_tensor("hs", [128, HQ, B, S], F32) as hs:
        recur(nc, io, hs, rk16, vscale, past)
        ffn(nc, io, sb, res, hs, past)


def program(nc, io):
    with ExitStack() as ctx:
        def tile(name, shape):
            return ctx.enter_context(nc.sbuf_tensor(name, shape, F32))

        def scratch(name, shape, dt=F32):
            return nc.dram_tensor(name, shape, dt, kind="Internal").ap()

        io["feat"] = [scratch(f"d_feat{j}", [NT, 128, 3 * HD], F16) for j in range(2)]
        io["val"] = scratch("d_val", [NT, 128, 2 * HD + 2 * H])
        io["diag"] = [scratch(f"d_diag{y}", [NT, 128, HD]) for y in range(2)]
        io["tinv"] = [scratch(f"d_tinv{y}", [NT, 128, H * BLK]) for y in range(2)]
        io["z"] = scratch("d_z", [128, HQ, NT, 128])
        res = tile("res", [128, NT, DM])
        vscale = tile("vscale", [128, 3])
        sb = {"rows": tile("rows", [128, 6, DM]), "ident": tile("ident", [128, 128])}
        rk16 = [ctx.enter_context(nc.sbuf_tensor(f"rk16_{j}", [128, HQ, 2, B * S // 2], F16)) for j in range(2)]
        with ExitStack() as early:
            def f16(name, shape):
                return early.enter_context(nc.sbuf_tensor(name, shape, F16))

            oT = f16("oT", [128, NT * 128])
            w16 = [f16(f"slow_w16_{j}", [128, NP]) for j in range(2)]
            pback = early.enter_context(nc.sbuf_tensor("proj_back", [128, 2], F32))
            embed(nc, io, sb, res, oT, w16, pback)
            features(nc, io, sb, oT, w16, pback, rk16, vscale)
        inverses(nc, io)
        past = ctx.enter_context(nc.sbuf_tensor("past", [128, 2, 2, B // 4, HD], F16))
        solve(nc, io, vscale, past)
        recur_and_ffn(nc, io, sb, res, rk16, vscale, past)


OUT = ((S, B, DM), "float32")


def kernel(**inputs):
    import concourse.bacc as _bacc
    from concourse.bass_utils import run_bass_kernel_spmd as _run

    a = {k: np.asarray(v) for k, v in inputs.items()}
    frames = a["x"][:, :NCH * 8, :].reshape(S, NCH, 8 * 16).transpose(2, 1, 0)
    sw = a["L0_attn_slow_W"].reshape(H, 5 * D + 2, DM)
    parts = [sw[:, j * D:(j + 1) * D].reshape(HD, DM) for j in (0, 1, 3, 2, 4)]
    parts[3:3] = [sw[:, 5 * D], sw[:, 5 * D + 1]]
    rows = np.stack([a[k] for k in ("L0_tok_b", "L0_tok_gamma", "L0_tok_beta", "L0_attn_ln_g", "L0_attn_ln_b",
                                    "L0_ffn_b2s")])
    tok = np.arange(128)
    b_, t_ = tok // S, tok % S
    same = b_[:, None] == b_[None, :]
    before = same & (t_[:, None] // BLK < t_[None, :] // BLK)
    causal = same & (t_[:, None] <= t_[None, :])
    step = np.arange(S // 2)
    b4, s4 = tok // 32, tok % 32
    see4 = (s4[:, None, None] <= step[None, :, None]) & (b4[:, None, None] == np.arange(16)[None, None, :] // 4)
    e_ = np.arange(E)
    given = {
        "frames": frames,
        "tok_w": a["L0_tok_W"].T.reshape(2, 128, DM).transpose(1, 0, 2),
        "rows": np.broadcast_to(rows[None], (128, 6, DM)),
        "ident": np.eye(128, dtype=np.float32),
        "slow_w": np.concatenate(parts, 0).T,
        "masks": np.stack([before, causal], 1).astype(np.float32) / np.float32(UNIT),
        "own_blk": (tok[:, None] // BLK == tok[None, :] // BLK).astype(np.float32),
        "see4": see4.astype(np.float32) / np.float32(UNIT),
        "out_w": a["L0_attn_out_W"].T.reshape(HQ, 128, DM).transpose(1, 0, 2),
        "wr": a["L0_ffn_Wr"],
        "w1": np.concatenate([a["L0_ffn_W1p"].transpose(1, 0, 2), a["L0_ffn_W1s"][:, None]], 1).reshape(DM, FC, 128),
        "b1": np.concatenate([a["L0_ffn_b1p"], a["L0_ffn_b1s"][None]], 0).reshape(FC, 128).T,
        "w2": np.concatenate([a["L0_ffn_W2p"], a["L0_ffn_W2s"][None]], 0).reshape(FC, 128, DM).transpose(1, 0, 2),
        "b2p": np.broadcast_to(a["L0_ffn_b2p"][None], (128, E, DM)),
        "earlier": np.broadcast_to((e_[None, :] < e_[:, None]).astype(np.float32), (128, E, E)),
    }
    nc = _bacc.Bacc("TRN2", target_bir_lowering=False, num_devices=1)
    arrays, io = {}, {}
    for name, v in given.items():
        v = np.ascontiguousarray(v)
        arrays[f"in_{name}"] = v
        io[name] = nc.dram_tensor(f"in_{name}", v.shape, mybir.dt.from_np(v.dtype), kind="ExternalInput").ap()
    io["out"] = nc.dram_tensor("out", OUT[0], F32, kind="ExternalOutput").ap()
    program(nc, io)
    r = _run(nc, [arrays], core_ids=[0])
    return r.results[0]["out"]
```
